# Optimizing a Trainium2 kernel written in Bass

```python
import numpy as np
import jax
import jax.numpy as jnp

def _softmax(x, axis=-1):
    return jax.nn.softmax(x, axis=axis)

def _gelu(x):
    return jax.nn.gelu(x, approximate=True)

def _silu(x):
    return jax.nn.silu(x)

def _sigmoid(x):
    return jax.nn.sigmoid(x)

def _layernorm(x, axis=-1, eps=1e-05):
    m = jnp.mean(x, axis=axis, keepdims=True)
    v = jnp.var(x, axis=axis, keepdims=True)
    return (x - m) / jnp.sqrt(v + eps)

def _scatter_add(tgt, idx, src, axis=0):
    return tgt.at[idx].add(src)

def _segment_sum(src, seg, n):
    return jax.ops.segment_sum(src, seg, n)
kernel_name = 'mk_xattn_ffn_d4_seqx_r4_fea24a'

def setup_inputs(seed: int=0):
    np.random.seed(seed)
    _w = jnp.asarray

    def _rec_inputs():
        import jax
        import jax.numpy as jnp
        _rk = jax.random.key(seed)
        x = -0.0002928 + 1 * jax.random.normal(jax.random.fold_in(_rk, 1), (32, 128, 256), jnp.float32)
        _lenS = 128 - jax.random.randint(jax.random.fold_in(_rk, 7), (32,), 0, max(1, 128 // 4) + 1, jnp.int32)
        _lenS2 = 128 - jax.random.randint(jax.random.fold_in(_rk, 8), (32,), 0, max(1, 128 // 4) + 1, jnp.int32)
        _ctx_1024P = jax.random.normal(jax.random.fold_in(_rk, 11), (32, 16, 256), jnp.float32)
        _ctx_1024c = jax.random.dirichlet(jax.random.fold_in(_rk, 511), 0.3 * jnp.ones((16,), jnp.float32), (32, 128))
        _ctx_1024t = jnp.einsum('bsk,bkd->bsd', _ctx_1024c, _ctx_1024P)
        _ctx_1024t = _ctx_1024t * jax.lax.rsqrt(jnp.mean(jnp.square(_ctx_1024t)) + 1e-12) * 0.953939
        ctx_1024 = -1.39393e-06 + 0.999914 * (_ctx_1024t + 0.3 * jax.random.normal(jax.random.fold_in(_rk, 611), (32, 128, 256), jnp.float32))
        fside_Bx16xSxS2_0 = 9.80324e-06 + 0.100009 * jax.random.normal(jax.random.fold_in(_rk, 12), (32, 16, 128, 128), jnp.float32)
        fside_SxS2_0 = -2.64403e-05 + 0.100002 * jax.random.normal(jax.random.fold_in(_rk, 14), (128, 128), jnp.float32)
        _validS = jnp.arange(128)[None, :] < _lenS[:, None]
        _validS2 = jnp.arange(128)[None, :] < _lenS2[:, None]
        _causal = jnp.tril(jnp.ones((128, 128), dtype=bool))
        mask_BxS2_bf0 = jnp.logical_not(jnp.ones((32, 128), dtype=bool))
        return (x, ctx_1024, fside_Bx16xSxS2_0, fside_SxS2_0, mask_BxS2_bf0)
    x, ctx_1024, fside_Bx16xSxS2_0, fside_SxS2_0, mask_BxS2_bf0 = _rec_inputs()

    def _L0_xattn_setup():
        import jax, jax.numpy as jnp
        import numpy as np
        D_MODEL = 256
        N_HEAD = 16
        D_HEAD = D_MODEL // N_HEAD
        B, Q, K = (2, 512, 512)
        key = jax.random.key(seed)
        ks = jax.random.split(key, 11)
        s = 1.0 / np.sqrt(D_MODEL)
        return {'q': jax.random.normal(ks[0], (B, Q, D_MODEL), jnp.float32), 'k': jax.random.normal(ks[1], (B, K, D_MODEL), jnp.float32), 'v': jax.random.normal(ks[2], (B, K, D_MODEL), jnp.float32), 'Wq': jax.random.normal(ks[3], (D_MODEL, D_MODEL), jnp.float32) * s, 'bq': jnp.zeros((D_MODEL,), jnp.float32), 'Wk': jax.random.normal(ks[4], (D_MODEL, D_MODEL), jnp.float32) * s, 'bk': jnp.zeros((D_MODEL,), jnp.float32), 'Wv': jax.random.normal(ks[5], (D_MODEL, D_MODEL), jnp.float32) * s, 'bv': jnp.zeros((D_MODEL,), jnp.float32), 'Wo': jax.random.normal(ks[6], (D_MODEL, D_MODEL), jnp.float32) * s, 'bo': jnp.zeros((D_MODEL,), jnp.float32)}
    _L0_xattn_all = _L0_xattn_setup()
    _L0_xattn_in = {k: v for k, v in _L0_xattn_all.items() if k in ('Wq', 'bq', 'Wk', 'bk', 'Wv', 'bv', 'Wo', 'bo')}
    del _L0_xattn_all

    def _L0_ffn_setup():
        import jax, jax.numpy as jnp
        import numpy as np
        BS, L, D = (4, 512, 256)
        H, E, K = (8, 16, 2)
        HD = D // H
        I = 1024 // H
        key = jax.random.key(seed)
        ks = jax.random.split(key, 10)
        s = lambda k, shp, fan: jax.random.normal(k, shp, jnp.float32) / np.sqrt(fan)
        return {'x': jax.random.normal(ks[0], (BS, L, D), jnp.float32), 'Wm': s(ks[1], (D, D), D), 'bm': jnp.zeros((D,), jnp.float32), 'expert_emb': jax.random.normal(ks[2], (HD, E), jnp.float32), 'W1': s(ks[3], (E, HD, I), HD), 'b1': jnp.zeros((E, I), jnp.float32), 'W2': s(ks[4], (E, I, HD), I), 'b2': jnp.zeros((E, HD), jnp.float32), 'Wo': s(ks[5], (D, D), D), 'bo': jnp.zeros((D,), jnp.float32)}
    _L0_ffn_all = _L0_ffn_setup()
    _L0_ffn_in = {k: v for k, v in _L0_ffn_all.items() if k in ('Wm', 'bm', 'expert_emb', 'W1', 'b1', 'W2', 'b2', 'Wo', 'bo')}
    del _L0_ffn_all

    def _L1_xattn_setup():
        import jax, jax.numpy as jnp
        import numpy as np
        B, L, DM, H, M = (4, 512, 256, 16, 64)
        D = DM // H
        CHUNK = 128
        KERNEL_EPS = 0.0001
        NORM_STAB = 1e-06

        def performer_forward(q, k, v, Wq, bq, Wk, bk, Wv, bv, Wo, bo, random_features):
            b, l, dm = q.shape
            d, m = random_features.shape
            h = dm // d

            def heads(x, W, bias):
                return (x @ W + bias).reshape(b, l, h, d).transpose(0, 2, 1, 3)
            qh, kh, vh = (heads(q, Wq, bq), heads(k, Wk, bk), heads(v, Wv, bv))
            scale = dm ** 0.25
            qs, ksc = (qh / scale, kh / scale)
            pq = jnp.einsum('bhld,dm->bhlm', qs, random_features)
            pk = jnp.einsum('bhld,dm->bhlm', ksc, random_features)
            hk = -0.5 * jnp.sum(ksc * ksc, axis=-1, keepdims=True)
            k_stab = jnp.max(hk)
            c = m ** (-0.5)
            qp = c * (jnp.exp(pq) + KERNEL_EPS)
            kp = c * (jnp.exp(hk + pk - k_stab) + KERNEL_EPS)
            C = CHUNK
            N = l // C
            qc = qp.reshape(b, h, N, C, m)
            kc = kp.reshape(b, h, N, C, m)
            vc = vh.reshape(b, h, N, C, d)
            tril = jnp.tril(jnp.ones((C, C), dtype=qp.dtype))
            A = jnp.einsum('bhnim,bhnjm->bhnij', qc, kc) * tril
            Ssum = jnp.einsum('bhnjm,bhnjd->bhnmd', kc, vc)
            Sprev = jnp.cumsum(Ssum, axis=2) - Ssum
            num = jnp.einsum('bhnij,bhnjd->bhnid', A, vc) + jnp.einsum('bhnim,bhnmd->bhnid', qc, Sprev)
            zsum = kc.sum(axis=3)
            zprev = jnp.cumsum(zsum, axis=2) - zsum
            den = A.sum(axis=-1) + jnp.einsum('bhnim,bhnm->bhni', qc, zprev)
            den = den + 2.0 * NORM_STAB * (jnp.abs(den) <= NORM_STAB).astype(den.dtype)
            out = (num / den[..., None]).reshape(b, h, l, d)
            ctx = out.transpose(0, 2, 1, 3).reshape(b, l, dm)
            return ctx @ Wo + bo
        key = jax.random.key(seed)
        ks = jax.random.split(key, 12)
        n = lambda k, shape, s=1.0: jax.random.normal(k, shape, jnp.float32) * s
        w = DM ** (-0.5)
        return {'q': n(ks[0], (B, L, DM)), 'k': n(ks[1], (B, L, DM)), 'v': n(ks[2], (B, L, DM)), 'Wq': n(ks[3], (DM, DM), w), 'bq': n(ks[4], (DM,), 0.01), 'Wk': n(ks[5], (DM, DM), w), 'bk': n(ks[6], (DM,), 0.01), 'Wv': n(ks[7], (DM, DM), w), 'bv': n(ks[8], (DM,), 0.01), 'Wo': n(ks[9], (DM, DM), w), 'bo': n(ks[10], (DM,), 0.01), 'random_features': n(ks[11], (D, M))}
    _L1_xattn_all = _L1_xattn_setup()
    _L1_xattn_in = {k: v for k, v in _L1_xattn_all.items() if k in ('Wq', 'bq', 'Wk', 'bk', 'Wv', 'bv', 'Wo', 'bo', 'random_features')}
    del _L1_xattn_all

    def _L1_ffn_setup():
        import jax, jax.numpy as jnp
        import numpy as np
        D_MODEL = 256
        N_EXPERTS = 8
        TOP_K = 2
        LN_EPS = 1e-05
        key = jax.random.key(seed)
        ks = jax.random.split(key, 8)
        B, S, d, E = (2, 512, D_MODEL, N_EXPERTS)
        f = 2 * d
        s_in = 0.02
        return {'x': jax.random.normal(ks[0], (B, S, d), jnp.float32), 'Wg': jax.random.normal(ks[1], (d, E), jnp.float32) * s_in, 'bg': jnp.zeros((E,), jnp.float32), 'W1': jax.random.normal(ks[2], (E, d, f), jnp.float32) * s_in, 'b1': jnp.zeros((E, f), jnp.float32), 'W2': jax.random.normal(ks[3], (E, f, d), jnp.float32) * s_in, 'b2': jnp.zeros((E, d), jnp.float32), 'gamma': jnp.ones((d,), jnp.float32), 'beta': jnp.zeros((d,), jnp.float32)}
    _L1_ffn_all = _L1_ffn_setup()
    _L1_ffn_in = {k: v for k, v in _L1_ffn_all.items() if k in ('Wg', 'bg', 'W1', 'b1', 'W2', 'b2', 'gamma', 'beta')}
    del _L1_ffn_all

    def _L2_xattn_setup():
        import jax, jax.numpy as jnp
        import numpy as np
        D_MODEL, D_K, D_V, N_HEADS = (256, 64, 64, 16)
        key = jax.random.key(seed)
        ks = jax.random.split(key, 7)
        B, S = (4, 512)
        scale = 1.0 / np.sqrt(D_MODEL)
        return {'q': jax.random.normal(ks[0], (B, S, D_MODEL), jnp.float32), 'k': jax.random.normal(ks[1], (B, S, D_MODEL), jnp.float32), 'v': jax.random.normal(ks[2], (B, S, D_MODEL), jnp.float32), 'Wq': jax.random.normal(ks[3], (D_MODEL, N_HEADS * D_K), jnp.float32) * scale, 'Wk': jax.random.normal(ks[4], (D_MODEL, N_HEADS * D_K), jnp.float32) * scale, 'Wv': jax.random.normal(ks[5], (D_MODEL, N_HEADS * D_V), jnp.float32) * scale, 'Wo': jax.random.normal(ks[6], (N_HEADS * D_V, D_MODEL), jnp.float32) * (1.0 / np.sqrt(N_HEADS * D_V))}
    _L2_xattn_all = _L2_xattn_setup()
    _L2_xattn_in = {k: v for k, v in _L2_xattn_all.items() if k in ('Wq', 'Wk', 'Wv', 'Wo')}
    del _L2_xattn_all

    def _L2_ffn_setup():
        import jax, jax.numpy as jnp
        import numpy as np
        LN_EPS = 1e-05

        def layernorm(x, g, b):
            mu = jnp.mean(x, axis=-1, keepdims=True)
            var = jnp.mean((x - mu) ** 2, axis=-1, keepdims=True)
            return (x - mu) * jax.lax.rsqrt(var + LN_EPS) * g + b

        def act_quant_fake(x):
            scale = 127.0 / jnp.clip(jnp.max(jnp.abs(x), axis=-1, keepdims=True), 1e-05)
            return jnp.clip(jnp.round(x * scale), -128.0, 127.0) / scale

        def weight_quant_fake(w):
            scale = 1.0 / jnp.clip(jnp.mean(jnp.abs(w)), 1e-05)
            return jnp.clip(jnp.round(w * scale), -1.0, 1.0) / scale

        def bitlinear(x, w, b):
            dqx = act_quant_fake(x)
            dqw = weight_quant_fake(w)
            return jnp.einsum('btd,hd->bth', dqx, dqw) + b
        key = jax.random.key(seed)
        ks = jax.random.split(key, 5)
        B, T, D, H = (8, 1024, 256, 1024)
        return {'x': jax.random.normal(ks[0], (B, T, D), dtype=jnp.float32), 'ln1_g': jnp.ones((D,), jnp.float32), 'ln1_b': jnp.zeros((D,), jnp.float32), 'w1': jax.random.normal(ks[1], (H, D), dtype=jnp.float32) * (1.0 / np.sqrt(D)), 'b1': jax.random.normal(ks[2], (H,), dtype=jnp.float32) * 0.02, 'ln2_g': jnp.ones((H,), jnp.float32), 'ln2_b': jnp.zeros((H,), jnp.float32), 'w2': jax.random.normal(ks[3], (D, H), dtype=jnp.float32) * (1.0 / np.sqrt(H)), 'b2': jax.random.normal(ks[4], (D,), jnp.float32) * 0.02}
    _L2_ffn_all = _L2_ffn_setup()
    _L2_ffn_in = {k: v for k, v in _L2_ffn_all.items() if k in ('ln1_g', 'ln1_b', 'w1', 'b1', 'ln2_g', 'ln2_b', 'w2', 'b2')}
    del _L2_ffn_all

    def _L3_xattn_setup():
        import jax, jax.numpy as jnp
        import numpy as np
        E = 256
        H = 16
        D = E // H
        key = jax.random.key(seed)
        ks = jax.random.split(key, 12)
        B, T, S = (2, 512, 512)
        inp = {'query': jax.random.normal(ks[0], (B, T, E), jnp.float32), 'key': jax.random.normal(ks[1], (B, S, E), jnp.float32), 'value': jax.random.normal(ks[2], (B, S, E), jnp.float32), 'spatial_bias': jax.random.normal(ks[3], (B, H, T, S), jnp.float32) * 0.1, 'directional_bias': jax.random.normal(ks[4], (B, H, T, S), jnp.float32) * 0.1, 'key_padding_mask': jnp.zeros((B, S), dtype=bool), 'attn_mask': jax.random.normal(ks[5], (T, S), jnp.float32) * 0.1, 'Wq': jax.random.normal(ks[6], (E, E), jnp.float32) / np.sqrt(E), 'bq': jnp.zeros((E,), jnp.float32), 'Wk': jax.random.normal(ks[7], (E, E), jnp.float32) / np.sqrt(E), 'bk': jnp.zeros((E,), jnp.float32), 'Wv': jax.random.normal(ks[8], (E, E), jnp.float32) / np.sqrt(E), 'bv': jnp.zeros((E,), jnp.float32), 'Wo': jax.random.normal(ks[9], (E, E), jnp.float32) / np.sqrt(E), 'bo': jnp.zeros((E,), jnp.float32)}
        return inp
    _L3_xattn_all = _L3_xattn_setup()
    _L3_xattn_in = {k: v for k, v in _L3_xattn_all.items() if k in ('Wq', 'bq', 'Wk', 'bk', 'Wv', 'bv', 'Wo', 'bo')}
    del _L3_xattn_all

    def _L3_ffn_setup():
        import jax, jax.numpy as jnp
        import numpy as np
        E = 8
        K = 2
        DIM = 256
        DFF = 512

        def _moe(x, Wg, bg, w1, w2):
            B, S, D = x.shape
            t = x.reshape(-1, D)
            logits = t @ Wg.T + bg
            probs = jax.nn.softmax(logits, axis=-1)
            topw, topi = jax.lax.top_k(probs, K)
            topw = topw / jnp.sum(topw, axis=-1, keepdims=True)
            combine = jnp.sum(jax.nn.one_hot(topi, E, dtype=t.dtype) * topw[..., None], axis=1)

            def body(acc, packed):
                w1e, w2e, ce = packed
                h = t @ w1e.T
                gate, up = jnp.split(h, 2, axis=-1)
                a = jax.nn.silu(gate) * up
                o = a @ w2e.T
                return (acc + ce[:, None] * o, None)
            out, _ = jax.lax.scan(body, jnp.zeros_like(t), (w1, w2, combine.T))
            return out.reshape(B, S, D)
        key = jax.random.key(seed)
        ks = jax.random.split(key, 5)
        B, S = (4, 512)
        x = jax.random.normal(ks[0], (B, S, DIM), dtype=jnp.float32)
        Wg = jax.random.normal(ks[1], (E, DIM), dtype=jnp.float32) * 0.02
        bg = jax.random.normal(ks[2], (E,), dtype=jnp.float32) * 0.02
        w1 = jax.random.normal(ks[3], (E, DFF, DIM), dtype=jnp.float32) * 0.02
        w2 = jax.random.normal(ks[4], (E, DIM, DFF // 2), dtype=jnp.float32) * 0.02
        return {'x': x, 'Wg': Wg, 'bg': bg, 'w1': w1, 'w2': w2}
    _L3_ffn_all = _L3_ffn_setup()
    _L3_ffn_in = {k: v for k, v in _L3_ffn_all.items() if k in ('Wg', 'bg', 'w1', 'w2')}
    del _L3_ffn_all
    return {'x': x, 'ctx_1024': ctx_1024, 'fside_Bx16xSxS2_0': fside_Bx16xSxS2_0, 'fside_SxS2_0': fside_SxS2_0, 'mask_BxS2_bf0': mask_BxS2_bf0, 'L0_xattn_Wq': _L0_xattn_in['Wq'], 'L0_xattn_bq': _L0_xattn_in['bq'], 'L0_xattn_Wk': _L0_xattn_in['Wk'], 'L0_xattn_bk': _L0_xattn_in['bk'], 'L0_xattn_Wv': _L0_xattn_in['Wv'], 'L0_xattn_bv': _L0_xattn_in['bv'], 'L0_xattn_Wo': _L0_xattn_in['Wo'], 'L0_xattn_bo': _L0_xattn_in['bo'], 'L0_ffn_Wm': _L0_ffn_in['Wm'], 'L0_ffn_bm': _L0_ffn_in['bm'], 'L0_ffn_expert_emb': _L0_ffn_in['expert_emb'], 'L0_ffn_W1': _L0_ffn_in['W1'], 'L0_ffn_b1': _L0_ffn_in['b1'], 'L0_ffn_W2': _L0_ffn_in['W2'], 'L0_ffn_b2': _L0_ffn_in['b2'], 'L0_ffn_Wo': _L0_ffn_in['Wo'], 'L0_ffn_bo': _L0_ffn_in['bo'], 'L1_xattn_Wq': _L1_xattn_in['Wq'], 'L1_xattn_bq': _L1_xattn_in['bq'], 'L1_xattn_Wk': _L1_xattn_in['Wk'], 'L1_xattn_bk': _L1_xattn_in['bk'], 'L1_xattn_Wv': _L1_xattn_in['Wv'], 'L1_xattn_bv': _L1_xattn_in['bv'], 'L1_xattn_Wo': _L1_xattn_in['Wo'], 'L1_xattn_bo': _L1_xattn_in['bo'], 'L1_xattn_random_features': _L1_xattn_in['random_features'], 'L1_ffn_Wg': _L1_ffn_in['Wg'], 'L1_ffn_bg': _L1_ffn_in['bg'], 'L1_ffn_W1': _L1_ffn_in['W1'], 'L1_ffn_b1': _L1_ffn_in['b1'], 'L1_ffn_W2': _L1_ffn_in['W2'], 'L1_ffn_b2': _L1_ffn_in['b2'], 'L1_ffn_gamma': _L1_ffn_in['gamma'], 'L1_ffn_beta': _L1_ffn_in['beta'], 'L2_xattn_Wq': _L2_xattn_in['Wq'], 'L2_xattn_Wk': _L2_xattn_in['Wk'], 'L2_xattn_Wv': _L2_xattn_in['Wv'], 'L2_xattn_Wo': _L2_xattn_in['Wo'], 'L2_ffn_ln1_g': _L2_ffn_in['ln1_g'], 'L2_ffn_ln1_b': _L2_ffn_in['ln1_b'], 'L2_ffn_w1': _L2_ffn_in['w1'], 'L2_ffn_b1': _L2_ffn_in['b1'], 'L2_ffn_ln2_g': _L2_ffn_in['ln2_g'], 'L2_ffn_ln2_b': _L2_ffn_in['ln2_b'], 'L2_ffn_w2': _L2_ffn_in['w2'], 'L2_ffn_b2': _L2_ffn_in['b2'], 'L3_xattn_Wq': _L3_xattn_in['Wq'], 'L3_xattn_bq': _L3_xattn_in['bq'], 'L3_xattn_Wk': _L3_xattn_in['Wk'], 'L3_xattn_bk': _L3_xattn_in['bk'], 'L3_xattn_Wv': _L3_xattn_in['Wv'], 'L3_xattn_bv': _L3_xattn_in['bv'], 'L3_xattn_Wo': _L3_xattn_in['Wo'], 'L3_xattn_bo': _L3_xattn_in['bo'], 'L3_ffn_Wg': _L3_ffn_in['Wg'], 'L3_ffn_bg': _L3_ffn_in['bg'], 'L3_ffn_w1': _L3_ffn_in['w1'], 'L3_ffn_w2': _L3_ffn_in['w2']}

def reference(x, ctx_1024, fside_Bx16xSxS2_0, fside_SxS2_0, mask_BxS2_bf0, L0_xattn_Wq, L0_xattn_bq, L0_xattn_Wk, L0_xattn_bk, L0_xattn_Wv, L0_xattn_bv, L0_xattn_Wo, L0_xattn_bo, L0_ffn_Wm, L0_ffn_bm, L0_ffn_expert_emb, L0_ffn_W1, L0_ffn_b1, L0_ffn_W2, L0_ffn_b2, L0_ffn_Wo, L0_ffn_bo, L1_xattn_Wq, L1_xattn_bq, L1_xattn_Wk, L1_xattn_bk, L1_xattn_Wv, L1_xattn_bv, L1_xattn_Wo, L1_xattn_bo, L1_xattn_random_features, L1_ffn_Wg, L1_ffn_bg, L1_ffn_W1, L1_ffn_b1, L1_ffn_W2, L1_ffn_b2, L1_ffn_gamma, L1_ffn_beta, L2_xattn_Wq, L2_xattn_Wk, L2_xattn_Wv, L2_xattn_Wo, L2_ffn_ln1_g, L2_ffn_ln1_b, L2_ffn_w1, L2_ffn_b1, L2_ffn_ln2_g, L2_ffn_ln2_b, L2_ffn_w2, L2_ffn_b2, L3_xattn_Wq, L3_xattn_bq, L3_xattn_Wk, L3_xattn_bk, L3_xattn_Wv, L3_xattn_bv, L3_xattn_Wo, L3_xattn_bo, L3_ffn_Wg, L3_ffn_bg, L3_ffn_w1, L3_ffn_w2):
    import jax
    import jax.numpy as jnp

    def _L0_xattn_ref(q, k, v, Wq, bq, Wk, bk, Wv, bv, Wo, bo):
        import jax, jax.numpy as jnp
        import numpy as np
        D_MODEL = 256
        N_HEAD = 16
        D_HEAD = D_MODEL // N_HEAD
        B, Q, K = (2, 512, 512)
        Bq, Qlen, D = q.shape
        Klen = k.shape[1]
        qh = (q @ Wq + bq).reshape(Bq, Qlen, N_HEAD, D_HEAD).transpose(0, 2, 1, 3)
        kh = (k @ Wk + bk).reshape(Bq, Klen, N_HEAD, D_HEAD).transpose(0, 2, 1, 3)
        vh = (v @ Wv + bv).reshape(Bq, Klen, N_HEAD, D_HEAD).transpose(0, 2, 1, 3)
        logits = jnp.einsum('bhqd,bhkd->bhqk', qh, kh) / np.sqrt(D_HEAD).astype(np.float32)
        attn = jax.nn.softmax(logits, axis=-1)
        out = jnp.einsum('bhqk,bhkd->bhqd', attn, vh)
        out = out.transpose(0, 2, 1, 3).reshape(Bq, Qlen, D)
        return out @ Wo + bo

    def _L0_ffn_ref(x, Wm, bm, expert_emb, W1, b1, W2, b2, Wo, bo):
        import jax, jax.numpy as jnp
        import numpy as np
        BS, L, D = (4, 512, 256)
        H, E, K = (8, 16, 2)
        HD = D // H
        I = 1024 // H
        bs, L_, d = x.shape
        h = x @ Wm + bm
        t = h.reshape(bs * L_ * H, HD)
        logits = t @ expert_emb
        w = jax.nn.softmax(logits, axis=-1)
        topw, topi = jax.lax.top_k(w, K)
        hmid = jax.nn.gelu(jnp.einsum('td,edi->tei', t, W1) + b1, approximate=False)
        eo = jnp.einsum('tei,eio->teo', hmid, W2) + b2
        sel = jnp.take_along_axis(eo, topi[:, :, None], axis=1)
        comb = (sel * topw[:, :, None]).sum(axis=1)
        out = comb.reshape(bs, L_, d)
        return out @ Wo + bo

    def _L1_xattn_ref(q, k, v, Wq, bq, Wk, bk, Wv, bv, Wo, bo, random_features):
        import jax, jax.numpy as jnp
        import numpy as np
        B, L, DM, H, M = (4, 512, 256, 16, 64)
        D = DM // H
        CHUNK = 128
        KERNEL_EPS = 0.0001
        NORM_STAB = 1e-06

        def performer_forward(q, k, v, Wq, bq, Wk, bk, Wv, bv, Wo, bo, random_features):
            b, l, dm = q.shape
            d, m = random_features.shape
            h = dm // d

            def heads(x, W, bias):
                return (x @ W + bias).reshape(b, l, h, d).transpose(0, 2, 1, 3)
            qh, kh, vh = (heads(q, Wq, bq), heads(k, Wk, bk), heads(v, Wv, bv))
            scale = dm ** 0.25
            qs, ksc = (qh / scale, kh / scale)
            pq = jnp.einsum('bhld,dm->bhlm', qs, random_features)
            pk = jnp.einsum('bhld,dm->bhlm', ksc, random_features)
            hk = -0.5 * jnp.sum(ksc * ksc, axis=-1, keepdims=True)
            k_stab = jnp.max(hk)
            c = m ** (-0.5)
            qp = c * (jnp.exp(pq) + KERNEL_EPS)
            kp = c * (jnp.exp(hk + pk - k_stab) + KERNEL_EPS)
            C = CHUNK
            N = l // C
            qc = qp.reshape(b, h, N, C, m)
            kc = kp.reshape(b, h, N, C, m)
            vc = vh.reshape(b, h, N, C, d)
            tril = jnp.tril(jnp.ones((C, C), dtype=qp.dtype))
            A = jnp.einsum('bhnim,bhnjm->bhnij', qc, kc) * tril
            Ssum = jnp.einsum('bhnjm,bhnjd->bhnmd', kc, vc)
            Sprev = jnp.cumsum(Ssum, axis=2) - Ssum
            num = jnp.einsum('bhnij,bhnjd->bhnid', A, vc) + jnp.einsum('bhnim,bhnmd->bhnid', qc, Sprev)
            zsum = kc.sum(axis=3)
            zprev = jnp.cumsum(zsum, axis=2) - zsum
            den = A.sum(axis=-1) + jnp.einsum('bhnim,bhnm->bhni', qc, zprev)
            den = den + 2.0 * NORM_STAB * (jnp.abs(den) <= NORM_STAB).astype(den.dtype)
            out = (num / den[..., None]).reshape(b, h, l, d)
            ctx = out.transpose(0, 2, 1, 3).reshape(b, l, dm)
            return ctx @ Wo + bo
        return performer_forward(q, k, v, Wq, bq, Wk, bk, Wv, bv, Wo, bo, random_features)

    def _L1_ffn_ref(x, Wg, bg, W1, b1, W2, b2, gamma, beta):
        import jax, jax.numpy as jnp
        import numpy as np
        D_MODEL = 256
        N_EXPERTS = 8
        TOP_K = 2
        LN_EPS = 1e-05
        logits = jnp.einsum('bsd,de->bse', x, Wg) + bg
        topk_vals, topk_idx = jax.lax.top_k(logits, TOP_K)
        topk_w = jax.nn.softmax(topk_vals, axis=-1)
        h = jax.nn.relu(jnp.einsum('bsd,edf->bsef', x, W1) + b1)
        eo = jnp.einsum('bsef,efd->bsed', h, W2) + b2
        sel = jnp.take_along_axis(eo, topk_idx[..., None], axis=2)
        mixed = jnp.sum(sel * topk_w[..., None], axis=2)
        y = mixed + x
        mu = jnp.mean(y, axis=-1, keepdims=True)
        var = jnp.mean(jnp.square(y - mu), axis=-1, keepdims=True)
        return gamma * (y - mu) * jax.lax.rsqrt(var + LN_EPS) + beta

    def _L2_xattn_ref(q, k, v, Wq, Wk, Wv, Wo):
        import jax, jax.numpy as jnp
        import numpy as np
        D_MODEL, D_K, D_V, N_HEADS = (256, 64, 64, 16)
        B, Sq, _ = q.shape
        Sk = k.shape[1]
        qh = (q @ Wq).reshape(B, Sq, N_HEADS, D_K).transpose(0, 2, 1, 3)
        kh = (k @ Wk).reshape(B, Sk, N_HEADS, D_K).transpose(0, 2, 1, 3)
        vh = (v @ Wv).reshape(B, Sk, N_HEADS, D_V).transpose(0, 2, 1, 3)
        scores = jnp.einsum('bhqd,bhkd->bhqk', qh, kh) / jnp.sqrt(jnp.float32(D_K))
        probs = jax.nn.softmax(scores, axis=-1)
        out = jnp.einsum('bhqk,bhkd->bhqd', probs, vh)
        out = out.transpose(0, 2, 1, 3).reshape(B, Sq, N_HEADS * D_V)
        return out @ Wo

    def _L2_ffn_ref(x, ln1_g, ln1_b, w1, b1, ln2_g, ln2_b, w2, b2):
        import jax, jax.numpy as jnp
        import numpy as np
        LN_EPS = 1e-05

        def layernorm(x, g, b):
            mu = jnp.mean(x, axis=-1, keepdims=True)
            var = jnp.mean((x - mu) ** 2, axis=-1, keepdims=True)
            return (x - mu) * jax.lax.rsqrt(var + LN_EPS) * g + b

        def act_quant_fake(x):
            scale = 127.0 / jnp.clip(jnp.max(jnp.abs(x), axis=-1, keepdims=True), 1e-05)
            return jnp.clip(jnp.round(x * scale), -128.0, 127.0) / scale

        def weight_quant_fake(w):
            scale = 1.0 / jnp.clip(jnp.mean(jnp.abs(w)), 1e-05)
            return jnp.clip(jnp.round(w * scale), -1.0, 1.0) / scale

        def bitlinear(x, w, b):
            dqx = act_quant_fake(x)
            dqw = weight_quant_fake(w)
            return jnp.einsum('btd,hd->bth', dqx, dqw) + b
        h = layernorm(x, ln1_g, ln1_b)
        h = bitlinear(h, w1, b1)
        h = jax.nn.gelu(h, approximate=False)
        h = layernorm(h, ln2_g, ln2_b)
        h = bitlinear(h, w2, b2)
        return h

    def _L3_xattn_ref(query, key, value, spatial_bias, directional_bias, key_padding_mask, attn_mask, Wq, bq, Wk, bk, Wv, bv, Wo, bo):
        import jax, jax.numpy as jnp
        import numpy as np
        E = 256
        H = 16
        D = E // H
        B, T, _ = query.shape
        S = key.shape[1]
        scale = D ** (-0.5)
        q = (query @ Wq.T + bq).reshape(B, T, H, D).transpose(0, 2, 1, 3)
        k = (key @ Wk.T + bk).reshape(B, S, H, D).transpose(0, 2, 1, 3)
        v = (value @ Wv.T + bv).reshape(B, S, H, D).transpose(0, 2, 1, 3)
        scores = jnp.einsum('bhtd,bhsd->bhts', q, k) * scale
        scores = scores + attn_mask[None, None, :, :]
        pad = key_padding_mask[:, None, None, :]
        scores = jnp.where(pad, -jnp.inf, scores)
        if T == S:
            scores = scores + spatial_bias + directional_bias
        probs = jax.nn.softmax(scores, axis=-1)
        out = jnp.einsum('bhts,bhsd->bhtd', probs, v)
        out = out.transpose(0, 2, 1, 3).reshape(B, T, E)
        return out @ Wo.T + bo

    def _L3_ffn_ref(x, Wg, bg, w1, w2):
        import jax, jax.numpy as jnp
        import numpy as np
        E = 8
        K = 2
        DIM = 256
        DFF = 512

        def _moe(x, Wg, bg, w1, w2):
            B, S, D = x.shape
            t = x.reshape(-1, D)
            logits = t @ Wg.T + bg
            probs = jax.nn.softmax(logits, axis=-1)
            topw, topi = jax.lax.top_k(probs, K)
            topw = topw / jnp.sum(topw, axis=-1, keepdims=True)
            combine = jnp.sum(jax.nn.one_hot(topi, E, dtype=t.dtype) * topw[..., None], axis=1)

            def body(acc, packed):
                w1e, w2e, ce = packed
                h = t @ w1e.T
                gate, up = jnp.split(h, 2, axis=-1)
                a = jax.nn.silu(gate) * up
                o = a @ w2e.T
                return (acc + ce[:, None] * o, None)
            out, _ = jax.lax.scan(body, jnp.zeros_like(t), (w1, w2, combine.T))
            return out.reshape(B, S, D)
        return _moe(x, Wg, bg, w1, w2)
    x = x + _L0_xattn_ref(_layernorm(x, axis=-1), ctx_1024, ctx_1024, L0_xattn_Wq, L0_xattn_bq, L0_xattn_Wk, L0_xattn_bk, L0_xattn_Wv, L0_xattn_bv, L0_xattn_Wo, L0_xattn_bo)
    x = x + _L0_ffn_ref(_layernorm(x, axis=-1), L0_ffn_Wm, L0_ffn_bm, L0_ffn_expert_emb, L0_ffn_W1, L0_ffn_b1, L0_ffn_W2, L0_ffn_b2, L0_ffn_Wo, L0_ffn_bo)
    x = x + _L1_xattn_ref(_layernorm(x, axis=-1), ctx_1024, ctx_1024, L1_xattn_Wq, L1_xattn_bq, L1_xattn_Wk, L1_xattn_bk, L1_xattn_Wv, L1_xattn_bv, L1_xattn_Wo, L1_xattn_bo, L1_xattn_random_features)
    x = x + _L1_ffn_ref(_layernorm(x, axis=-1), L1_ffn_Wg, L1_ffn_bg, L1_ffn_W1, L1_ffn_b1, L1_ffn_W2, L1_ffn_b2, L1_ffn_gamma, L1_ffn_beta)
    x = x + _L2_xattn_ref(_layernorm(x, axis=-1), ctx_1024, ctx_1024, L2_xattn_Wq, L2_xattn_Wk, L2_xattn_Wv, L2_xattn_Wo)
    x = x + _L2_ffn_ref(_layernorm(x, axis=-1), L2_ffn_ln1_g, L2_ffn_ln1_b, L2_ffn_w1, L2_ffn_b1, L2_ffn_ln2_g, L2_ffn_ln2_b, L2_ffn_w2, L2_ffn_b2)
    x = x + _L3_xattn_ref(_layernorm(x, axis=-1), ctx_1024, ctx_1024, fside_Bx16xSxS2_0, fside_Bx16xSxS2_0, mask_BxS2_bf0, fside_SxS2_0, L3_xattn_Wq, L3_xattn_bq, L3_xattn_Wk, L3_xattn_bk, L3_xattn_Wv, L3_xattn_bv, L3_xattn_Wo, L3_xattn_bo)
    x = x + _L3_ffn_ref(_layernorm(x, axis=-1), L3_ffn_Wg, L3_ffn_bg, L3_ffn_w1, L3_ffn_w2)
    return x

_drawn_inputs = setup_inputs


def setup_inputs(seed=0):
    import zlib

    import numpy as np

    out = dict(_drawn_inputs(seed))
    spreads = {'L0_xattn_bq': (0.0, 0.1),
     'L0_xattn_bk': (0.0, 0.8),
     'L0_xattn_bv': (0.0, 0.1),
     'L0_xattn_bo': (0.0, 0.1),
     'L0_ffn_bm': (0.0, 0.1),
     'L0_ffn_b1': (0.0, 0.1),
     'L0_ffn_b2': (0.0, 0.1),
     'L0_ffn_bo': (0.0, 0.1),
     'L1_ffn_bg': (0.0, 0.341),
     'L1_ffn_b1': (0.0, 0.717),
     'L1_ffn_b2': (0.0, 0.268),
     'L1_ffn_gamma': (1.0, 0.2),
     'L1_ffn_beta': (0.0, 0.1),
     'L2_ffn_ln1_g': (1.0, 0.2),
     'L2_ffn_ln1_b': (0.0, 0.279),
     'L2_ffn_ln2_g': (1.0, 0.2),
     'L2_ffn_ln2_b': (0.0, 0.311),
     'L3_xattn_bq': (0.0, 0.8),
     'L3_xattn_bk': (0.0, 0.8),
     'L3_xattn_bv': (0.0, 0.1),
     'L3_xattn_bo': (0.0, 0.1)}
    factors = {'fside_Bx16xSxS2_0': 6.166,
     'fside_SxS2_0': 8.0,
     'L1_xattn_bq': 8.0,
     'L1_xattn_bk': 8.0,
     'L1_xattn_bv': 6.885,
     'L1_xattn_bo': 6.388,
     'L2_ffn_b1': 6.011,
     'L2_ffn_b2': 7.623,
     'L3_ffn_Wg': 8.0,
     'L3_ffn_bg': 8.0,
     'L3_ffn_w1': 8.0,
     'L3_ffn_w2': 8.0}
    for name, (base, spread) in spreads.items():
        noise = np.random.default_rng([zlib.crc32(name.encode()), seed]).standard_normal(out[name].shape)
        drawn = base * np.exp(spread * noise) if base else spread * noise
        out[name] = jnp.asarray(drawn.astype(out[name].dtype))
    for name, factor in factors.items():
        out[name] = (out[name] * factor).astype(out[name].dtype)
    return out
```

```python
from contextlib import ExitStack

import numpy as np

import concourse.bass as bass
from concourse import mybir

ALU = mybir.AluOpType
ACT = mybir.ActivationFunctionType
AX = mybir.AxisListType
F32 = mybir.dt.float32
F16 = mybir.dt.float16
BF16 = mybir.dt.bfloat16
I32 = mybir.dt.int32
U8 = mybir.dt.uint8

P = 128
BATCH = 32
D = 256
KT = D // P
HEADS = 16
BANK = 512
LN_EPS = 1e-5
RSQRT_SEED = float(0x5F3759DF)
ROUND = 1.5 * 2.0 ** 23
NEVER = 1e30


def detach_wait(eng):
    eng.nop(nofuse=True)


class Steps:

    def __init__(self, eng, sem, start, per_turn=None):
        self.eng, self.sem, self.start, self.n, self.per_turn = eng, sem, start, 0, per_turn

    def link(self, instruction):
        self.n += 1
        instruction.then_inc(self.sem, 1)
        self.eng.wait_ge(self.sem, self.start + self.n)

    def close(self):
        assert self.n == self.per_turn, f"{self.n} linked steps, {self.per_turn} declared"


def rsqrt(dve, steps, var, half, root, tmp, eps):
    steps.link(dve.tensor_scalar(var, var, eps, None, ALU.add))
    steps.link(dve.tensor_scalar(half, var.bitcast(I32), 1, None, ALU.logical_shift_right))
    steps.link(dve.tensor_scalar(root.bitcast(I32), half, -1.0, RSQRT_SEED, ALU.mult, ALU.add))
    for _ in range(3):
        steps.link(dve.scalar_tensor_tensor(out=tmp, in0=root, scalar=-0.5, in1=root, op0=ALU.mult, op1=ALU.mult))
        steps.link(dve.tensor_tensor(tmp, tmp, var, ALU.mult))
        steps.link(dve.scalar_tensor_tensor(out=root, in0=tmp, scalar=1.5, in1=root, op0=ALU.add, op1=ALU.mult))


RSQRT_STEPS = 12


class Norm:

    STEPS = 2 + RSQRT_STEPS

    def __init__(self, core, group, name="ln"):
        self.group = group
        self.stats = core.sb(name + "_stats", [P, group, 6])
        self.mean_var = core.sb(name + "_mean_var", [P, group, 2])
        self.half = core.sb(name + "_half", [P, group], I32)
        self.root = core.sb(name + "_root", [P, group])
        self.tmp = core.sb(name + "_tmp", [P, group])

    def statistics(self, dve, steps, source):
        for j in range(self.group - 1):
            dve.bn_stats(self.stats[:, j, :], source(j))
        steps.link(dve.bn_stats(self.stats[:, self.group - 1, :], source(self.group - 1)))
        detach_wait(dve)
        for j in range(self.group - 1):
            dve.bn_aggr(self.mean_var[:, j, :], self.stats[:, j, :])
        steps.link(dve.bn_aggr(self.mean_var[:, self.group - 1, :], self.stats[:, self.group - 1, :]))
        rsqrt(dve, steps, self.mean_var[:, :, 1], self.half[:, :], self.root[:, :], self.tmp[:, :], LN_EPS)

    def apply(self, dve, out, source, j):
        return dve.tensor_scalar(out, source, self.mean_var[:, j, 0:1], self.root[:, j:j + 1],
                                 ALU.subtract, ALU.mult)


class Core:

    def __init__(self, nc, ctx, phase):
        self.nc, self.ctx, self.phase, self.sems = nc, ctx, phase, []
        ctx.callback(self.free_semaphores)

    def free_semaphores(self):
        self.nc.clear_and_free_semaphores(self.sems)
        self.nc.all_engine_barrier()

    def sb(self, name, shape, dt=F32):
        return self.ctx.enter_context(self.nc.sbuf_tensor(f"{self.phase}_{name}", shape, dt))

    def ps(self, name, shape, dt=F32):
        return self.ctx.enter_context(self.nc.psum_tensor(f"{self.phase}_{name}", shape, dt))

    def sem(self, name):
        self.sems.append(self.nc.alloc_semaphore(f"{self.phase}_{name}"))
        return self.sems[-1]


ATTN16 = [("wq", (KT, D)), ("wk", (KT, D)), ("wv", (KT, D)), ("wo", (KT, D)),
          ("bq", (2,)), ("bk", (2,)), ("bv", (D,)), ("bo", (D,))]
W64 = HEADS * 64
PARTS = {
    "L0x": ATTN16,
    "L0f": [("wm", (KT, D)), ("wo", (KT, D)), ("emb", (KT, P)), ("w1", (16, P)), ("w2", (16, 32)), ("b2", (KT, P)),
            ("b1", (16,)), ("bm", (KT,)), ("bo", (D,))],
    "L1x": ATTN16 + [("rf", (4, P))],
    "L1f": [("w1", (8, KT, 512)), ("w2", (8, 4, D)), ("wg", (KT, P)), ("bg", (8,)), ("b1", (8, 4)), ("b2", (8, D)),
            ("gamma", (D,)), ("beta", (D,))],
    "L2x": [("wq", (KT, W64)), ("wk", (KT, W64)), ("wv", (KT, W64)), ("wo", (8, D))],
    "L2f": [("w1", (KT, 1024)), ("w2", (8, D)), ("g1", (D,)), ("c1", (D,)), ("b1", (1024,)), ("g2", (1024,)),
            ("c2", (1024,)), ("b2", (D,))],
    "L3x": ATTN16 + [("mask", (P,))],
    "L3f": [("w1", (8, KT, 512)), ("w2", (8, 2, D)), ("wg", (KT, P)), ("bg", (8,))],
    "const": [("ident", (P,)), ("pick8", (8,)), ("pick2", (2,)), ("feat2", (2,)), ("causal", (P,)), ("half", (4, P)),
              ("headsum", (8,)), ("iota8", (8,)), ("iota16", (16,)), ("ones", (P,))],
}
SIDE = {"L0x": 1, "L1x": 1, "L2x": 1, "L3x": 1, "L0f": 0, "L1f": 0, "L2f": 0, "L3f": 0}


def columns(phase):
    return sum(int(np.prod(shape)) for _, shape in PARTS[phase])


def views(store, phase):
    out, at = {}, 0
    for name, shape in PARTS[phase]:
        n = int(np.prod(shape))
        v = store[:, at:at + n]
        if len(shape) == 2:
            v = v.rearrange("p (a b) -> p a b", a=shape[0])
        if len(shape) == 3:
            v = v.rearrange("p (a b c) -> p a b c", a=shape[0], b=shape[1])
        out[name] = v
        at += n
    return out


class Shared:

    def __init__(self, nc, ctx, dram):
        self.nc, self.dram = nc, dram
        self.x = ctx.enter_context(nc.sbuf_tensor("x_sb", [P, BATCH, D], F32))
        self.const_store = ctx.enter_context(nc.sbuf_tensor("const_sb", [P, columns("const")], F32))
        self.stores = [ctx.enter_context(nc.sbuf_tensor(f"params{s}", [P, max(columns(p) for p in SIDE if SIDE[p] == s)], F32))
                       for s in range(2)]
        self.kstab = ctx.enter_context(nc.sbuf_tensor("neg_kstab", [P, 1], F32))
        self.const = views(self.const_store, "const")
        self.loaded = {p: nc.alloc_semaphore(f"params_{p}") for p in SIDE}
        self.loads = {}
        self.x_loaded = nc.alloc_semaphore("x_loaded")
        self.const_loaded = nc.alloc_semaphore("const_loaded")

    def params(self, phase):
        return views(self.stores[SIDE[phase]], phase)

    def load_params(self, sp, phase):
        n, step, self.loads[phase] = columns(phase), 4096, 0
        for at in range(0, n, step):
            to = min(at + step, n)
            sp.dma_start(self.stores[SIDE[phase]][:, at:to], self.dram["p_" + phase][:, at:to]).then_inc(self.loaded[phase], 16)
            self.loads[phase] += 16

    def wait_params(self, eng, phase):
        eng.wait_ge(self.loaded[phase], self.loads[phase])


def first_loads(nc, sh, phases):
    with nc.Block() as block:
        @block.sync
        def _(sp):
            sp.dma_start(sh.const_store[:, :], sh.dram["p_const"]).then_inc(sh.const_loaded, 16)
            sh.load_params(sp, phases[0])
            for q in range(4):
                b = BATCH // 4
                sp.dma_start(sh.x[:, q * b:(q + 1) * b, :],
                             sh.dram["x"][q * b:(q + 1) * b].rearrange("b s d -> s b d")).then_inc(sh.x_loaded, 16)
            sp.wait_ge(sh.const_loaded, 16)
            sp.wait_ge(sh.x_loaded, 64)


def last_stores(nc, sh):
    stored = nc.alloc_semaphore("out_stored")
    with nc.Block() as block:
        @block.sync
        def _(sp):
            for q in range(4):
                b = BATCH // 4
                sp.dma_start(sh.dram["out"][q * b:(q + 1) * b].rearrange("b s d -> s b d"),
                             sh.x[:, q * b:(q + 1) * b, :]).then_inc(stored, 16)
            sp.wait_ge(stored, 64)


class Chunks:

    def __init__(self, emptied_by):
        self.by = emptied_by

    def total(self, who):
        return self.by.count(who)

    def emptied(self, c):
        return self.by[:c + 1].count(self.by[c])


def attention_phase(nc, sh, phase, dh, next_phase):
    G = 2
    TURNS = BATCH // G
    T = G * P
    W = HEADS * dh
    NT = W // P
    VAR = P // dh
    HW = dh + 1
    VW = HEADS * HW + P - HW
    UH = 4
    UB = HEADS // UH
    U = G * UB
    HO = HEADS if dh == 16 else UH
    biased = dh == 16
    masked = phase == "L3x"
    w, c = sh.params(phase), sh.const
    pick = c["pick8"] if dh == 16 else c["pick2"]
    NO = NT
    OC = -(-NO // 4)
    VC = 1 if dh == 16 else 2 * G
    chunks = Chunks(["v"] + ["a"] * (2 * NT // 2) + ["v"] * VC + (["a"] * OC + ["v"]) * G)
    CQ, CK, CV, CO = 1, 1 + NT // 2, 1 + NT, 1 + NT + VC
    NA, NV, NC = chunks.total("a"), chunks.total("v"), len(chunks.by)

    with ExitStack() as ctx:
        core = Core(nc, ctx, phase)
        norm = Norm(core, G)
        xn = core.sb("xn", [P, G, D])
        xnT = core.sb("xnT", [P, KT, T])
        cT = core.sb("ctxT", [P, KT, T])
        qT = core.sb("qT", [P, NT, T])
        kT = core.sb("kT", [P, NT, T])
        qm = core.sb("q_masked", [P, VAR, NT, T])
        v = core.sb("v_ones", [P, G, VW])
        d = core.sb("centered", [P, 2, UH, P])
        p = core.sb("probs", [P, 2, UH, P])
        pT = core.sb("probsT", [P, 2, UH, P])
        mx = core.sb("row_max", [P, 2, UH])
        rc = core.sb("recip_den", [P, 2, HO])
        o = qT[:, :, :].rearrange("p n t -> p (n t)").rearrange("p (j w) -> p j w", j=G)
        oT = core.sb("heads_outT", [P, NO, P])
        if masked:
            side = core.sb("side", [P, HEADS, P])
            pad_words = core.sb("pad", [P, BATCH, P // 4], I32)
            pad = pad_words[:, :, :].bitcast(U8)
            hm = core.sb("half_mask", [P, P])
            hmb = core.sb("half_mask_b", [P, P])
            sm = core.sb("side_mask", [P, 2, UH, P])
        S = core.ps("S", [P, 2, UH, P])
        PT = core.ps("PT", [P, 2, UH, P])
        O = core.ps("O", [P, 2, BANK])
        gen = core.ps("gen", [P, 2, BANK])

        ctx_loaded = core.sem("ctx_loaded")
        xn_ready, bias_added = core.sem("xn_ready"), core.sem("bias_added")
        filled, emptied_a, emptied_v = core.sem("gen_filled"), core.sem("gen_emptied_act"), core.sem("gen_emptied_dve")
        qm_ready = core.sem("q_masked_ready")
        v_set = core.sem("v_ones_set")
        scored, centered, exped = core.sem("scored"), core.sem("centered"), core.sem("exped")
        turned, turned_out = core.sem("probs_turned"), core.sem("probsT_ready")
        summed, normed = core.sem("heads_summed"), core.sem("heads_normed")
        dve_step = core.sem("dve_step")
        side_loaded, side_used, side_ready, pad_loaded, pool_step = (core.sem(s) for s in (
            "side_loaded", "side_used", "side_mask_ready", "pad_loaded", "pool_step"))
        x_loads = sh.dram["ctxT"]
        block = ctx.enter_context(nc.Block())
        emptied = {"a": (emptied_a, NA), "v": (emptied_v, NV)}

        @block.sync
        def _(sp):
            if next_phase:
                sh.load_params(sp, next_phase)

            def load_ctx(turn):
                sp.dma_start(cT[:, :, :], x_loads[:, :, bass.ts(turn, T)]).then_inc(ctx_loaded, 16)

            load_ctx(0)
            with sp.Fori(0, TURNS - 1) as i:
                sp.wait_ge(emptied_v, i * NV + 1 + VC)
                load_ctx(i + 1)

        @block.gpsimd
        def _(pool):
            pool.memset(v[:, :, :], 1.0).then_inc(v_set, 1)
            sh.wait_params(pool, phase)
            if masked:
                pool.dma_start(pad_words[:, :, :], sh.dram["pad"].partition_broadcast(P)).then_inc(pad_loaded, 16)
                pool.tensor_scalar(hm[:, :], w["mask"], 0.5, 1.0, ALU.mult, ALU.mult).then_inc(pool_step, 1)
                pool.wait_ge(pool_step, 1)
                pool.wait_ge(pad_loaded, 16)
            with pool.Fori(0, TURNS) as i:
                if biased:
                    pool.wait_ge(xn_ready, (i + 1) * G)
                    for j in range(G):
                        pool.tensor_tensor(sh.x[:, i * G + j, :], sh.x[:, i * G + j, :], w["bo"],
                                           ALU.add).then_inc(bias_added, 1)
                pool.wait_ge(emptied_a, i * NA + CK - CQ)
                detach_wait(pool)
                for m in range(VAR):
                    pool.tensor_scalar(qm[:, m, :, :], qT[:, :, :], pick[:, m:m + 1], 1.0,
                                       ALU.mult, ALU.mult).then_inc(qm_ready, 1)
                if masked:
                    for j in range(G):
                        pool.dma_start(side[:, :, :], sh.dram["side"][i * G + j].rearrange("h q k -> q h k")).then_inc(side_loaded, 16)
                        pool.tensor_copy(hmb[:, :], pad[:, i * G + j, :]).then_inc(pool_step, 1)
                        pool.wait_ge(pool_step, 1 + (i * G + j) * 3 + 1)
                        detach_wait(pool)
                        pool.tensor_scalar(hmb[:, :], hmb[:, :], -NEVER, 1.0, ALU.mult, ALU.mult).then_inc(pool_step, 1)
                        pool.wait_ge(pool_step, 1 + (i * G + j) * 3 + 2)
                        pool.tensor_tensor(hmb[:, :], hmb[:, :], hm[:, :], ALU.add).then_inc(pool_step, 1)
                        pool.wait_ge(pool_step, 1 + (i * G + j) * 3 + 3)
                        pool.wait_ge(side_loaded, (i * G + j + 1) * 16)
                        for r in range(UB):
                            n = j * UB + r
                            if n >= 2:
                                pool.wait_ge(side_used, i * U + n - 1)
                            pool.tensor_tensor(sm[:, n % 2, :, :], side[:, r * UH:(r + 1) * UH, :],
                                               hmb[:, :].unsqueeze(1).broadcast_to([P, UH, P]), ALU.add).then_inc(side_ready, 1)
                        pool.wait_ge(side_ready, (i * G + j + 1) * UB)

        @block.scalar
        def _(act):
            sh.wait_params(act, phase)
            with act.Fori(0, TURNS) as i:
                for ch in range(NT):
                    dst, bias = (qT, "bq") if ch < NT // 2 else (kT, "bk")
                    tile = (ch % (NT // 2)) * 2
                    cc = CQ + ch
                    act.wait_ge(filled, i * NC + cc + 1)
                    for t in range(2):
                        src = gen[:, cc % 2, t * T:(t + 1) * T]
                        if biased:
                            last = act.activation(dst[:, tile + t, :], src, ACT.Identity, bias=w[bias][:, tile + t:tile + t + 1])
                        elif t == 0:
                            last = act.activation(dst[:, tile:tile + 2, :], gen[:, cc % 2, :].rearrange("p (a b) -> p a b", a=2), ACT.Copy)
                    last.then_inc(emptied_a, 1)
                for u in range(U + 1):
                    if u < U:
                        act.wait_ge(centered, i * U + u + 1)
                        act.activation(p[:, u % 2, :, :], d[:, u % 2, :, :], ACT.Exp).then_inc(exped, 1)
                    if u >= 1:
                        act.wait_ge(turned, i * U + u)
                        act.activation(pT[:, (u - 1) % 2, :, :], PT[:, (u - 1) % 2, :, :], ACT.Copy).then_inc(turned_out, 1)
                for j in range(G):
                    for k in range(OC):
                        cc = CO + j * (OC + 1) + k
                        act.wait_ge(filled, i * NC + cc + 1)
                        n = min(4, NO - 4 * k)
                        act.activation(oT[:, 4 * k:4 * k + n, :], gen[:, cc % 2, 0:n * P].rearrange("p (a b) -> p a b", a=n),
                                       ACT.Copy).then_inc(emptied_a, 1)

        @block.tensor
        def _(pe):
            def free_bank(i, cc):
                if cc >= 2:
                    s, per = emptied[chunks.by[cc - 2]]
                    pe.wait_ge(s, i * per + chunks.emptied(cc - 2))

            def project(i, cc, weights, source, tile):
                free_bank(i, cc)
                for t in range(2):
                    for k in range(KT):
                        mm = pe.matmul(gen[:, cc % 2, t * T:(t + 1) * T], weights[:, k, (tile + t) * P:(tile + t + 1) * P],
                                       source[:, k, :], start=(k == 0), stop=(k == KT - 1))
                mm.then_inc(filled, 1)

            sh.wait_params(pe, phase)
            with pe.Fori(0, TURNS) as i:
                pe.wait_ge(xn_ready, (i + 1) * G)
                for k in range(KT):
                    for j in range(G):
                        mm = pe.transpose(gen[:, 0, k * T + j * P:k * T + (j + 1) * P], xn[:, j, k * P:(k + 1) * P], c["ident"])
                mm.then_inc(filled, 1)
                pe.wait_ge(emptied_v, i * NV + 1)
                for n in range(NT // 2):
                    project(i, CQ + n, w["wq"], xnT, 2 * n)
                pe.wait_ge(ctx_loaded, (i + 1) * 16)
                for n in range(NT // 2):
                    project(i, CK + n, w["wk"], cT, 2 * n)
                if dh == 16:
                    free_bank(i, CV)
                    for j in range(G):
                        for k in range(KT):
                            mm = pe.matmul(gen[:, CV % 2, j * D:(j + 1) * D], cT[:, k, j * P:(j + 1) * P], w["wv"][:, k, :],
                                           start=(k == 0), stop=(k == KT - 1))
                    mm.then_inc(filled, 1)
                else:
                    for n in range(VC):
                        free_bank(i, CV + n)
                        j, half = n // 2, n % 2
                        for k in range(KT):
                            mm = pe.matmul(gen[:, (CV + n) % 2, :], cT[:, k, j * P:(j + 1) * P],
                                           w["wv"][:, k, half * BANK:(half + 1) * BANK], start=(k == 0), stop=(k == KT - 1))
                        mm.then_inc(filled, 1)
                pe.wait_ge(emptied_a, i * NA + NT)
                for u in range(U + 2):
                    if u < U:
                        j, h0 = u // UB, (u % UB) * UH
                        if u < UB:
                            pe.wait_ge(qm_ready, i * VAR + min(h0 + UH, VAR))
                        if u >= 2:
                            pe.wait_ge(centered, i * U + u - 1)
                        for r in range(UH):
                            h = h0 + r
                            mm = pe.matmul(S[:, u % 2, r, :], qm[:, h % VAR, h // VAR, j * P:(j + 1) * P],
                                           kT[:, h // VAR, j * P:(j + 1) * P], start=True, stop=True)
                        mm.then_inc(scored, 1)
                    if 1 <= u <= U:
                        n = u - 1
                        pe.wait_ge(exped, i * U + n + 1)
                        if n >= 2:
                            pe.wait_ge(turned_out, i * U + n - 1)
                        for r in range(UH):
                            mm = pe.transpose(PT[:, n % 2, r, :], p[:, n % 2, r, :], c["ident"])
                        mm.then_inc(turned, 1)
                    if u >= 2:
                        n = u - 2
                        j, h0 = n // UB, (n % UB) * UH
                        if n == 0:
                            pe.wait_ge(emptied_v, i * NV + 1 + VC)
                        pe.wait_ge(turned_out, i * U + n + 1)
                        if dh != 16 and n >= 2:
                            pe.wait_ge(normed, i * U + n - 1)
                        bank, first = (j, 0) if dh == 16 else (n % 2, h0)
                        for r in range(UH):
                            h = h0 + r
                            mm = pe.matmul(O[:, bank, (h - first) * HW:(h - first) * HW + P], pT[:, n % 2, r, :],
                                           v[:, j, h * HW:h * HW + P], start=True, stop=True, skip_group_check=True)
                        if dh != 16 or n % UB == UB - 1:
                            mm.then_inc(summed, 1)
                per = G if dh == 16 else U
                for j in range(G):
                    pe.wait_ge(normed, i * per + (j + 1) * per // G)
                    for k in range(OC):
                        cc = CO + j * (OC + 1) + k
                        free_bank(i, cc)
                        for t in range(4 * k, min(4 * k + 4, NO)):
                            mm = pe.transpose(gen[:, cc % 2, (t - 4 * k) * P:(t - 4 * k + 1) * P], o[:, j, t * P:(t + 1) * P], c["ident"])
                        mm.then_inc(filled, 1)
                    cc = CO + j * (OC + 1) + OC
                    free_bank(i, cc)
                    pe.wait_ge(emptied_a, i * NA + NT + (j + 1) * OC)
                    for t in range(NO):
                        mm = pe.matmul(gen[:, cc % 2, 0:D], oT[:, t, :], w["wo"][:, t, :], start=(t == 0), stop=(t == NO - 1))
                    mm.then_inc(filled, 1)

        @block.vector
        def _(dve):
            steps_per_turn = Norm.STEPS + (G if dh == 16 else U) + U
            sh.wait_params(dve, phase)
            dve.wait_ge(v_set, 1)
            with dve.Fori(0, TURNS) as i:
                steps = Steps(dve, dve_step, i * steps_per_turn, steps_per_turn)
                norm.statistics(dve, steps, lambda j: sh.x[:, i * G + j, :])
                for j in range(G):
                    norm.apply(dve, xn[:, j, :], sh.x[:, i * G + j, :], j).then_inc(xn_ready, 1)
                dve.wait_ge(filled, i * NC + 1)
                dve.tensor_copy(xnT[:, :, :], gen[:, 0, :].rearrange("p (a b) -> p a b", a=KT)).then_inc(emptied_v, 1)
                for n in range(VC):
                    cc = CV + n
                    dve.wait_ge(filled, i * NC + cc + 1)
                    if dh == 16:
                        for j in range(G):
                            last = dve.tensor_tensor(v[:, j, 0:HEADS * HW].rearrange("p (h e) -> p h e", e=HW)[:, :, 0:dh],
                                                     gen[:, cc % 2, j * D:(j + 1) * D].rearrange("p (h e) -> p h e", e=dh),
                                                     w["bv"].rearrange("p (h e) -> p h e", e=dh), ALU.add)
                        last.then_inc(emptied_v, 1)
                    else:
                        j, h0 = n // 2, (n % 2) * 8
                        dve.tensor_copy(v[:, j, h0 * HW:(h0 + 8) * HW].rearrange("p (h e) -> p h e", e=HW)[:, :, 0:dh],
                                        gen[:, cc % 2, :].rearrange("p (h e) -> p h e", e=dh)).then_inc(emptied_v, 1)

                def normalize(n):
                    dve.wait_ge(summed, (i * (G if dh == 16 else U)) + n + 1)
                    ps = O[:, n % 2, 0:HO * HW].rearrange("p (h e) -> p h e", e=HW)
                    steps.link(dve.reciprocal(rc[:, n % 2, :].unsqueeze(2), ps[:, :, dh:HW]))
                    j, h0 = (n, 0) if dh == 16 else (n // UB, (n % UB) * UH)
                    dve.tensor_tensor(o[:, j, h0 * dh:(h0 + HO) * dh].rearrange("p (h e) -> p h e", e=dh), ps[:, :, 0:dh],
                                      rc[:, n % 2, :].unsqueeze(2).broadcast_to([P, HO, dh]), ALU.mult).then_inc(normed, 1)

                for u in range(U + 3):
                    if u < U:
                        dve.wait_ge(scored, i * U + u + 1)
                        scores = S[:, u % 2, :, :]
                        if masked:
                            dve.wait_ge(side_ready, i * U + u + 1)
                            if u >= 2:
                                dve.wait_ge(exped, i * U + u - 1)
                            dve.scalar_tensor_tensor(out=d[:, u % 2, :, :].rearrange("p a b -> p (a b)"),
                                                     in0=sm[:, u % 2, :, :].rearrange("p a b -> p (a b)"), scalar=2.0,
                                                     in1=scores.rearrange("p a b -> p (a b)"), op0=ALU.mult, op1=ALU.add).then_inc(side_used, 1)
                            dve.wait_ge(side_used, i * U + u + 1)
                            scores = d[:, u % 2, :, :]
                        elif u >= 2:
                            dve.wait_ge(exped, i * U + u - 1)
                        steps.link(dve.tensor_reduce(mx[:, u % 2, :], scores, AX.X, ALU.max))
                        dve.tensor_tensor(d[:, u % 2, :, :], scores, mx[:, u % 2, :].unsqueeze(2).broadcast_to([P, UH, P]),
                                          ALU.subtract).then_inc(centered, 1)
                    if dh != 16 and u >= 3:
                        normalize(u - 3)
                    if dh == 16 and u >= UB + 2 and (u - UB - 2) % UB == 0:
                        normalize((u - UB - 2) // UB)
                for j in range(G):
                    cc = CO + j * (OC + 1) + OC
                    dve.wait_ge(filled, i * NC + cc + 1)
                    if biased:
                        dve.wait_ge(bias_added, i * G + j + 1)
                    dve.tensor_tensor(sh.x[:, i * G + j, :], gen[:, cc % 2, 0:D], sh.x[:, i * G + j, :], ALU.add).then_inc(emptied_v, 1)
                dve.wait_ge(emptied_v, (i + 1) * NV)
                steps.close()


def key_bound(nc, sh, w):
    T = 512
    TURNS = BATCH * P // T
    c = sh.const
    with ExitStack() as ctx:
        core = Core(nc, ctx, "kstab")
        cT = core.sb("ctxT", [P, KT, T])
        k2 = core.sb("k_squared", [P, KT, T])
        bk = core.sb("bk_scaled", [P, 2])
        top = core.sb("top", [P, TURNS])
        top1 = core.sb("top1", [P, 1])
        topT = core.sb("topT", [P, 1])
        K = core.ps("K", [P, 2, T])
        H = core.ps("H", [P, 2, T])
        loaded, projected, squared, headed, topped, step = (core.sem(s) for s in (
            "ctx_loaded", "projected", "squared", "headed", "topped", "dve_step"))
        block = ctx.enter_context(nc.Block())

        @block.sync
        def _(sp):
            sp.dma_start(cT[:, :, :], sh.dram["ctxT"][:, :, 0:T]).then_inc(loaded, 16)
            with sp.Fori(0, TURNS - 1) as i:
                sp.wait_ge(projected, i + 1)
                sp.dma_start(cT[:, :, :], sh.dram["ctxT"][:, :, bass.ts(i + 1, T)]).then_inc(loaded, 16)

        @block.tensor
        def _(pe):
            sh.wait_params(pe, "L1x")
            with pe.Fori(0, TURNS) as i:
                pe.wait_ge(loaded, (i + 1) * 16)
                for t in range(2):
                    for k in range(KT):
                        mm = pe.matmul(K[:, t, :], w["wk"][:, k, t * P:(t + 1) * P], cT[:, k, :], start=(k == 0), stop=(k == 1))
                mm.then_inc(projected, 1)
                pe.wait_ge(squared, (i + 1) * 2)
                pe.wait_ge(topped, i + 1)
                for t in range(2):
                    mm = pe.matmul(H[0:8, t, :], c["headsum"], k2[:, t, :], start=True, stop=True)
                mm.then_inc(headed, 1)
            pe.wait_ge(step, 2)
            pe.transpose(H[0:1, 0, 0:8], top1[0:8, 0:1], c["ident"][0:8, 0:8]).then_inc(headed, 1)
            pe.wait_ge(step, 3)
            pe.matmul(H[:, 1, 0:1], c["ones"][0:1, :], topT[0:1, :], start=True, stop=True).then_inc(headed, 1)

        @block.scalar
        def _(act):
            act.wait_ge(step, 1)
            with act.Fori(0, TURNS) as i:
                act.wait_ge(projected, i + 1)
                for t in range(2):
                    act.activation(k2[:, t, :], K[:, t, :], ACT.Square, bias=bk[:, t:t + 1], scale=0.25).then_inc(squared, 1)

        @block.vector
        def _(dve):
            sh.wait_params(dve, "L1x")
            dve.tensor_scalar(bk[:, :], w["bk"], 0.25, None, ALU.mult).then_inc(step, 1)
            dve.sem_inc(topped, 1)
            with dve.Fori(0, TURNS) as i:
                dve.wait_ge(headed, i + 1)
                dve.tensor_reduce(top[0:8, bass.ds(i, 1)], H[0:8, :, :].rearrange("p a b -> p (a b)"), AX.X, ALU.max).then_inc(topped, 1)
            dve.wait_ge(topped, TURNS + 1)
            dve.tensor_reduce(top1[0:8, :], top[0:8, :], AX.X, ALU.max).then_inc(step, 1)
            dve.wait_ge(headed, TURNS + 1)
            dve.tensor_reduce(topT[0:1, :], H[0:1, 0, 0:8], AX.X, ALU.max).then_inc(step, 1)
            dve.wait_ge(headed, TURNS + 2)
            dve.tensor_scalar(sh.kstab[:, :], H[:, 1, 0:1], -1.0, None, ALU.mult).then_inc(step, 1)
            dve.wait_ge(step, 4)


def performer_phase(nc, sh, phase, next_phase):
    G = 2
    TURNS = BATCH // G
    T = G * P
    dh, HW = 16, 17
    VW = HEADS * HW + P - HW
    UH, UB = 4, 4
    U = G * UB
    PAIRS = HEADS // 2
    EPS, STAB = 1e-4, 1e-6
    w, c = sh.params(phase), sh.const
    chunks = Chunks(["v", "a", "a"] + ["a"] * 8 + ["v"] + ["a", "v"] * G)
    CFQ, CFK, CV, CO = 3, 7, 11, 12
    NA, NV, NC = chunks.total("a"), chunks.total("v"), len(chunks.by)
    key_bound(nc, sh, w)

    with ExitStack() as ctx:
        core = Core(nc, ctx, phase)
        norm = Norm(core, G)
        xn = core.sb("xn", [P, G, D])
        xnT = core.sb("xnT", [P, KT, T])
        cT = core.sb("ctxT", [P, KT, T])
        qT = core.sb("qT", [P, 2, T])
        kT = core.sb("kT", [P, 2, T])
        k2 = core.sb("k_squared", [P, 2, T])
        b4 = core.sb("biases_scaled", [P, 2, 2])
        qe = core.sb("q_exp", [P, PAIRS, T])
        kf = core.sb("k_features", [P, PAIRS, T])
        qf = core.sb("q_features", [P, 2, PAIRS, T])
        v = core.sb("v_ones", [P, G, VW])
        at = core.sb("products", [P, 2, UH, P])
        den = core.sb("den", [P, HEADS])
        low = core.sb("den_low", [P, HEADS])
        o = core.sb("heads_out", [P, G, D])
        oT = core.sb("heads_outT", [P, 2, P])
        S = core.ps("S", [P, 2, UH, P])
        O = core.ps("O", [P, 2, BANK])
        gen = core.ps("gen", [P, 2, BANK])
        (ctx_loaded, xn_ready, bias_added, filled, emptied_a, emptied_v, qf_ready, kf_ready, v_set, scored, cut, summed,
         normed, dve_step, squared, scaled) = (core.sem(s) for s in (
            "ctx_loaded", "xn_ready", "bias_added", "gen_filled", "gen_emptied_act", "gen_emptied_dve", "q_features",
            "k_features", "v_ones_set", "scored", "cut", "heads_summed", "heads_normed", "dve_step", "k_squared", "scaled"))
        block = ctx.enter_context(nc.Block())
        emptied = {"a": (emptied_a, NA), "v": (emptied_v, NV)}

        @block.sync
        def _(sp):
            if next_phase:
                sh.load_params(sp, next_phase)
            sp.dma_start(cT[:, :, :], sh.dram["ctxT"][:, :, 0:T]).then_inc(ctx_loaded, 16)
            with sp.Fori(0, TURNS - 1) as i:
                sp.wait_ge(emptied_v, i * NV + 2)
                sp.dma_start(cT[:, :, :], sh.dram["ctxT"][:, :, bass.ts(i + 1, T)]).then_inc(ctx_loaded, 16)

        @block.gpsimd
        def _(pool):
            pool.memset(v[:, :, :], 1.0).then_inc(v_set, 1)
            sh.wait_params(pool, phase)
            with pool.Fori(0, TURNS) as i:
                pool.wait_ge(xn_ready, (i + 1) * G)
                for j in range(G):
                    pool.tensor_tensor(sh.x[:, i * G + j, :], sh.x[:, i * G + j, :], w["bo"], ALU.add).then_inc(bias_added, 1)
                for n in range(4):
                    pool.wait_ge(emptied_a, i * NA + CFQ + n)
                    detach_wait(pool)
                    for m in range(2):
                        pool.tensor_scalar(qf[:, m, 2 * n:2 * n + 2, :], qe[:, 2 * n:2 * n + 2, :], EPS, c["feat2"][:, m:m + 1],
                                           ALU.add, ALU.mult).then_inc(qf_ready, 1)

        @block.scalar
        def _(act):
            sh.wait_params(act, phase)
            for n, bias in enumerate(("bq", "bk")):
                act.activation(b4[:, n, :], w[bias], ACT.Copy, scale=0.25).then_inc(scaled, 1)
            act.wait_ge(scaled, 2)
            with act.Fori(0, TURNS) as i:
                for n, dst in enumerate((qT, kT)):
                    act.wait_ge(filled, i * NC + n + 2)
                    for t in range(2):
                        last = act.activation(dst[:, t, :], gen[:, (n + 1) % 2, t * T:(t + 1) * T], ACT.Identity,
                                              bias=b4[:, n, t:t + 1], scale=0.25)
                    last.then_inc(emptied_a, 1)
                act.wait_ge(emptied_a, i * NA + 2)
                act.activation(k2[:, :, :], kT[:, :, :], ACT.Square).then_inc(squared, 1)
                for n in range(8):
                    cc = CFQ + n
                    act.wait_ge(filled, i * NC + cc + 1)
                    src = gen[:, cc % 2, :].rearrange("p (a b) -> p a b", a=2)
                    if n < 4:
                        act.activation(qe[:, 2 * n:2 * n + 2, :], src, ACT.Exp).then_inc(emptied_a, 1)
                    else:
                        act.activation(kf[:, 2 * n - 8:2 * n - 6, :], src, ACT.Exp, bias=sh.kstab[:, :]).then_inc(emptied_a, 1)
                for j in range(G):
                    cc = CO + 2 * j
                    act.wait_ge(filled, i * NC + cc + 1)
                    act.activation(oT[:, :, :], gen[:, cc % 2, 0:D].rearrange("p (a b) -> p a b", a=2), ACT.Copy).then_inc(emptied_a, 1)

        @block.tensor
        def _(pe):
            def free_bank(i, cc):
                if cc >= 2:
                    s, per = emptied[chunks.by[cc - 2]]
                    pe.wait_ge(s, i * per + chunks.emptied(cc - 2))

            sh.wait_params(pe, phase)
            with pe.Fori(0, TURNS) as i:
                pe.wait_ge(xn_ready, (i + 1) * G)
                for k in range(KT):
                    for j in range(G):
                        mm = pe.transpose(gen[:, 0, k * T + j * P:k * T + (j + 1) * P], xn[:, j, k * P:(k + 1) * P], c["ident"])
                mm.then_inc(filled, 1)
                for n, (weights, source) in enumerate(((w["wq"], xnT), (w["wk"], cT))):
                    if n == 0:
                        pe.wait_ge(emptied_v, i * NV + 1)
                    else:
                        free_bank(i, 2)
                        pe.wait_ge(ctx_loaded, (i + 1) * 16)
                    for t in range(2):
                        for k in range(KT):
                            mm = pe.matmul(gen[:, (n + 1) % 2, t * T:(t + 1) * T], weights[:, k, t * P:(t + 1) * P], source[:, k, :],
                                           start=(k == 0), stop=(k == KT - 1))
                    mm.then_inc(filled, 1)
                for n in range(8):
                    cc = CFQ + n
                    free_bank(i, cc)
                    if n == 0:
                        pe.wait_ge(emptied_a, i * NA + 2)
                    if n == 4:
                        pe.wait_ge(squared, i + 1)
                    for a in range(2):
                        t, s = divmod((2 * n + a) % PAIRS, 4)
                        out = gen[:, cc % 2, a * T:(a + 1) * T]
                        mm = pe.matmul(out, w["rf"][:, s, :], (qT if n < 4 else kT)[:, t, :], start=True, stop=(n < 4))
                        if n >= 4:
                            mm = pe.matmul(out, c["half"][:, s, :], k2[:, t, :], start=False, stop=True)
                    mm.then_inc(filled, 1)
                free_bank(i, CV)
                for j in range(G):
                    for k in range(KT):
                        mm = pe.matmul(gen[:, CV % 2, j * D:(j + 1) * D], cT[:, k, j * P:(j + 1) * P], w["wv"][:, k, :],
                                       start=(k == 0), stop=(k == KT - 1))
                mm.then_inc(filled, 1)
                pe.wait_ge(emptied_v, i * NV + 2)
                for u in range(U + 1):
                    if u < U:
                        j, h0 = u // UB, (u % UB) * UH
                        if u < UB:
                            pe.wait_ge(qf_ready, i * 8 + 2 * u + 2)
                            pe.wait_ge(kf_ready, i * 4 + u + 1)
                        if u >= 2:
                            pe.wait_ge(cut, i * U + u - 1)
                        for r in range(UH):
                            h = h0 + r
                            mm = pe.matmul(S[:, u % 2, r, :], kf[:, h // 2, j * P:(j + 1) * P],
                                           qf[:, h % 2, h // 2, j * P:(j + 1) * P], start=True, stop=True)
                        mm.then_inc(scored, 1)
                    if u >= 1:
                        n = u - 1
                        j, h0 = n // UB, (n % UB) * UH
                        pe.wait_ge(cut, i * U + n + 1)
                        for r in range(UH):
                            h = h0 + r
                            mm = pe.matmul(O[:, j, h * HW:h * HW + P], at[:, n % 2, r, :], v[:, j, h * HW:h * HW + P],
                                           start=True, stop=True, skip_group_check=True)
                        if n % UB == UB - 1:
                            mm.then_inc(summed, 1)
                for j in range(G):
                    pe.wait_ge(normed, i * G + j + 1)
                    free_bank(i, CO + 2 * j)
                    for t in range(2):
                        mm = pe.transpose(gen[:, (CO + 2 * j) % 2, t * P:(t + 1) * P], o[:, j, t * P:(t + 1) * P], c["ident"])
                    mm.then_inc(filled, 1)
                    free_bank(i, CO + 2 * j + 1)
                    pe.wait_ge(emptied_a, i * NA + 10 + j + 1)
                    for t in range(2):
                        mm = pe.matmul(gen[:, (CO + 2 * j + 1) % 2, 0:D], oT[:, t, :], w["wo"][:, t, :], start=(t == 0), stop=(t == 1))
                    mm.then_inc(filled, 1)

        @block.vector
        def _(dve):
            steps_per_turn = Norm.STEPS + 4 * G
            sh.wait_params(dve, phase)
            dve.wait_ge(v_set, 1)
            with dve.Fori(0, TURNS) as i:
                steps = Steps(dve, dve_step, i * steps_per_turn, steps_per_turn)
                norm.statistics(dve, steps, lambda j: sh.x[:, i * G + j, :])
                for j in range(G):
                    norm.apply(dve, xn[:, j, :], sh.x[:, i * G + j, :], j).then_inc(xn_ready, 1)
                dve.wait_ge(filled, i * NC + 1)
                dve.tensor_copy(xnT[:, :, :], gen[:, 0, :].rearrange("p (a b) -> p a b", a=KT)).then_inc(emptied_v, 1)
                for n in range(4):
                    dve.wait_ge(emptied_a, i * NA + CFK + n)
                    dve.tensor_scalar(kf[:, 2 * n:2 * n + 2, :], kf[:, 2 * n:2 * n + 2, :], EPS, 0.125, ALU.add, ALU.mult).then_inc(kf_ready, 1)
                dve.wait_ge(filled, i * NC + CV + 1)
                for j in range(G):
                    last = dve.tensor_tensor(v[:, j, 0:HEADS * HW].rearrange("p (h e) -> p h e", e=HW)[:, :, 0:dh],
                                             gen[:, CV % 2, j * D:(j + 1) * D].rearrange("p (h e) -> p h e", e=dh),
                                             w["bv"].rearrange("p (h e) -> p h e", e=dh), ALU.add)
                last.then_inc(emptied_v, 1)

                def normalize(j):
                    dve.wait_ge(summed, i * G + j + 1)
                    ps = O[:, j, 0:HEADS * HW].rearrange("p (h e) -> p h e", e=HW)
                    steps.link(dve.tensor_copy(den[:, :].unsqueeze(2), ps[:, :, dh:HW]))
                    steps.link(dve.tensor_scalar(low[:, :], den[:, :], STAB, 2.0 * STAB, ALU.is_le, ALU.mult))
                    steps.link(dve.tensor_tensor(den[:, :], den[:, :], low[:, :], ALU.add))
                    steps.link(dve.reciprocal(den[:, :], den[:, :]))
                    dve.tensor_tensor(o[:, j, :].rearrange("p (h e) -> p h e", e=dh), ps[:, :, 0:dh],
                                      den[:, :].unsqueeze(2).broadcast_to([P, HEADS, dh]), ALU.mult).then_inc(normed, 1)

                for u in range(U + 2):
                    if u < U:
                        dve.wait_ge(scored, i * U + u + 1)
                        dve.tensor_tensor(at[:, u % 2, :, :], S[:, u % 2, :, :], c["causal"].unsqueeze(1).broadcast_to([P, UH, P]),
                                          ALU.mult).then_inc(cut, 1)
                    if u >= UB + 1 and (u - UB - 1) % UB == 0:
                        normalize((u - UB - 1) // UB)
                for j in range(G):
                    dve.wait_ge(filled, i * NC + CO + 2 * j + 2)
                    dve.wait_ge(bias_added, i * G + j + 1)
                    dve.tensor_tensor(sh.x[:, i * G + j, :], gen[:, (CO + 2 * j + 1) % 2, 0:D], sh.x[:, i * G + j, :],
                                      ALU.add).then_inc(emptied_v, 1)
                dve.wait_ge(emptied_v, (i + 1) * NV)
                steps.close()


def first_of_max(dve, steps, out, scores, best, marks, iota, n, size):
    steps.link(dve.tensor_reduce(best, scores, AX.X, ALU.max))
    steps.link(dve.tensor_tensor(marks, scores, best.unsqueeze(2).broadcast_to([P, n, size]), ALU.is_equal))
    steps.link(dve.scalar_tensor_tensor(out=marks, in0=marks, scalar=-float(size), in1=iota, op0=ALU.mult, op1=ALU.add))
    return marks


FIRST_STEPS = 5


def top_two(dve, steps, chosen, scores, rest, marks, best, second, iota, n, size):
    wide = lambda a: a.unsqueeze(2).broadcast_to([P, n, size])
    first_of_max(dve, steps, chosen, scores, best, marks, iota, n, size)
    steps.link(dve.tensor_reduce(second, marks, AX.X, ALU.min))
    steps.link(dve.tensor_tensor(chosen, marks, wide(second), ALU.is_equal))
    steps.link(dve.scalar_tensor_tensor(out=rest, in0=chosen, scalar=-NEVER, in1=scores, op0=ALU.mult, op1=ALU.add))
    first_of_max(dve, steps, chosen, rest, second, marks, iota, n, size)
    steps.link(dve.tensor_reduce(second, marks, AX.X, ALU.min))
    steps.link(dve.tensor_tensor(marks, marks, wide(second), ALU.is_equal))
    steps.link(dve.tensor_tensor(chosen, chosen, marks, ALU.add))


TOP_TWO_STEPS = 12


def experts_phase(nc, sh, phase, next_phase):
    G = 4
    TURNS = BATCH // G
    T = G * P
    E = 8
    relu = phase == "L1f"
    NF = 4 if relu else 2
    w, c = sh.params(phase), sh.const
    with ExitStack() as ctx:
        core = Core(nc, ctx, phase)
        norm = Norm(core, G)
        xn = core.sb("xn", [P, G, D])
        xnT = core.sb("xnT", [P, KT, T])
        hid = core.sb("hidden", [P, 2, NF, T])
        acc = core.sb("mixed", [P, G, D])
        lg, rest, marks, chosen, gate = (core.sb(n, [P, G, E]) for n in ("logits", "rest", "marks", "chosen", "gates"))
        best, second, total = (core.sb(n, [P, G]) for n in ("best", "second", "total"))
        if relu:
            norm2 = Norm(core, G, "close")
        else:
            silu = core.sb("silu", [P, 2, T])
        Z = core.ps("Z", [P, 4, T])
        Y = core.ps("Y", [P, 2, 2, D])
        gen = core.ps("gen", [P, 2, T])
        (xn_ready, filled, xT_v, xT_a, logits_read, hid_pre, hid_a, hid_v, summed, mixed, dve_step, centered, exped,
         bias_added) = (core.sem(s) for s in (
            "xn_ready", "gen_filled", "xnT_dve", "xnT_act", "logits_read", "hidden_summed", "hidden_act", "hidden_dve",
            "outputs_summed", "outputs_mixed", "dve_step", "logits_centered", "logits_exped", "bias_added"))
        block = ctx.enter_context(nc.Block())

        @block.sync
        def _(sp):
            if next_phase:
                sh.load_params(sp, next_phase)

        @block.gpsimd
        def _(pool):
            if relu:
                sh.wait_params(pool, phase)
                with pool.Fori(0, TURNS) as i:
                    pool.wait_ge(xn_ready, (i + 1) * G)
                    for j in range(G):
                        pool.tensor_tensor(sh.x[:, i * G + j, :], sh.x[:, i * G + j, :], w["beta"], ALU.add).then_inc(bias_added, 1)

        @block.scalar
        def _(act):
            sh.wait_params(act, phase)
            with act.Fori(0, TURNS) as i:
                act.wait_ge(filled, i * 3 + 2)
                act.activation(xnT[:, 1, :], gen[:, 1, :], ACT.Copy).then_inc(xT_a, 1)

                def exps():
                    act.wait_ge(centered, i + 1)
                    act.activation(gate[:, :, :], gate[:, :, :], ACT.Exp).then_inc(exped, 1)

                if relu:
                    exps()
                for e in range(E):
                    if e >= 2:
                        act.wait_ge(summed, (i * E + e - 1) * 2)
                    for f in range(NF):
                        act.wait_ge(hid_pre, (i * E + e) * 4 + f + 1)
                        if relu:
                            act.activation(hid[:, e % 2, f, :], Z[:, f, :], ACT.Relu, bias=w["b1"][:, e, f:f + 1]).then_inc(hid_a, 1)
                        else:
                            if e >= 1:
                                act.wait_ge(hid_v, (i * E + e - 1) * 2 + f + 1)
                            act.activation(silu[:, f, :], Z[:, f, :], ACT.Silu).then_inc(hid_a, 1)
                    if e == 0 and not relu:
                        exps()

        @block.tensor
        def _(pe):
            sh.wait_params(pe, phase)
            with pe.Fori(0, TURNS) as i:
                pe.wait_ge(xn_ready, (i + 1) * G)
                for k in range(KT):
                    for j in range(G):
                        mm = pe.transpose(gen[:, k, j * P:(j + 1) * P], xn[:, j, k * P:(k + 1) * P], c["ident"])
                    mm.then_inc(filled, 1)
                pe.wait_ge(xT_v, i + 1)
                pe.wait_ge(xT_a, i + 1)
                for j in range(G):
                    for k in range(KT):
                        mm = pe.matmul(gen[:, 0, j * P:(j + 1) * P], xnT[:, k, j * P:(j + 1) * P], w["wg"][:, k, :],
                                       start=(k == 0), stop=(k == KT - 1))
                mm.then_inc(filled, 1)
                for e in range(E + 1):
                    if e < E:
                        for f in range(4):
                            if e >= 1:
                                if relu:
                                    pe.wait_ge(hid_a, (i * E + e - 1) * 4 + f + 1)
                                elif f < 2:
                                    pe.wait_ge(hid_a, (i * E + e - 1) * 2 + f + 1)
                                else:
                                    pe.wait_ge(hid_v, (i * E + e - 1) * 2 + f - 1)
                            for k in range(KT):
                                mm = pe.matmul(Z[:, f, :], w["w1"][:, e, k, f * P:(f + 1) * P], xnT[:, k, :],
                                               start=(k == 0), stop=(k == KT - 1))
                            mm.then_inc(hid_pre, 1)
                    if e >= 1:
                        m = e - 1
                        if relu:
                            pe.wait_ge(hid_a, (i * E + m + 1) * 4)
                        else:
                            pe.wait_ge(hid_v, (i * E + m + 1) * 2)
                        for pair in range(2):
                            if m >= 1:
                                pe.wait_ge(mixed, (i * E + m - 1) * 2 + pair + 1)
                            for j in range(2):
                                b = 2 * pair + j
                                for f in range(NF):
                                    mm = pe.matmul(Y[:, pair, j, :], hid[:, m % 2, f, b * P:(b + 1) * P], w["w2"][:, m, f, :],
                                                   start=(f == 0), stop=(f == NF - 1))
                            mm.then_inc(summed, 1)

        @block.vector
        def _(dve):
            per = Norm.STEPS + TOP_TWO_STEPS + (7 + E + 1 + Norm.STEPS + 2 if relu else 7)
            sh.wait_params(dve, phase)
            with dve.Fori(0, TURNS) as i:
                steps = Steps(dve, dve_step, i * per, per)
                norm.statistics(dve, steps, lambda j: sh.x[:, i * G + j, :])
                for j in range(G):
                    norm.apply(dve, xn[:, j, :], sh.x[:, i * G + j, :], j).then_inc(xn_ready, 1)
                dve.wait_ge(filled, i * 3 + 1)
                dve.tensor_copy(xnT[:, 0, :], gen[:, 0, :]).then_inc(xT_v, 1)

                def multiply(e):
                    for f in range(2):
                        if e >= 2 and f == 0:
                            dve.wait_ge(summed, (i * E + e - 1) * 2)
                        dve.wait_ge(hid_a, (i * E + e) * 2 + f + 1)
                        dve.wait_ge(hid_pre, (i * E + e) * 4 + f + 3)
                        dve.tensor_tensor(hid[:, e % 2, f, :], silu[:, f, :], Z[:, f + 2, :], ALU.mult).then_inc(hid_v, 1)

                dve.wait_ge(filled, i * 3 + 3)
                steps.link(dve.tensor_tensor(lg[:, :, :], gen[:, 0, :].rearrange("p (j e) -> p j e", j=G)[:, :, 0:E],
                                             w["bg"].unsqueeze(1).broadcast_to([P, G, E]), ALU.add))
                steps.link(dve.tensor_reduce(best[:, :], lg[:, :, :], AX.X, ALU.max))
                dve.tensor_tensor(gate[:, :, :], lg[:, :, :], best[:, :].unsqueeze(2).broadcast_to([P, G, E]),
                                  ALU.subtract).then_inc(centered, 1)
                dve.wait_ge(centered, i + 1)
                if not relu:
                    multiply(0)
                top_two(dve, steps, chosen[:, :, :], lg[:, :, :], rest[:, :, :], marks[:, :, :], best[:, :], second[:, :],
                        c["iota8"].unsqueeze(1).broadcast_to([P, G, E]), G, E)
                dve.wait_ge(exped, i + 1)
                steps.link(dve.tensor_tensor(gate[:, :, :], gate[:, :, :], chosen[:, :, :], ALU.mult))
                steps.link(dve.tensor_reduce(total[:, :], gate[:, :, :], AX.X, ALU.add))
                steps.link(dve.reciprocal(total[:, :], total[:, :]))
                steps.link(dve.tensor_tensor(gate[:, :, :], gate[:, :, :], total[:, :].unsqueeze(2).broadcast_to([P, G, E]), ALU.mult))
                if relu:
                    for e in range(E):
                        for j in range(G):
                            if e == 0:
                                last = dve.tensor_scalar(acc[:, j, :], w["b2"][:, e, :],
                                                         gate[:, j, e:e + 1], None, ALU.mult)
                            else:
                                last = dve.scalar_tensor_tensor(out=acc[:, j, :], in0=w["b2"][:, e, :], scalar=gate[:, j, e:e + 1],
                                                                in1=acc[:, j, :], op0=ALU.mult, op1=ALU.add)
                        steps.link(last)
                for e in range(E):
                    if not relu and e + 1 < E:
                        multiply(e + 1)
                    for pair in range(2):
                        dve.wait_ge(summed, (i * E + e) * 2 + pair + 1)
                        for j in range(2):
                            b = 2 * pair + j
                            if e == 0 and not relu:
                                last = dve.tensor_scalar(acc[:, b, :], Y[:, pair, j, :], gate[:, b, e:e + 1], None, ALU.mult)
                            else:
                                last = dve.scalar_tensor_tensor(out=acc[:, b, :], in0=Y[:, pair, j, :], scalar=gate[:, b, e:e + 1],
                                                                in1=acc[:, b, :], op0=ALU.mult, op1=ALU.add)
                        last.then_inc(mixed, 1)
                dve.wait_ge(mixed, (i + 1) * E * 2)
                if relu:
                    steps.link(dve.tensor_tensor(acc[:, :, :], acc[:, :, :], xn[:, :, :], ALU.add))
                    norm2.statistics(dve, steps, lambda j: acc[:, j, :])
                    for j in range(G):
                        last = norm2.apply(dve, acc[:, j, :], acc[:, j, :], j)
                    steps.link(last)
                    steps.link(dve.tensor_tensor(acc[:, :, :], acc[:, :, :], w["gamma"].unsqueeze(1).broadcast_to([P, G, D]), ALU.mult))
                    dve.wait_ge(bias_added, (i + 1) * G)
                steps.link(dve.tensor_tensor(sh.x[:, bass.ts(i, G), :], sh.x[:, bass.ts(i, G), :], acc[:, :, :], ALU.add))
                steps.close()


def head_experts_phase(nc, sh, phase, next_phase):
    G = 4
    TURNS = BATCH // G
    T = G * P
    E, NH = 16, 8
    N = G * NH
    w, c = sh.params(phase), sh.const
    chunks = Chunks(["v", "a", "a", "a", "v", "a", "a", "a", "v", "v"])
    NA, NV, NC = chunks.total("a"), chunks.total("v"), len(chunks.by)
    with ExitStack() as ctx:
        core = Core(nc, ctx, phase)
        norm = Norm(core, G)
        xn = core.sb("xn", [P, G, D])
        xnT = core.sb("xnT", [P, KT, T])
        hT = core.sb("hT", [P, KT, T])
        acc = hT
        hi = core.sb("h_high", [P, KT, T], F16)
        lo = core.sb("h_low", [P, KT, T], F16)
        stack = core.sb("h_stacked", [P, KT, 4, T], F16)
        w1s = core.sb("w1_stacked", [P, E, P], F16)
        hid = core.sb("hidden", [P, 2, 2, T])
        gb = core.sb("gates_wide", [P, 2, KT, T])
        tmp = core.sb("gated", [P, 2, T])
        gT = core.sb("gatesT", [P, T])
        pr, rest, marks, chosen = (core.sb(n, [P, N, E]) for n in ("softmax", "rest", "marks", "chosen"))
        best, second = (core.sb(n, [P, N]) for n in ("best", "second"))
        Z = core.ps("Z", [P, 2, 2, T])
        O = core.ps("O", [P, 2, T])
        gen = core.ps("gen", [P, 2, T])
        (xn_ready, bias_added, filled, emptied_a, emptied_v, high, low, stacked, centered, exped, gated, stored, hid_pre,
         hid_ready, summed, weighted, mixed, dve_step, w1_ready) = (core.sem(s) for s in (
            "xn_ready", "bias_added", "gen_filled", "gen_emptied_act", "gen_emptied_dve", "h_high", "h_low", "h_stacked",
            "logits_centered", "logits_exped", "gates_ready", "gates_stored", "hidden_summed", "hidden_ready",
            "outputs_summed", "outputs_weighted", "outputs_mixed", "dve_step", "w1_stacked"))
        block = ctx.enter_context(nc.Block())
        emptied = {"a": (emptied_a, NA), "v": (emptied_v, NV)}
        wide = [core.sem(f"gates_wide{n}") for n in range(2)]
        WIDE = E // 2 * KT * 16
        M = E * KT
        H = 2 * M

        @block.sync
        def _(sp):
            if next_phase:
                sh.load_params(sp, next_phase)
            with sp.Fori(0, TURNS) as i:
                for part in range(4):
                    if part == 0:
                        sp.wait_ge(high, (i + 1) * 2)
                    if part == 2:
                        sp.wait_ge(low, i + 1)
                    for s in range(4):
                        sp.dma_start(stack[32 * part:32 * part + 32, :, s, :],
                                     (hi if part < 2 else lo)[32 * s:32 * s + 32, :, :]).then_inc(stacked, 16)
                sp.wait_ge(emptied_a, i * NA + 4)
                sp.dma_start(sh.dram["gates"][i], gT[:, :]).then_inc(stored, 16)
                sp.wait_ge(stored, (i + 1) * 16)
                for e in range(E):
                    if e >= 2:
                        sp.wait_ge(weighted, i * M + (e - 1) * KT)
                    for t in range(KT):
                        rows = sh.dram["gates"][i, t * 64 + e:t * 64 + e + 3 * E + 1:E, :]
                        sp.dma_start(gb[:, e % 2, t, :], rows.unsqueeze(1).broadcast_to([4, 32, T])).then_inc(wide[e % 2], 16)

        @block.gpsimd
        def _(pool):
            sh.wait_params(pool, phase)
            with pool.Fori(0, TURNS) as i:
                pool.wait_ge(xn_ready, (i + 1) * G)
                for j in range(G):
                    pool.tensor_tensor(sh.x[:, i * G + j, :], sh.x[:, i * G + j, :], w["bo"], ALU.add).then_inc(bias_added, 1)
                pool.wait_ge(emptied_a, i * NA + 6)
                for m in range(M):
                    pool.wait_ge(weighted, i * M + m + 1)
                    if m >= KT:
                        pool.wait_ge(mixed, i * M + m - 1)
                    pool.tensor_tensor(acc[:, m % KT, :], acc[:, m % KT, :], tmp[:, m % 2, :], ALU.add).then_inc(mixed, 1)

        @block.scalar
        def _(act):
            sh.wait_params(act, phase)
            with act.Fori(0, TURNS) as i:
                act.wait_ge(filled, i * NC + 2)
                act.activation(xnT[:, 1, :], gen[:, 1, :], ACT.Copy).then_inc(emptied_a, 1)
                for t in range(KT):
                    act.wait_ge(filled, i * NC + 3 + t)
                    act.activation(hi[:, t, :], gen[:, t, :], ACT.Identity, bias=w["bm"][:, t:t + 1]).then_inc(high, 1)
                    act.activation(hT[:, t, :], gen[:, t, :], ACT.Identity, bias=w["bm"][:, t:t + 1]).then_inc(emptied_a, 1)
                act.wait_ge(centered, i + 1)
                act.activation(pr[:, :, :], pr[:, :, :], ACT.Exp).then_inc(exped, 1)

                def hidden(n):
                    act.wait_ge(hid_pre, i * H + n + 1)
                    if n >= 2:
                        act.wait_ge(summed, i * H + n - 1)
                    act.activation(hid[:, n % 2, :, :], Z[:, n % 2, :, :], ACT.Gelu, bias=w["b1"][:, n // 4:n // 4 + 1]).then_inc(hid_ready, 1)

                hidden(0)
                hidden(1)
                act.wait_ge(filled, i * NC + 6)
                act.activation(gT[:, :], gen[:, 1, :], ACT.Copy).then_inc(emptied_a, 1)
                for t in range(KT):
                    act.wait_ge(filled, i * NC + 7 + t)
                    act.activation(acc[:, t, :], gen[:, t, :], ACT.Copy).then_inc(emptied_a, 1)
                for n in range(2, H):
                    hidden(n)

        @block.tensor
        def _(pe):
            def free_bank(i, cc):
                if cc >= 2:
                    s, per = emptied[chunks.by[cc - 2]]
                    pe.wait_ge(s, i * per + chunks.emptied(cc - 2))

            def first_product(i, n):
                e, t, half = n // 4, n // 2 % 2, n % 2
                if n >= 2:
                    pe.wait_ge(hid_ready, i * H + n - 1)
                for s in range(2):
                    mm = pe.matmul(Z[:, n % 2, s, :], w1s[:, e, :], stack[:, t, 2 * half + s, :], start=True, stop=True)
                mm.then_inc(hid_pre, 1)

            def second_product(i, n):
                e, t, half = n // 4, n // 2 % 2, n % 2
                m = 2 * e + t
                pe.wait_ge(hid_ready, i * H + n + 1)
                if half == 0 and m >= 2:
                    pe.wait_ge(weighted, i * M + m - 1)
                for s in range(2):
                    at = 32 * (2 * half + s)
                    mm = pe.matmul(O[at:at + 32, m % 2, :], w["w2"][:, e, :], hid[:, n % 2, s, :], start=True, stop=True)
                mm.then_inc(summed, 1)

            sh.wait_params(pe, phase)
            pe.wait_ge(w1_ready, 2)
            with pe.Fori(0, TURNS) as i:
                pe.wait_ge(xn_ready, (i + 1) * G)
                for k in range(KT):
                    for j in range(G):
                        mm = pe.transpose(gen[:, k, j * P:(j + 1) * P], xn[:, j, k * P:(k + 1) * P], c["ident"])
                    mm.then_inc(filled, 1)
                free_bank(i, 2)
                free_bank(i, 3)
                for t in range(KT):
                    for k in range(KT):
                        mm = pe.matmul(gen[:, t, :], w["wm"][:, k, t * P:(t + 1) * P], xnT[:, k, :], start=(k == 0), stop=(k == KT - 1))
                    mm.then_inc(filled, 1)
                free_bank(i, 4)
                free_bank(i, 5)
                for j in range(G):
                    for k in range(KT):
                        mm = pe.matmul(gen[:, 0, j * P:(j + 1) * P], hT[:, k, j * P:(j + 1) * P], w["emb"][:, k, :],
                                       start=(k == 0), stop=(k == KT - 1))
                mm.then_inc(filled, 1)
                pe.wait_ge(stacked, (i + 1) * 256)
                first_product(i, 0)
                first_product(i, 1)
                pe.wait_ge(gated, i + 1)
                for j in range(G):
                    mm = pe.transpose(gen[:, 1, j * P:(j + 1) * P], chosen[:, j * NH:(j + 1) * NH, :].rearrange("p h e -> p (h e)"), c["ident"])
                mm.then_inc(filled, 1)
                pe.wait_ge(emptied_v, i * NV + 2)
                pe.wait_ge(emptied_a, i * NA + 4)
                for t in range(KT):
                    mm = pe.matmul(gen[:, t, :], w["b2"][:, t, :], gT[:, :], start=True, stop=True)
                    mm.then_inc(filled, 1)
                for n in range(H):
                    if n >= 1 and n + 1 < H:
                        first_product(i, n + 1)
                    second_product(i, n)
                pe.wait_ge(mixed, (i + 1) * M)
                pe.wait_ge(emptied_a, (i + 1) * NA)
                for pair in range(2):
                    for j in range(2):
                        b = 2 * pair + j
                        for t in range(KT):
                            mm = pe.matmul(gen[:, pair, j * D:(j + 1) * D], acc[:, t, b * P:(b + 1) * P], w["wo"][:, t, :],
                                           start=(t == 0), stop=(t == KT - 1))
                    mm.then_inc(filled, 1)

        @block.vector
        def _(dve):
            per = Norm.STEPS + 4 + TOP_TWO_STEPS
            sh.wait_params(dve, phase)
            dve.tensor_copy(w1s[:, :, :], w["w1"]).then_inc(w1_ready, 1)
            dve.wait_ge(w1_ready, 1)
            for s in (1, 3):
                r = slice(32 * s, 32 * s + 32)
                last = dve.tensor_tensor(w1s[r, :, :], w["w1"][r, :, :], w1s[r, :, :], ALU.subtract)
            last.then_inc(w1_ready, 1)
            with dve.Fori(0, TURNS) as i:
                steps = Steps(dve, dve_step, i * per, per)
                norm.statistics(dve, steps, lambda j: sh.x[:, i * G + j, :])
                for j in range(G):
                    norm.apply(dve, xn[:, j, :], sh.x[:, i * G + j, :], j).then_inc(xn_ready, 1)
                dve.wait_ge(filled, i * NC + 1)
                dve.tensor_copy(xnT[:, 0, :], gen[:, 0, :]).then_inc(emptied_v, 1)
                dve.wait_ge(emptied_a, i * NA + 3)
                dve.tensor_tensor(lo[:, :, :], hT[:, :, :], hi[:, :, :], ALU.subtract).then_inc(low, 1)
                wide_ = lambda a: a.unsqueeze(2).broadcast_to([P, N, E])
                dve.wait_ge(filled, i * NC + 5)
                logits = gen[:, 0, :].rearrange("p (n e) -> p n e", e=E)
                steps.link(dve.tensor_reduce(best[:, :], logits, AX.X, ALU.max))
                dve.tensor_tensor(pr[:, :, :], logits, wide_(best[:, :]), ALU.subtract).then_inc(centered, 1)
                dve.sem_inc(emptied_v, 1)
                dve.wait_ge(exped, i + 1)
                steps.link(dve.tensor_reduce(best[:, :], pr[:, :, :], AX.X, ALU.add))
                steps.link(dve.reciprocal(best[:, :], best[:, :]))
                steps.link(dve.tensor_tensor(pr[:, :, :], pr[:, :, :], wide_(best[:, :]), ALU.mult))
                top_two(dve, steps, chosen[:, :, :], pr[:, :, :], rest[:, :, :], marks[:, :, :], best[:, :], second[:, :],
                        c["iota16"].unsqueeze(1).broadcast_to([P, N, E]), N, E)
                dve.tensor_tensor(chosen[:, :, :], chosen[:, :, :], pr[:, :, :], ALU.mult).then_inc(gated, 1)
                for m in range(M):
                    dve.wait_ge(summed, i * H + 2 * m + 2)
                    e = m // KT
                    dve.wait_ge(wide[e % 2], i * WIDE + (e // 2 + 1) * KT * 16)
                    if m >= 2:
                        dve.wait_ge(mixed, i * M + m - 1)
                    dve.tensor_tensor(tmp[:, m % 2, :], O[:, m % 2, :], gb[:, m // KT % 2, m % KT, :], ALU.mult).then_inc(weighted, 1)
                for pair in range(2):
                    dve.wait_ge(filled, i * NC + 9 + pair)
                    dve.wait_ge(bias_added, (i + 1) * G)
                    for j in range(2):
                        b = 2 * pair + j
                        last = dve.tensor_tensor(sh.x[:, i * G + b, :], gen[:, pair, j * D:(j + 1) * D], sh.x[:, i * G + b, :], ALU.add)
                    last.then_inc(emptied_v, 1)
                dve.wait_ge(emptied_v, (i + 1) * NV)
                steps.close()


def quantized_phase(nc, sh, phase, next_phase):
    G = 2
    TURNS = BATCH // G
    T = G * P
    F = 1024
    FT = F // P
    FLOOR = 1e-5
    w, c = sh.params(phase), sh.const
    with ExitStack() as ctx:
        core = Core(nc, ctx, phase)
        norm, again = Norm(core, G), Norm(core, G, "ln1")
        wq1 = core.sb("w1_ternary", [P, KT, F], BF16)
        wq2 = core.sb("w2_ternary", [P, FT, D], BF16)
        ident = core.sb("ident16", [P, P], BF16)
        ws = core.sb("weight_scales", [P, 2])
        wi = core.sb("weight_inverse", [P, 2])
        xn = core.sb("xn", [P, G, D])
        xq = core.sb("x_int", [P, G, D], BF16)
        xqT = core.sb("x_intT", [P, KT, T], BF16)
        amax, inv, back = (core.sb(n, [P, G]) for n in ("amax", "inverse", "back"))
        h = core.sb("hidden", [P, 2, F])
        hq = core.sb("hidden_int", [P, F], BF16)
        hqT = core.sb("hidden_intT", [P, FT, P], BF16)
        stats2 = core.sb("ln2_stats", [P, 2, 6])
        mv2 = core.sb("ln2_mean_var", [P, 2])
        half2 = core.sb("ln2_half", [P, 1], I32)
        root2, tmp2, amax2, inv2, back2 = (core.sb(n, [P, 1]) for n in ("ln2_root", "ln2_tmp", "amax2", "inverse2", "back2"))
        Hp = core.ps("H", [P, 2, F])
        XT = core.ps("XT", [P, KT, T], BF16)
        HT = core.ps("HT", [P, FT, P], BF16)
        Y = core.ps("Y", [P, BANK])
        WS = core.ps("WS", [P, BANK])
        (w_summed, w_total, w_ready, ident_ready, norm_ready, bias_added, quantized, x_turned, xT_ready, hid_pre, hid_linear,
         hid_act, hq_ready, h_turned, hT_ready, out_ready, out_added, dve_step) = (core.sem(s) for s in (
            "weights_summed", "weights_total", "weights_ready", "ident16_ready", "x_read", "bias_added", "x_quantized",
            "x_turned", "xT_ready", "hidden_summed", "hidden_scaled", "hidden_act", "hidden_quantized", "hidden_turned",
            "hiddenT_ready", "out_summed", "out_added", "dve_step"))
        block = ctx.enter_context(nc.Block())

        @block.sync
        def _(sp):
            if next_phase:
                sh.load_params(sp, next_phase)

        @block.gpsimd
        def _(pool):
            sh.wait_params(pool, phase)
            pool.tensor_copy(ident[:, :], c["ident"]).then_inc(ident_ready, 1)
            with pool.Fori(0, TURNS) as i:
                pool.wait_ge(norm_ready, i + 1)
                for j in range(G):
                    pool.tensor_tensor(sh.x[:, i * G + j, :], sh.x[:, i * G + j, :], w["b2"], ALU.add).then_inc(bias_added, 1)

        @block.scalar
        def _(act):
            with act.Fori(0, TURNS) as i:
                act.wait_ge(x_turned, i + 1)
                act.activation(xqT[:, :, :], XT[:, :, :], ACT.Copy).then_inc(xT_ready, 1)
                for j in range(G):
                    act.wait_ge(hid_linear, i * G + j + 1)
                    act.activation(h[:, j, :], h[:, j, :], ACT.Gelu).then_inc(hid_act, 1)
                for j in range(G):
                    act.wait_ge(h_turned, i * G + j + 1)
                    act.activation(hqT[:, :, :], HT[:, :, :], ACT.Copy).then_inc(hT_ready, 1)

        @block.tensor
        def _(pe):
            pe.wait_ge(w_summed, 2)
            pe.matmul(WS[:, 0:2], c["ones"], ws[:, :], start=True, stop=True).then_inc(w_total, 1)
            pe.wait_ge(w_ready, 2)
            pe.wait_ge(ident_ready, 1)
            with pe.Fori(0, TURNS) as i:
                pe.wait_ge(quantized, i + 1)
                for k in range(KT):
                    for j in range(G):
                        mm = pe.transpose(XT[:, k, j * P:(j + 1) * P], xq[:, j, k * P:(k + 1) * P], ident[:, :])
                mm.then_inc(x_turned, 1)
                pe.wait_ge(xT_ready, i + 1)
                for j in range(G):
                    for half in range(2):
                        for k in range(KT):
                            mm = pe.matmul(Hp[:, j, half * BANK:(half + 1) * BANK], xqT[:, k, j * P:(j + 1) * P],
                                           wq1[:, k, half * BANK:(half + 1) * BANK], start=(k == 0), stop=(k == KT - 1))
                    mm.then_inc(hid_pre, 1)
                for j in range(G):
                    pe.wait_ge(hq_ready, i * G + j + 1)
                    if j >= 1:
                        pe.wait_ge(hT_ready, i * G + j)
                    for t in range(FT):
                        mm = pe.transpose(HT[:, t, :], hq[:, t * P:(t + 1) * P], ident[:, :])
                    mm.then_inc(h_turned, 1)
                    pe.wait_ge(hT_ready, i * G + j + 1)
                    if j >= 1:
                        pe.wait_ge(out_added, i * G + j)
                    for t in range(FT):
                        mm = pe.matmul(Y[:, 0:D], hqT[:, t, :], wq2[:, t, :], start=(t == 0), stop=(t == FT - 1))
                    mm.then_inc(out_ready, 1)

        @block.vector
        def _(dve):
            def quantize(steps, values, ints, amax, inv, back, scale):
                steps.link(dve.tensor_scalar(amax, amax, FLOOR, None, ALU.max))
                steps.link(dve.reciprocal(inv, amax))
                dve.tensor_scalar(back, amax, 1.0 / 127.0, scale, ALU.mult, ALU.mult)
                steps.link(dve.tensor_scalar(inv, inv, 127.0, None, ALU.mult))
                return inv

            sh.wait_params(dve, phase)
            for n, part in enumerate(("w1", "w2")):
                dve.tensor_reduce(ws[:, n:n + 1], w[part].rearrange("p a b -> p (a b)"), AX.X, ALU.add,
                                  apply_absolute_value=True).then_inc(w_summed, 1)
            dve.wait_ge(w_total, 1)
            prep = Steps(dve, dve_step, 0, 6)
            prep.link(dve.tensor_scalar(ws[:, :], WS[:, 0:2], 1.0 / (D * F), FLOOR, ALU.mult, ALU.max))
            prep.link(dve.reciprocal(wi[:, :], ws[:, :]))
            for n, (part, out) in enumerate((("w1", wq1), ("w2", wq2))):
                prep.link(dve.tensor_scalar(w[part], w[part], wi[:, n:n + 1], ROUND, ALU.mult, ALU.add))
                prep.link(dve.tensor_scalar(w[part], w[part], -ROUND, 1.0, ALU.add, ALU.min))
                dve.tensor_scalar(out[:, :, :], w[part], -1.0, None, ALU.max).then_inc(w_ready, 1)
            prep.close()
            per = 2 * Norm.STEPS + 3 + 1 + 3 + 1 + G * (2 + RSQRT_STEPS + 3 + 1 + 3 + 1)
            with dve.Fori(0, TURNS) as i:
                steps = Steps(dve, dve_step, 6 + i * per, per)
                norm.statistics(dve, steps, lambda j: sh.x[:, i * G + j, :])
                for j in range(G):
                    last = norm.apply(dve, xn[:, j, :], sh.x[:, i * G + j, :], j)
                last.then_inc(norm_ready, 1)
                dve.wait_ge(norm_ready, i + 1)
                again.statistics(dve, steps, lambda j: xn[:, j, :])
                for j in range(G):
                    last = again.apply(dve, xn[:, j, :], xn[:, j, :], j)
                steps.link(last)
                wide = lambda a: a.unsqueeze(1).broadcast_to([P, G, D])
                steps.link(dve.tensor_tensor(xn[:, :, :], xn[:, :, :], wide(w["g1"]), ALU.mult))
                steps.link(dve.tensor_tensor(xn[:, :, :], xn[:, :, :], wide(w["c1"]), ALU.add))
                steps.link(dve.tensor_reduce(amax[:, :], xn[:, :, :], AX.X, ALU.max, apply_absolute_value=True))
                quantize(steps, xn, xq, amax[:, :], inv[:, :], back[:, :], ws[:, 0:1])
                for j in range(G):
                    last = dve.tensor_scalar(xn[:, j, :], xn[:, j, :], inv[:, j:j + 1], ROUND, ALU.mult, ALU.add)
                steps.link(last)
                dve.tensor_scalar(xq[:, :, :], xn[:, :, :], -ROUND, 127.0, ALU.add, ALU.min).then_inc(quantized, 1)
                for j in range(G):
                    dve.wait_ge(hid_pre, i * G + j + 1)
                    dve.scalar_tensor_tensor(out=h[:, j, :], in0=Hp[:, j, :], scalar=back[:, j:j + 1], in1=w["b1"],
                                             op0=ALU.mult, op1=ALU.add).then_inc(hid_linear, 1)
                for j in range(G):
                    hj = h[:, j, :]
                    dve.wait_ge(hid_act, i * G + j + 1)
                    dve.bn_stats(stats2[:, 0, :], hj[:, 0:BANK])
                    steps.link(dve.bn_stats(stats2[:, 1, :], hj[:, BANK:F]))
                    detach_wait(dve)
                    steps.link(dve.bn_aggr(mv2[:, :], stats2[:, :, :]))
                    rsqrt(dve, steps, mv2[:, 1:2], half2[:, :], root2[:, :], tmp2[:, :], LN_EPS)
                    steps.link(dve.tensor_scalar(hj, hj, mv2[:, 0:1], root2[:, :], ALU.subtract, ALU.mult))
                    steps.link(dve.tensor_tensor(hj, hj, w["g2"], ALU.mult))
                    steps.link(dve.tensor_tensor(hj, hj, w["c2"], ALU.add))
                    steps.link(dve.tensor_reduce(amax2[:, :], hj, AX.X, ALU.max, apply_absolute_value=True))
                    quantize(steps, hj, hq, amax2[:, :], inv2[:, :], back2[:, :], ws[:, 1:2])
                    steps.link(dve.tensor_scalar(hj, hj, inv2[:, :], ROUND, ALU.mult, ALU.add))
                    dve.tensor_scalar(hq[:, :], hj, -ROUND, 127.0, ALU.add, ALU.min).then_inc(hq_ready, 1)
                    dve.wait_ge(out_ready, i * G + j + 1)
                    dve.wait_ge(bias_added, i * G + j + 1)
                    dve.scalar_tensor_tensor(out=sh.x[:, i * G + j, :], in0=Y[:, 0:D], scalar=back2[:, :],
                                             in1=sh.x[:, i * G + j, :], op0=ALU.mult, op1=ALU.add).then_inc(out_added, 1)
                dve.wait_ge(out_added, (i + 1) * G)
                steps.close()


PHASES = ["L0x", "L0f", "L1x", "L1f", "L2x", "L2f", "L3x", "L3f"]


def build(nc, dram, phases=PHASES):
    with ExitStack() as ctx:
        sh = Shared(nc, ctx, dram)
        first_loads(nc, sh, phases)
        for n, phase in enumerate(phases):
            following = phases[n + 1] if n + 1 < len(phases) else None
            if phase in ("L0x", "L3x"):
                attention_phase(nc, sh, phase, 16, following)
            elif phase == "L2x":
                attention_phase(nc, sh, phase, 64, following)
            elif phase == "L0f":
                head_experts_phase(nc, sh, phase, following)
            elif phase == "L1x":
                performer_phase(nc, sh, phase, following)
            elif phase == "L2f":
                quantized_phase(nc, sh, phase, following)
            else:
                experts_phase(nc, sh, phase, following)
        last_stores(nc, sh)


def _rows(a, rows=P):
    return a.reshape(-1, rows, a.shape[-1]).transpose(1, 0, 2).reshape(rows, -1)


def _cols(a):
    return a.reshape(-1, P).T


def _wide(a):
    return np.broadcast_to(a.reshape(1, -1), (P, a.size))


def _constants():
    f = np.float32
    p, q = np.arange(P)[:, None], np.arange(P)[None, :]
    out = {
        "ident": (p == q), "pick8": 0.25 * (p // 16 == np.arange(8)), "pick2": 0.125 * (p // 64 == np.arange(2)),
        "feat2": 0.125 * (p // 64 == np.arange(2)), "causal": (p <= q),
        "half": -0.5 * np.concatenate([(p // 32 == s) & ((p % 32) // 16 == q // 64) for s in range(4)], 1),
        "headsum": -0.5 * (p // 16 == np.arange(8)),
        "iota8": np.broadcast_to(np.arange(8), (P, 8)), "iota16": np.broadcast_to(np.arange(16), (P, 16)),
        "ones": np.ones((P, P)),
    }
    return np.concatenate([out[n].astype(f) for n, _ in PARTS["const"]], 1)


def _pack(i):
    z = np.zeros
    f = np.float32

    def attn(k, transposed=False):
        g = lambda n: i[f"{k}_{n}"].T if transposed and n[0] == "W" else i[f"{k}_{n}"]
        return {"wq": _rows(g("Wq")), "wk": _rows(g("Wk")), "wv": _rows(g("Wv")), "wo": _rows(g("Wo")),
                "bq": _cols(g("bq")), "bk": _cols(g("bk")), "bv": _wide(g("bv")), "bo": _wide(g("bo"))}

    def padded(a, n):
        out = z((a.shape[0], n), f)
        out[:, :a.shape[1]] = a
        return out

    rf = z((P, 4, P), f)
    for s in range(4):
        for a in range(2):
            rf[32 * s + 16 * a:32 * s + 16 * a + 16, s, 64 * a:64 * a + 64] = i["L1_xattn_random_features"]
    emb = z((P, 2, 8, 16), f)
    b2 = z((8, 16, 2, 4, 32), f)
    for h in range(8):
        emb[32 * (h % 4):32 * (h % 4) + 32, h // 4, h, :] = i["L0_ffn_expert_emb"]
        b2[h, :, h // 4, h % 4, :] = i["L0_ffn_b2"]
    parts = {
        "L0x": attn("L0_xattn"),
        "L0f": {"wm": _rows(i["L0_ffn_Wm"]), "wo": _rows(i["L0_ffn_Wo"]), "emb": emb.reshape(P, -1),
                "w1": np.tile(i["L0_ffn_W1"].transpose(1, 0, 2).reshape(32, -1), (4, 1)),
                "w2": i["L0_ffn_W2"].transpose(1, 0, 2).reshape(P, -1), "b2": b2.reshape(P, -1),
                "b1": i["L0_ffn_b1"].T, "bm": _cols(i["L0_ffn_bm"]), "bo": _wide(i["L0_ffn_bo"])},
        "L1x": attn("L1_xattn") | {"rf": rf.reshape(P, -1)},
        "L1f": {"w1": i["L1_ffn_W1"].reshape(8, 2, P, 512).transpose(2, 0, 1, 3).reshape(P, -1),
                "w2": i["L1_ffn_W2"].reshape(8, 4, P, D).transpose(2, 0, 1, 3).reshape(P, -1),
                "wg": _rows(padded(i["L1_ffn_Wg"], P)), "bg": _wide(i["L1_ffn_bg"]),
                "b1": i["L1_ffn_b1"].reshape(8, 4, P).transpose(2, 0, 1).reshape(P, -1), "b2": _wide(i["L1_ffn_b2"]),
                "gamma": _wide(i["L1_ffn_gamma"]), "beta": _wide(i["L1_ffn_beta"])},
        "L2x": {"wq": _rows(i["L2_xattn_Wq"]), "wk": _rows(i["L2_xattn_Wk"]), "wv": _rows(i["L2_xattn_Wv"]),
                "wo": _rows(i["L2_xattn_Wo"])},
        "L2f": {"w1": _rows(i["L2_ffn_w1"].T), "w2": _rows(i["L2_ffn_w2"].T), "g1": _wide(i["L2_ffn_ln1_g"]),
                "c1": _wide(i["L2_ffn_ln1_b"]), "b1": _wide(i["L2_ffn_b1"]), "g2": _wide(i["L2_ffn_ln2_g"]),
                "c2": _wide(i["L2_ffn_ln2_b"]), "b2": _wide(i["L2_ffn_b2"])},
        "L3x": attn("L3_xattn", True) | {"mask": i["fside_SxS2_0"]},
        "L3f": {"w1": i["L3_ffn_w1"].transpose(0, 2, 1).reshape(8, 2, P, 512).transpose(2, 0, 1, 3).reshape(P, -1),
                "w2": i["L3_ffn_w2"].transpose(0, 2, 1).reshape(8, 2, P, D).transpose(2, 0, 1, 3).reshape(P, -1),
                "wg": _rows(padded(i["L3_ffn_Wg"].T, P)), "bg": _wide(i["L3_ffn_bg"])},
    }
    return {f"p_{ph}": np.ascontiguousarray(np.concatenate([parts[ph][n] for n, _ in PARTS[ph]], 1)) for ph in parts}


def _arrays(i):
    i = {k: np.asarray(v) for k, v in i.items()}
    arrays = {"x": i["x"], "side": i["fside_Bx16xSxS2_0"], "pad": i["mask_BxS2_bf0"].view(np.int32),
              "ctxT": np.ascontiguousarray(i["ctx_1024"].reshape(BATCH * P, KT, P).transpose(2, 1, 0)),
              "p_const": _constants()}
    arrays.update(_pack(i))
    return arrays


def _declare(nc, arrays):
    types = {"float32": F32, "int32": I32}
    dram = {n: nc.dram_tensor(f"{n}_dram", list(a.shape), types[str(a.dtype)], kind="ExternalInput").ap()
            for n, a in arrays.items()}
    dram["out"] = nc.dram_tensor("out_dram", [BATCH, P, D], F32, kind="ExternalOutput").ap()
    dram["gates"] = nc.dram_tensor("gates_dram", [8, P, 512], F32, kind="Internal").ap()
    return dram


def kernel(**inputs):
    from concourse import bacc
    from concourse.bass_utils import run_bass_kernel_spmd

    nc = bacc.Bacc("TRN2", target_bir_lowering=False, num_devices=1)
    arrays = _arrays(inputs)
    build(nc, _declare(nc, arrays))
    r = run_bass_kernel_spmd(nc, [{f"{n}_dram": a for n, a in arrays.items()}], core_ids=[0])
    return r.results[0]["out_dram"]
```

```python
from contextlib import ExitStack

import numpy as np

import concourse.bass as bass
from concourse import mybir

ALU = mybir.AluOpType
ACT = mybir.ActivationFunctionType
AX = mybir.AxisListType
F32 = mybir.dt.float32
F16 = mybir.dt.float16
BF16 = mybir.dt.bfloat16
I32 = mybir.dt.int32
U8 = mybir.dt.uint8

P = 128
BATCH = 32
D = 256
KT = D // P
HEADS = 16
BANK = 512
SPARE = 6
LN_EPS = 1e-5
RSQRT_SEED = float(0x5F3759DF)
ROUND = 1.5 * 2.0 ** 23
NEVER = 1e30


def detach_wait(eng):
    eng.nop(nofuse=True)


class Steps:

    def __init__(self, eng, sem, start, per_turn=None):
        self.eng, self.sem, self.start, self.n, self.per_turn = eng, sem, start, 0, per_turn

    def link(self, instruction):
        self.n += 1
        instruction.then_inc(self.sem, 1)
        self.eng.wait_ge(self.sem, self.start + self.n)

    def close(self):
        assert self.n == self.per_turn, f"{self.n} linked steps, {self.per_turn} declared"


def rsqrt(dve, steps, var, half, root, tmp, eps):
    rsqrt_seed(dve, steps, var, half, root, eps)
    rsqrt_rounds(dve, steps, var, root, tmp, 3)


def rsqrt_seed(dve, steps, var, half, root, eps):
    steps.link(dve.tensor_scalar(var, var, eps, None, ALU.add))
    steps.link(dve.tensor_scalar(half, var.bitcast(I32), 1, None, ALU.logical_shift_right))
    steps.link(dve.tensor_scalar(root.bitcast(I32), half, -1.0, RSQRT_SEED, ALU.mult, ALU.add))


def rsqrt_rounds(dve, steps, var, root, tmp, rounds):
    for _ in range(rounds):
        steps.link(dve.scalar_tensor_tensor(out=tmp, in0=root, scalar=-0.5, in1=root, op0=ALU.mult, op1=ALU.mult))
        steps.link(dve.tensor_tensor(tmp, tmp, var, ALU.mult))
        steps.link(dve.scalar_tensor_tensor(out=root, in0=tmp, scalar=1.5, in1=root, op0=ALU.add, op1=ALU.mult))


RSQRT_STEPS = 12


class Norm:

    STEPS = 2 + RSQRT_STEPS

    def __init__(self, core, group, name="ln"):
        self.group = group
        self.stats = core.sb(name + "_stats", [P, group, 6])
        self.mean_var = core.sb(name + "_mean_var", [P, group, 2])
        self.half = core.sb(name + "_half", [P, group], I32)
        self.root = core.sb(name + "_root", [P, group])
        self.tmp = core.sb(name + "_tmp", [P, group])

    def statistics(self, dve, steps, source):
        self.moments(dve, steps, source)
        rsqrt(dve, steps, self.mean_var[:, :, 1], self.half[:, :], self.root[:, :], self.tmp[:, :], LN_EPS)

    def part(self, dve, steps, source, n):
        if n == 0:
            self.moments(dve, steps, source)
        elif n == 1:
            rsqrt_seed(dve, steps, self.mean_var[:, :, 1], self.half[:, :], self.root[:, :], LN_EPS)
            rsqrt_rounds(dve, steps, self.mean_var[:, :, 1], self.root[:, :], self.tmp[:, :], 1)
        else:
            rsqrt_rounds(dve, steps, self.mean_var[:, :, 1], self.root[:, :], self.tmp[:, :], 2)

    PART_STARTS = (0, 2, 8)

    def moments(self, dve, steps, source):
        for j in range(self.group - 1):
            dve.bn_stats(self.stats[:, j, :], source(j))
        steps.link(dve.bn_stats(self.stats[:, self.group - 1, :], source(self.group - 1)))
        detach_wait(dve)
        for j in range(self.group - 1):
            dve.bn_aggr(self.mean_var[:, j, :], self.stats[:, j, :])
        steps.link(dve.bn_aggr(self.mean_var[:, self.group - 1, :], self.stats[:, self.group - 1, :]))

    def apply(self, dve, out, source, j):
        return dve.tensor_scalar(out, source, self.mean_var[:, j, 0:1], self.root[:, j:j + 1],
                                 ALU.subtract, ALU.mult)


class Core:

    def __init__(self, nc, ctx, phase):
        self.nc, self.ctx, self.phase, self.sems = nc, ctx, phase, []
        ctx.callback(self.free_semaphores)

    def free_semaphores(self):
        self.nc.clear_and_free_semaphores(self.sems)
        self.nc.all_engine_barrier()

    def sb(self, name, shape, dt=F32):
        return self.ctx.enter_context(self.nc.sbuf_tensor(f"{self.phase}_{name}", shape, dt))

    def ps(self, name, shape, dt=F32):
        return self.ctx.enter_context(self.nc.psum_tensor(f"{self.phase}_{name}", shape, dt))

    def sem(self, name):
        self.sems.append(self.nc.alloc_semaphore(f"{self.phase}_{name}"))
        return self.sems[-1]


ATTN16 = [("wq", (KT, D)), ("wk", (KT, D)), ("wv", (KT, D)), ("wo", (KT, D)),
          ("bq", (2,)), ("bk", (2,)), ("bv", (D,)), ("bo", (D,))]
W64 = HEADS * 64
PARTS = {
    "L0x": ATTN16,
    "L0f": [("wm", (KT, D)), ("wo", (KT, D)), ("emb", (KT, P)), ("w1", (16, P)), ("w2", (16, 32)), ("b2", (KT, P)),
            ("b1", (16,)), ("bm", (KT,)), ("bo", (D,))],
    "L1x": ATTN16 + [("rf", (4, P))],
    "L1f": [("w1", (8, KT, 512)), ("w2", (8, 4, D)), ("wg", (KT, P)), ("bg", (8,)), ("b1", (8, 4)), ("b2", (8, D)),
            ("gamma", (D,)), ("beta", (D,))],
    "L2x": [("wq", (KT, W64)), ("wk", (KT, W64)), ("wv", (KT, W64)), ("wo", (8, D))],
    "L2f": [("w1", (KT, 1024)), ("w2", (8, D)), ("g1", (D,)), ("c1", (D,)), ("b1", (1024,)), ("g2", (1024,)),
            ("c2", (1024,)), ("b2", (D,))],
    "L3x": ATTN16 + [("mask", (P,))],
    "L3f": [("w1", (8, KT, 512)), ("w2", (8, 2, D)), ("wg", (KT, P)), ("bg", (8,))],
    "const": [("ident", (P,)), ("pick8", (8,)), ("pick2", (2,)), ("feat2", (2,)), ("causal", (P,)), ("half", (4, P)),
              ("headsum", (8,)), ("iota8", (8,)), ("iota16", (16,)), ("ones", (P,))],
}
SIDE = {"L0x": 1, "L1x": 1, "L2x": 1, "L3x": 1, "L0f": 0, "L1f": 0, "L2f": 0, "L3f": 0}


def columns(phase):
    return sum(int(np.prod(shape)) for _, shape in PARTS[phase])


def views(store, phase):
    out, at = {}, 0
    for name, shape in PARTS[phase]:
        n = int(np.prod(shape))
        v = store[:, at:at + n]
        if len(shape) == 2:
            v = v.rearrange("p (a b) -> p a b", a=shape[0])
        if len(shape) == 3:
            v = v.rearrange("p (a b c) -> p a b c", a=shape[0], b=shape[1])
        out[name] = v
        at += n
    return out


class Shared:

    def __init__(self, nc, ctx, dram):
        self.nc, self.dram = nc, dram
        self.x = ctx.enter_context(nc.sbuf_tensor("x_sb", [P, BATCH + SPARE, D], F32))
        self.const_store = ctx.enter_context(nc.sbuf_tensor("const_sb", [P, columns("const")], F32))
        self.stores = [ctx.enter_context(nc.sbuf_tensor(f"params{s}", [P, max(columns(p) for p in SIDE if SIDE[p] == s)], F32))
                       for s in range(2)]
        self.kstab = ctx.enter_context(nc.sbuf_tensor("neg_kstab", [P, 1], F32))
        self.const = views(self.const_store, "const")
        self.loaded = {p: nc.alloc_semaphore(f"params_{p}") for p in SIDE}
        self.loads = {}
        self.x_loaded = nc.alloc_semaphore("x_loaded")
        self.const_loaded = nc.alloc_semaphore("const_loaded")

    def params(self, phase):
        return views(self.stores[SIDE[phase]], phase)

    def scratch(self, following, columns_before, shape):
        at = columns(following) + columns_before
        n = int(np.prod(shape))
        v = self.stores[0][:, at:at + n]
        if len(shape) == 2:
            return v.rearrange("p (a b) -> p a b", a=shape[0])
        return v.rearrange("p (a b c) -> p a b c", a=shape[0], b=shape[1])

    def load_params(self, sp, phase):
        n, step, self.loads[phase] = columns(phase), 4096, 0
        for at in range(0, n, step):
            to = min(at + step, n)
            sp.dma_start(self.stores[SIDE[phase]][:, at:to], self.dram["p_" + phase][:, at:to]).then_inc(self.loaded[phase], 16)
            self.loads[phase] += 16

    def wait_params(self, eng, phase):
        eng.wait_ge(self.loaded[phase], self.loads[phase])


def first_loads(nc, sh, phases):
    spare_set = nc.alloc_semaphore("spare_set")
    with nc.Block() as block:
        @block.gpsimd
        def _(pool):
            pool.memset(sh.x[:, BATCH:, :], 0.0).then_inc(spare_set, 1)
            pool.wait_ge(spare_set, 1)

        @block.sync
        def _(sp):
            sp.dma_start(sh.const_store[:, :], sh.dram["p_const"]).then_inc(sh.const_loaded, 16)
            sh.load_params(sp, phases[0])
            for q in range(4):
                b = BATCH // 4
                sp.dma_start(sh.x[:, q * b:(q + 1) * b, :],
                             sh.dram["x"][q * b:(q + 1) * b].rearrange("b s d -> s b d")).then_inc(sh.x_loaded, 16)
            sp.wait_ge(sh.const_loaded, 16)
            sp.wait_ge(sh.x_loaded, 64)


def last_stores(nc, sh):
    stored = nc.alloc_semaphore("out_stored")
    with nc.Block() as block:
        @block.sync
        def _(sp):
            for q in range(4):
                b = BATCH // 4
                sp.dma_start(sh.dram["out"][q * b:(q + 1) * b].rearrange("b s d -> s b d"),
                             sh.x[:, q * b:(q + 1) * b, :]).then_inc(stored, 16)
            sp.wait_ge(stored, 64)


class Turn:

    def __init__(self, i, k):
        self.i, self.k = i, k
        self.n, self.slot, self.round = i * 2 + k, k % 2, i + k // 2

    def plus(self, k):
        return Turn(self.i, self.k + k)


class Bank:

    def __init__(self, core, number, before, turn):
        self.before, self.turn = before, turn
        self.filled, self.emptied = core.sem(f"bank{number}_filled"), core.sem(f"bank{number}_emptied")

    def uses_before(self, name, b):
        if isinstance(b.n, int) and (name, b.n) in self.before:
            return self.before.index((name, b.n))
        place = [n for n, _ in self.turn].index(name)
        return (b.n - self.turn[place][1]) * len(self.turn) + (len(self.before) + place)


class Banks:

    def __init__(self, core, psum, tables):
        self.psum = psum
        self.banks = [Bank(core, k, before, turn) for k, (before, turn) in enumerate(tables)]

    def find(self, name):
        return next(k for k, bank in enumerate(self.banks) if name in [n for n, _ in bank.turn])

    def open(self, eng):
        for bank in self.banks:
            eng.sem_inc(bank.emptied, 1)

    def at(self, name):
        return self.psum[:, self.find(name), :]

    def filled(self, name):
        return self.banks[self.find(name)].filled

    def emptied(self, name):
        return self.banks[self.find(name)].emptied

    def until_free(self, name, b):
        return self.banks[self.find(name)].uses_before(name, b) + 1

    def until_filled(self, name, b):
        return self.banks[self.find(name)].uses_before(name, b) + 1

    def until_emptied(self, name, b):
        return self.banks[self.find(name)].uses_before(name, b) + 2


FOLLOWING = {"L2x": "L2f", "L3x": "L3f"}


def attention_phase(nc, sh, phase, dh, next_phase):
    W = HEADS * dh
    NT = W // P
    VAR = P // dh
    HW = dh + 1
    VW = HEADS * HW + P - HW
    UH = 4
    U = HEADS // UH
    small = dh == 16
    HO = HEADS if small else UH
    biased = small
    masked = phase == "L3x"
    w, c = sh.params(phase), sh.const
    pick = c["pick8"] if small else c["pick2"]
    if small:
        BT = 2
        tables = [([("xT", 0), ("v0", 0), ("xT", 1)], [("v0", 1), ("xT", 2)]),
                  ([("q0", 0), ("k0", 0)], [("q0", 1), ("k0", 1), ("outT0", 0), ("proj", 0)])]
    else:
        BT = 4
        tables = [([("xT", 0), ("q0", 0), ("q1", 0), ("v1", 0), ("xT", 1)], [("q0", 1), ("q1", 1), ("outT0", 0), ("xT", 2), ("v1", 1)]),
                  ([("k0", 0), ("k1", 0), ("v0", 0)], [("k0", 1), ("k1", 1), ("v0", 1), ("outT1", 0), ("proj", 0)])]
    NB = NT // BT

    with ExitStack() as ctx:
        core = Core(nc, ctx, phase)
        norm = Norm(core, 2)
        xn = core.sb("xn", [P, 2, D])
        xnT = core.sb("xnT", [P, KT, P])
        cT = core.sb("ctxT", [P, 2, KT, P])
        qT = core.sb("qT", [P, NT, P])
        kT = core.sb("kT", [P, 2, NT, P])
        if small:
            qm = core.sb("q_masked", [P, 2, VAR, NT, P])
            qms = [qm[:, s, :, :, :] for s in range(2)]
        else:
            qms = [sh.scratch(FOLLOWING[phase], s * VAR * NT * P, (VAR, NT, P)) for s in range(2)]
        v = core.sb("v_ones", [P, 2, VW])
        d = core.sb("centered", [P, 2, UH, P])
        p = core.sb("probs", [P, 2, UH, P])
        pT = core.sb("probsT", [P, 2, UH, P])
        mx = core.sb("row_max", [P, 2, UH])
        rc = core.sb("recip_den", [P, 2, HO])
        o = core.sb("heads_out", [P, W])
        oT = core.sb("heads_outT", [P, NT, P])
        if masked:
            sides = [sh.scratch(FOLLOWING[phase], s * HEADS * P, (HEADS, P)) for s in range(2)]
            pad_words = core.sb("pad", [P, BATCH + 1, P // 4], I32)
            pad = pad_words[:, :, :].bitcast(U8)
            half_causal = core.sb("half_causal", [P, P])
            half_mask = core.sb("half_mask", [P, P])
            sm = core.sb("side_mask", [P, 2, UH, P])
        S = core.ps("S", [P, 2, UH, P])
        PT = core.ps("PT", [P, 2, UH, P])
        O = core.ps("O", [P, 2, BANK])
        gen = core.ps("gen", [P, 2, BANK])
        banks = Banks(core, gen, tables)

        ctx_loaded = [core.sem(f"ctx{s}_loaded") for s in range(2)]
        side_loaded = [core.sem(f"side{s}_loaded") for s in range(2)]
        (xn_ready, bias_added, qm_ready, v_set, scored, centered, exped, turned, turned_out, summed, normed, norm_step,
         max_step, recip_step, sum_step, side_used, side_ready, pad_set, pad_loaded, mask_step) = (core.sem(s) for s in (
            "xn_ready", "bias_added", "q_masked_ready", "v_ones_set", "scored", "centered", "exped", "probs_turned",
            "probsT_ready", "heads_summed", "heads_normed", "norm_step", "max_step", "recip_step", "masked_sum", "side_mask_used",
            "side_mask_ready", "pad_set", "pad_loaded", "mask_step"))
        block = ctx.enter_context(nc.Block())

        def unit(b, u):
            return b.n * U + u

        @block.sync
        def _(sp):
            def load_ctx(b, source):
                sp.dma_start(cT[:, b.slot, :, :], sh.dram["ctxT"][:, :, bass.ts(source, P)]).then_inc(ctx_loaded[b.slot], 16)

            def load_side(b, source):
                sp.dma_start(sides[b.slot], sh.dram["side"][:, bass.ts(source, HEADS), :]).then_inc(side_loaded[b.slot], 16)

            for k in range(2):
                load_ctx(Turn(0, k), k)
                if masked:
                    load_side(Turn(0, k), k)
            if next_phase:
                sh.load_params(sp, next_phase)

            def following(b, source):
                last = f"v{NB - 1}"
                sp.wait_ge(banks.emptied(last), banks.until_emptied(last, b))
                load_ctx(b.plus(2), source)
                if masked:
                    sp.wait_ge(side_ready, unit(b, U))
                    load_side(b.plus(2), source)

            following(Turn(0, 0), 2)
            with sp.Fori(0, BATCH // 2 - 2) as i:
                for s in range(1, 3):
                    b = Turn(i, s)
                    following(b, b.n + 2)
            following(Turn(0, BATCH - 3), BATCH - 1)
            following(Turn(0, BATCH - 2), 0)

        @block.gpsimd
        def _(pool):
            def bias(b):
                pool.wait_ge(xn_ready, b.n + 1)
                pool.tensor_tensor(sh.x[:, b.n, :], sh.x[:, b.n, :], w["bo"], ALU.add).then_inc(bias_added, 1)

            def mask_queries(b, k):
                pool.wait_ge(banks.emptied(f"q{k}"), banks.until_emptied(f"q{k}", b))
                detach_wait(pool)
                for m in range(VAR):
                    pool.tensor_scalar(qms[b.slot][:, m, k * BT:(k + 1) * BT, :], qT[:, k * BT:(k + 1) * BT, :], pick[:, m:m + 1], 1.0,
                                       ALU.mult, ALU.mult).then_inc(qm_ready, 1)

            def halve_mask(b):
                pool.tensor_copy(half_mask[:, :], pad[:, b.n, :]).then_inc(mask_step, 1)
                pool.wait_ge(mask_step, b.n * 3 + 2)
                detach_wait(pool)
                pool.tensor_scalar(half_mask[:, :], half_mask[:, :], -NEVER, 1.0, ALU.mult, ALU.mult).then_inc(mask_step, 1)
                pool.wait_ge(mask_step, b.n * 3 + 3)
                pool.tensor_tensor(half_mask[:, :], half_mask[:, :], half_causal[:, :], ALU.add).then_inc(mask_step, 1)
                pool.wait_ge(mask_step, b.n * 3 + 4)

            def mask_side(b, u, first=False):
                if u == 0:
                    pool.wait_ge(side_loaded[b.slot], (b.round + 1) * 16)
                if not first:
                    pool.wait_ge(side_used, unit(b, u) - 1)
                pool.tensor_tensor(sm[:, u % 2, :, :], sides[b.slot][:, u * UH:(u + 1) * UH, :],
                                   half_mask[:, :].unsqueeze(1).broadcast_to([P, UH, P]), ALU.add).then_inc(side_ready, 1)

            pool.memset(v[:, :, :], 1.0).then_inc(v_set, 1)
            sh.wait_params(pool, phase)
            if masked:
                pool.memset(pad_words[:, BATCH:, :], 0).then_inc(pad_set, 1)
                pool.wait_ge(pad_set, 1)
                pool.dma_start(pad_words[:, 0:BATCH, :], sh.dram["pad"].partition_broadcast(P)).then_inc(pad_loaded, 16)
                pool.tensor_scalar(half_causal[:, :], w["mask"], 0.5, 1.0, ALU.mult, ALU.mult).then_inc(mask_step, 1)
                pool.wait_ge(mask_step, 1)
                pool.wait_ge(pad_loaded, 16)
            start = Turn(0, 0)
            if biased:
                bias(start)
            for k in range(NB):
                mask_queries(start, k)
            if masked:
                halve_mask(start)
                mask_side(start, 0, first=True)
                mask_side(start, 1, first=True)
            with pool.Fori(0, BATCH // 2) as i:
                for s in range(2):
                    b = Turn(i, s)
                    if masked:
                        mask_side(b, 2)
                        mask_side(b, 3)
                    for k in range(NB):
                        mask_queries(b.plus(1), k)
                    if masked:
                        pool.wait_ge(side_ready, unit(b, U))
                        halve_mask(b.plus(1))
                        mask_side(b.plus(1), 0)
                        mask_side(b.plus(1), 1)
                    if biased:
                        bias(b.plus(1))

        @block.scalar
        def _(act):
            def empty_projection(b, name, k):
                dst = qT[:, k * BT:(k + 1) * BT, :] if name == "q" else kT[:, b.slot, k * BT:(k + 1) * BT, :]
                chunk = f"{name}{k}"
                act.wait_ge(banks.filled(chunk), banks.until_filled(chunk, b))
                src = banks.at(chunk)[:, 0:BT * P].rearrange("p (a b) -> p a b", a=BT)
                if biased:
                    for t in range(BT):
                        last = act.activation(dst[:, t, :], src[:, t, :], ACT.Identity, bias=w["b" + name][:, t:t + 1])
                else:
                    last = act.activation(dst, src, ACT.Copy)
                last.then_inc(banks.emptied(chunk), 1)

            def exponentiate(b, u):
                n = unit(b, u)
                act.wait_ge(centered, n + 1)
                act.activation(p[:, u % 2, :, :], d[:, u % 2, :, :], ACT.Exp).then_inc(exped, 1)

            def empty_probs(b, u):
                n = unit(b, u)
                act.wait_ge(turned, n + 1)
                act.activation(pT[:, u % 2, :, :], PT[:, u % 2, :, :], ACT.Copy).then_inc(turned_out, 1)

            def empty_outputs(b, k):
                chunk = f"outT{k}"
                act.wait_ge(banks.filled(chunk), banks.until_filled(chunk, b))
                act.activation(oT[:, k * BT:(k + 1) * BT, :], banks.at(chunk)[:, 0:BT * P].rearrange("p (a b) -> p a b", a=BT),
                               ACT.Copy).then_inc(banks.emptied(chunk), 1)

            sh.wait_params(act, phase)
            start = Turn(0, 0)
            for k in range(NB):
                empty_projection(start, "q", k)
                empty_projection(start, "k", k)
            exponentiate(start, 0)
            exponentiate(start, 1)
            empty_probs(start, 0)
            with act.Fori(0, BATCH // 2) as i:
                for s in range(2):
                    b = Turn(i, s)
                    for u in range(U):
                        empty_probs(b.plus((u + 1) // U), (u + 1) % U)
                        if u < NB:
                            empty_projection(b.plus(1), "q", u)
                        exponentiate(b.plus((u + 2) // U), (u + 2) % U)
                        if u == 1 if small else u < NB:
                            empty_projection(b.plus(1), "k", 0 if small else u)
                        if u >= U - NB:
                            empty_outputs(b, u - U + NB)

        @block.tensor
        def _(pe):
            def turn_rows(b):
                pe.wait_ge(xn_ready, b.n + 1)
                pe.wait_ge(banks.emptied("xT"), banks.until_free("xT", b))
                for k in range(KT):
                    mm = pe.transpose(banks.at("xT")[:, k * P:(k + 1) * P], xn[:, b.slot, k * P:(k + 1) * P], c["ident"])
                mm.then_inc(banks.filled("xT"), 1)

            def project(b, name, n):
                chunk = f"{name}{n}"
                pe.wait_ge(banks.emptied(chunk), banks.until_free(chunk, b))
                if name == "q":
                    pe.wait_ge(banks.emptied("xT"), banks.until_emptied("xT", b))
                elif name == "k":
                    pe.wait_ge(ctx_loaded[b.slot], (b.round + 1) * 16)
                if name == "v":
                    for k in range(KT):
                        mm = pe.matmul(banks.at(chunk)[:, 0:BT * P], cT[:, b.slot, k, :], w["wv"][:, k, n * BT * P:(n + 1) * BT * P],
                                       start=(k == 0), stop=(k == KT - 1))
                else:
                    for t in range(BT):
                        for k in range(KT):
                            mm = pe.matmul(banks.at(chunk)[:, t * P:(t + 1) * P], w["w" + name][:, k, (n * BT + t) * P:(n * BT + t + 1) * P],
                                           xnT[:, k, :] if name == "q" else cT[:, b.slot, k, :], start=(k == 0), stop=(k == KT - 1))
                mm.then_inc(banks.filled(chunk), 1)

            def score(b, u, first=False):
                n = unit(b, u)
                tiles = range(u * UH // VAR, (u * UH + UH - 1) // VAR + 1)
                chunk = tiles[-1] // BT
                pe.wait_ge(qm_ready, b.n * VAR * NB + (chunk + 1) * VAR)
                pe.wait_ge(banks.emptied(f"k{chunk}"), banks.until_emptied(f"k{chunk}", b))
                if not first:
                    pe.wait_ge(centered, n - 1)
                for r in range(UH):
                    h = u * UH + r
                    mm = pe.matmul(S[:, u % 2, r, :], qms[b.slot][:, h % VAR, h // VAR, :], kT[:, b.slot, h // VAR, :],
                                   start=True, stop=True)
                mm.then_inc(scored, 1)

            def turn_probs(b, u):
                pe.wait_ge(exped, unit(b, u) + 1)
                for r in range(UH):
                    mm = pe.transpose(PT[:, u % 2, r, :], p[:, u % 2, r, :], c["ident"])
                mm.then_inc(turned, 1)

            def sum_heads(b, u):
                n = unit(b, u)
                if u == 0:
                    for k in range(NB):
                        pe.wait_ge(banks.emptied(f"v{k}"), banks.until_emptied(f"v{k}", b))
                pe.wait_ge(turned_out, n + 1)
                if not small:
                    pe.wait_ge(normed, n + 1)
                bank, first = (b.slot, 0) if small else (u % 2, u * UH)
                for r in range(UH):
                    h = u * UH + r
                    mm = pe.matmul(O[:, bank, (h - first) * HW:(h - first) * HW + P], pT[:, u % 2, r, :],
                                   v[:, b.slot, h * HW:h * HW + P], start=True, stop=True, skip_group_check=True)
                if not small or u == U - 1:
                    mm.then_inc(summed, 1)

            def turn_outputs(b, k):
                chunk = f"outT{k}"
                pe.wait_ge(normed, b.n + 1 if small else b.n * U + (k + 1) * U // NB + 2)
                pe.wait_ge(banks.emptied(chunk), banks.until_free(chunk, b))
                for t in range(BT):
                    at = (k * BT + t) * P
                    mm = pe.transpose(banks.at(chunk)[:, t * P:(t + 1) * P], o[:, at:at + P], c["ident"])
                mm.then_inc(banks.filled(chunk), 1)

            def project_out(b):
                pe.wait_ge(banks.emptied("proj"), banks.until_free("proj", b))
                for k in range(NB):
                    pe.wait_ge(banks.emptied(f"outT{k}"), banks.until_emptied(f"outT{k}", b))
                for t in range(NT):
                    mm = pe.matmul(banks.at("proj")[:, 0:D], oT[:, t, :], w["wo"][:, t, :], start=(t == 0), stop=(t == NT - 1))
                mm.then_inc(banks.filled("proj"), 1)

            sh.wait_params(pe, phase)
            start = Turn(0, 0)
            turn_rows(start)
            for k in range(NB):
                project(start, "q", k)
                project(start, "k", k)
            for k in range(NB):
                project(start, "v", k)
            turn_rows(start.plus(1))
            score(start, 0, first=True)
            score(start, 1, first=True)
            turn_probs(start, 0)
            with pe.Fori(0, BATCH // 2) as i:
                for s in range(2):
                    b = Turn(i, s)
                    for u in range(U):
                        score(b.plus((u + 2) // U), (u + 2) % U)
                        if u < NB:
                            project(b.plus(1), "q", u)
                        turn_probs(b.plus((u + 1) // U), (u + 1) % U)
                        if u == 1 if small else u < NB:
                            project(b.plus(1), "k", 0 if small else u)
                        sum_heads(b, u)
                        if small and u == 2:
                            project(b.plus(1), "v", 0)
                        if u == U - 1:
                            turn_rows(b.plus(2))
                        if not small and u == U - 2:
                            project(b.plus(1), "v", 0)
                            turn_outputs(b, 0)
                    turn_outputs(b, NB - 1)
                    if not small:
                        project(b.plus(1), "v", NB - 1)
                    project_out(b)

        @block.vector
        def _(dve):
            def norm_part(b, n):
                steps = Steps(dve, norm_step, b.round * Norm.STEPS + Norm.PART_STARTS[n])
                norm.part(dve, steps, lambda j: sh.x[:, b.n + j, :], n)

            def norm_rows(b):
                for j in range(2):
                    norm.apply(dve, xn[:, j, :], sh.x[:, b.n + j, :], j).then_inc(xn_ready, 1)

            def empty_rows(b):
                dve.wait_ge(banks.filled("xT"), banks.until_filled("xT", b))
                dve.tensor_copy(xnT[:, :, :], banks.at("xT")[:, 0:KT * P].rearrange("p (a b) -> p a b", a=KT)).then_inc(banks.emptied("xT"), 1)

            def empty_values(b, k):
                chunk = f"v{k}"
                dve.wait_ge(banks.filled(chunk), banks.until_filled(chunk, b))
                n = BT * P // dh
                dst = v[:, b.slot, k * n * HW:(k + 1) * n * HW].rearrange("p (h e) -> p h e", e=HW)[:, :, 0:dh]
                src = banks.at(chunk)[:, 0:n * dh].rearrange("p (h e) -> p h e", e=dh)
                if biased:
                    last = dve.tensor_tensor(dst, src, w["bv"].rearrange("p (h e) -> p h e", e=dh), ALU.add)
                else:
                    last = dve.tensor_copy(dst, src)
                last.then_inc(banks.emptied(chunk), 1)

            def center(b, u, first=False):
                n = unit(b, u)
                dve.wait_ge(scored, n + 1)
                if not first:
                    dve.wait_ge(exped, n - 1)
                scores = S[:, u % 2, :, :]
                if masked:
                    dve.wait_ge(side_ready, n + 1)
                    dve.scalar_tensor_tensor(out=d[:, u % 2, :, :].rearrange("p a b -> p (a b)"),
                                             in0=sm[:, u % 2, :, :].rearrange("p a b -> p (a b)"), scalar=2.0,
                                             in1=scores.rearrange("p a b -> p (a b)"), op0=ALU.mult, op1=ALU.add).then_inc(side_used, 1)
                    dve.wait_ge(side_used, n + 1)
                    scores = d[:, u % 2, :, :]
                dve.tensor_reduce(mx[:, u % 2, :], scores, AX.X, ALU.max).then_inc(max_step, 1)
                dve.wait_ge(max_step, n + 1)
                dve.tensor_tensor(d[:, u % 2, :, :], scores, mx[:, u % 2, :].unsqueeze(2).broadcast_to([P, UH, P]),
                                  ALU.subtract).then_inc(centered, 1)

            def normalize(b, u):
                n, slot, at = (b.n, b.slot, 0) if small else (unit(b, u), u % 2, u * UH * dh)
                dve.wait_ge(summed, n + 1)
                ps = O[:, slot, 0:HO * HW].rearrange("p (h e) -> p h e", e=HW)
                dve.reciprocal(rc[:, slot, :].unsqueeze(2), ps[:, :, dh:HW]).then_inc(recip_step, 1)
                dve.wait_ge(recip_step, n + 1)
                dve.tensor_tensor(o[:, at:at + HO * dh].rearrange("p (h e) -> p h e", e=dh), ps[:, :, 0:dh],
                                  rc[:, slot, :].unsqueeze(2).broadcast_to([P, HO, dh]), ALU.mult).then_inc(normed, 1)

            def add_out(b):
                dve.wait_ge(banks.filled("proj"), banks.until_filled("proj", b))
                if biased:
                    dve.wait_ge(bias_added, b.n + 1)
                dve.tensor_tensor(sh.x[:, b.n, :], banks.at("proj")[:, 0:D], sh.x[:, b.n, :], ALU.add).then_inc(banks.emptied("proj"), 1)

            sh.wait_params(dve, phase)
            banks.open(dve)
            if not small:
                dve.sem_inc(normed, 2)
            dve.wait_ge(v_set, 1)
            start = Turn(0, 0)
            for n in range(3):
                norm_part(start, n)
            norm_rows(start)
            dve.wait_ge(xn_ready, 2)
            empty_rows(start)
            for k in range(NB):
                empty_values(start, k)
            empty_rows(start.plus(1))
            center(start, 0, first=True)
            center(start, 1, first=True)
            for n in range(3):
                norm_part(start.plus(2), n)
            with dve.Fori(0, BATCH // 2) as i:
                for s in range(2):
                    b = Turn(i, s)
                    for u in range(U):
                        center(b.plus((u + 2) // U), (u + 2) % U)
                        if s == 0 and u == 0:
                            norm_rows(b.plus(2))
                        if s == 1 and u == 0:
                            dve.wait_ge(xn_ready, b.n + 3)
                        if s == 1 and u < 3:
                            norm_part(b.plus(3), u)
                        if not small or u == U - 1:
                            normalize(b, u)
                        if u == U - 1:
                            empty_rows(b.plus(2))
                        if u == U - 2:
                            empty_values(b.plus(1), 0)
                    if not small:
                        empty_values(b.plus(1), NB - 1)
                    add_out(b)
class Chunks:

    def __init__(self, emptied_by):
        self.by = emptied_by

    def total(self, who):
        return self.by.count(who)

    def emptied(self, c):
        return self.by[:c + 1].count(self.by[c])




def key_bound(nc, sh, w):
    T = 512
    TURNS = BATCH * P // T
    c = sh.const
    with ExitStack() as ctx:
        core = Core(nc, ctx, "kstab")
        cT = core.sb("ctxT", [P, KT, T])
        k2 = core.sb("k_squared", [P, KT, T])
        bk = core.sb("bk_scaled", [P, 2])
        top = core.sb("top", [P, TURNS])
        top1 = core.sb("top1", [P, 1])
        topT = core.sb("topT", [P, 1])
        K = core.ps("K", [P, 2, T])
        H = core.ps("H", [P, 2, T])
        loaded, projected, squared, headed, topped, step = (core.sem(s) for s in (
            "ctx_loaded", "projected", "squared", "headed", "topped", "dve_step"))
        block = ctx.enter_context(nc.Block())

        @block.sync
        def _(sp):
            sp.dma_start(cT[:, :, :], sh.dram["ctxT"][:, :, 0:T]).then_inc(loaded, 16)
            with sp.Fori(0, TURNS - 1) as i:
                sp.wait_ge(projected, i + 1)
                sp.dma_start(cT[:, :, :], sh.dram["ctxT"][:, :, bass.ts(i + 1, T)]).then_inc(loaded, 16)

        @block.tensor
        def _(pe):
            sh.wait_params(pe, "L1x")
            with pe.Fori(0, TURNS) as i:
                pe.wait_ge(loaded, (i + 1) * 16)
                for t in range(2):
                    for k in range(KT):
                        mm = pe.matmul(K[:, t, :], w["wk"][:, k, t * P:(t + 1) * P], cT[:, k, :], start=(k == 0), stop=(k == 1))
                mm.then_inc(projected, 1)
                pe.wait_ge(squared, (i + 1) * 2)
                pe.wait_ge(topped, i + 1)
                for t in range(2):
                    mm = pe.matmul(H[0:8, t, :], c["headsum"], k2[:, t, :], start=True, stop=True)
                mm.then_inc(headed, 1)
            pe.wait_ge(step, 2)
            pe.transpose(H[0:1, 0, 0:8], top1[0:8, 0:1], c["ident"][0:8, 0:8]).then_inc(headed, 1)
            pe.wait_ge(step, 3)
            pe.matmul(H[:, 1, 0:1], c["ones"][0:1, :], topT[0:1, :], start=True, stop=True).then_inc(headed, 1)

        @block.scalar
        def _(act):
            act.wait_ge(step, 1)
            with act.Fori(0, TURNS) as i:
                act.wait_ge(projected, i + 1)
                for t in range(2):
                    act.activation(k2[:, t, :], K[:, t, :], ACT.Square, bias=bk[:, t:t + 1], scale=0.25).then_inc(squared, 1)

        @block.vector
        def _(dve):
            sh.wait_params(dve, "L1x")
            dve.tensor_scalar(bk[:, :], w["bk"], 0.25, None, ALU.mult).then_inc(step, 1)
            dve.sem_inc(topped, 1)
            with dve.Fori(0, TURNS) as i:
                dve.wait_ge(headed, i + 1)
                dve.tensor_reduce(top[0:8, bass.ds(i, 1)], H[0:8, :, :].rearrange("p a b -> p (a b)"), AX.X, ALU.max).then_inc(topped, 1)
            dve.wait_ge(topped, TURNS + 1)
            dve.tensor_reduce(top1[0:8, :], top[0:8, :], AX.X, ALU.max).then_inc(step, 1)
            dve.wait_ge(headed, TURNS + 1)
            dve.tensor_reduce(topT[0:1, :], H[0:1, 0, 0:8], AX.X, ALU.max).then_inc(step, 1)
            dve.wait_ge(headed, TURNS + 2)
            dve.tensor_scalar(sh.kstab[:, :], H[:, 1, 0:1], -1.0, None, ALU.mult).then_inc(step, 1)
            dve.wait_ge(step, 4)


def performer_phase(nc, sh, phase, next_phase):
    G = 2
    TURNS = BATCH // G
    T = G * P
    dh, HW = 16, 17
    VW = HEADS * HW + P - HW
    UH, UB = 4, 4
    U = G * UB
    PAIRS = HEADS // 2
    EPS, STAB = 1e-4, 1e-6
    w, c = sh.params(phase), sh.const
    chunks = Chunks(["v", "a", "a"] + ["a"] * 8 + ["v"] + ["a", "v"] * G)
    CFQ, CFK, CV, CO = 3, 7, 11, 12
    NA, NV, NC = chunks.total("a"), chunks.total("v"), len(chunks.by)
    key_bound(nc, sh, w)

    with ExitStack() as ctx:
        core = Core(nc, ctx, phase)
        norm = Norm(core, G)
        xn = core.sb("xn", [P, G, D])
        xnT = core.sb("xnT", [P, KT, T])
        cT = core.sb("ctxT", [P, KT, T])
        qT = core.sb("qT", [P, 2, T])
        kT = core.sb("kT", [P, 2, T])
        k2 = core.sb("k_squared", [P, 2, T])
        b4 = core.sb("biases_scaled", [P, 2, 2])
        qe = core.sb("q_exp", [P, PAIRS, T])
        kf = core.sb("k_features", [P, PAIRS, T])
        qf = core.sb("q_features", [P, 2, PAIRS, T])
        v = core.sb("v_ones", [P, G, VW])
        at = core.sb("products", [P, 2, UH, P])
        den = core.sb("den", [P, HEADS])
        low = core.sb("den_low", [P, HEADS])
        o = core.sb("heads_out", [P, G, D])
        oT = core.sb("heads_outT", [P, 2, P])
        S = core.ps("S", [P, 2, UH, P])
        O = core.ps("O", [P, 2, BANK])
        gen = core.ps("gen", [P, 2, BANK])
        (ctx_loaded, xn_ready, bias_added, filled, emptied_a, emptied_v, qf_ready, kf_ready, v_set, scored, cut, summed,
         normed, dve_step, squared, scaled) = (core.sem(s) for s in (
            "ctx_loaded", "xn_ready", "bias_added", "gen_filled", "gen_emptied_act", "gen_emptied_dve", "q_features",
            "k_features", "v_ones_set", "scored", "cut", "heads_summed", "heads_normed", "dve_step", "k_squared", "scaled"))
        block = ctx.enter_context(nc.Block())
        emptied = {"a": (emptied_a, NA), "v": (emptied_v, NV)}

        @block.sync
        def _(sp):
            if next_phase:
                sh.load_params(sp, next_phase)
            sp.dma_start(cT[:, :, :], sh.dram["ctxT"][:, :, 0:T]).then_inc(ctx_loaded, 16)
            with sp.Fori(0, TURNS - 1) as i:
                sp.wait_ge(emptied_v, i * NV + 2)
                sp.dma_start(cT[:, :, :], sh.dram["ctxT"][:, :, bass.ts(i + 1, T)]).then_inc(ctx_loaded, 16)

        @block.gpsimd
        def _(pool):
            pool.memset(v[:, :, :], 1.0).then_inc(v_set, 1)
            sh.wait_params(pool, phase)
            with pool.Fori(0, TURNS) as i:
                pool.wait_ge(xn_ready, (i + 1) * G)
                for j in range(G):
                    pool.tensor_tensor(sh.x[:, i * G + j, :], sh.x[:, i * G + j, :], w["bo"], ALU.add).then_inc(bias_added, 1)
                for n in range(4):
                    pool.wait_ge(emptied_a, i * NA + CFQ + n)
                    detach_wait(pool)
                    for m in range(2):
                        pool.tensor_scalar(qf[:, m, 2 * n:2 * n + 2, :], qe[:, 2 * n:2 * n + 2, :], EPS, c["feat2"][:, m:m + 1],
                                           ALU.add, ALU.mult).then_inc(qf_ready, 1)

        @block.scalar
        def _(act):
            sh.wait_params(act, phase)
            for n, bias in enumerate(("bq", "bk")):
                act.activation(b4[:, n, :], w[bias], ACT.Copy, scale=0.25).then_inc(scaled, 1)
            act.wait_ge(scaled, 2)
            with act.Fori(0, TURNS) as i:
                for n, dst in enumerate((qT, kT)):
                    act.wait_ge(filled, i * NC + n + 2)
                    for t in range(2):
                        last = act.activation(dst[:, t, :], gen[:, (n + 1) % 2, t * T:(t + 1) * T], ACT.Identity,
                                              bias=b4[:, n, t:t + 1], scale=0.25)
                    last.then_inc(emptied_a, 1)
                act.wait_ge(emptied_a, i * NA + 2)
                act.activation(k2[:, :, :], kT[:, :, :], ACT.Square).then_inc(squared, 1)
                for n in range(8):
                    cc = CFQ + n
                    act.wait_ge(filled, i * NC + cc + 1)
                    src = gen[:, cc % 2, :].rearrange("p (a b) -> p a b", a=2)
                    if n < 4:
                        act.activation(qe[:, 2 * n:2 * n + 2, :], src, ACT.Exp).then_inc(emptied_a, 1)
                    else:
                        act.activation(kf[:, 2 * n - 8:2 * n - 6, :], src, ACT.Exp, bias=sh.kstab[:, :]).then_inc(emptied_a, 1)
                for j in range(G):
                    cc = CO + 2 * j
                    act.wait_ge(filled, i * NC + cc + 1)
                    act.activation(oT[:, :, :], gen[:, cc % 2, 0:D].rearrange("p (a b) -> p a b", a=2), ACT.Copy).then_inc(emptied_a, 1)

        @block.tensor
        def _(pe):
            def free_bank(i, cc):
                if cc >= 2:
                    s, per = emptied[chunks.by[cc - 2]]
                    pe.wait_ge(s, i * per + chunks.emptied(cc - 2))

            sh.wait_params(pe, phase)
            with pe.Fori(0, TURNS) as i:
                pe.wait_ge(xn_ready, (i + 1) * G)
                for k in range(KT):
                    for j in range(G):
                        mm = pe.transpose(gen[:, 0, k * T + j * P:k * T + (j + 1) * P], xn[:, j, k * P:(k + 1) * P], c["ident"])
                mm.then_inc(filled, 1)
                for n, (weights, source) in enumerate(((w["wq"], xnT), (w["wk"], cT))):
                    if n == 0:
                        pe.wait_ge(emptied_v, i * NV + 1)
                    else:
                        free_bank(i, 2)
                        pe.wait_ge(ctx_loaded, (i + 1) * 16)
                    for t in range(2):
                        for k in range(KT):
                            mm = pe.matmul(gen[:, (n + 1) % 2, t * T:(t + 1) * T], weights[:, k, t * P:(t + 1) * P], source[:, k, :],
                                           start=(k == 0), stop=(k == KT - 1))
                    mm.then_inc(filled, 1)
                for n in range(8):
                    cc = CFQ + n
                    free_bank(i, cc)
                    if n == 0:
                        pe.wait_ge(emptied_a, i * NA + 2)
                    if n == 4:
                        pe.wait_ge(squared, i + 1)
                    for a in range(2):
                        t, s = divmod((2 * n + a) % PAIRS, 4)
                        out = gen[:, cc % 2, a * T:(a + 1) * T]
                        mm = pe.matmul(out, w["rf"][:, s, :], (qT if n < 4 else kT)[:, t, :], start=True, stop=(n < 4))
                        if n >= 4:
                            mm = pe.matmul(out, c["half"][:, s, :], k2[:, t, :], start=False, stop=True)
                    mm.then_inc(filled, 1)
                free_bank(i, CV)
                for j in range(G):
                    for k in range(KT):
                        mm = pe.matmul(gen[:, CV % 2, j * D:(j + 1) * D], cT[:, k, j * P:(j + 1) * P], w["wv"][:, k, :],
                                       start=(k == 0), stop=(k == KT - 1))
                mm.then_inc(filled, 1)
                pe.wait_ge(emptied_v, i * NV + 2)
                for u in range(U + 1):
                    if u < U:
                        j, h0 = u // UB, (u % UB) * UH
                        if u < UB:
                            pe.wait_ge(qf_ready, i * 8 + 2 * u + 2)
                            pe.wait_ge(kf_ready, i * 4 + u + 1)
                        if u >= 2:
                            pe.wait_ge(cut, i * U + u - 1)
                        for r in range(UH):
                            h = h0 + r
                            mm = pe.matmul(S[:, u % 2, r, :], kf[:, h // 2, j * P:(j + 1) * P],
                                           qf[:, h % 2, h // 2, j * P:(j + 1) * P], start=True, stop=True)
                        mm.then_inc(scored, 1)
                    if u >= 1:
                        n = u - 1
                        j, h0 = n // UB, (n % UB) * UH
                        pe.wait_ge(cut, i * U + n + 1)
                        for r in range(UH):
                            h = h0 + r
                            mm = pe.matmul(O[:, j, h * HW:h * HW + P], at[:, n % 2, r, :], v[:, j, h * HW:h * HW + P],
                                           start=True, stop=True, skip_group_check=True)
                        if n % UB == UB - 1:
                            mm.then_inc(summed, 1)
                for j in range(G):
                    pe.wait_ge(normed, i * G + j + 1)
                    free_bank(i, CO + 2 * j)
                    for t in range(2):
                        mm = pe.transpose(gen[:, (CO + 2 * j) % 2, t * P:(t + 1) * P], o[:, j, t * P:(t + 1) * P], c["ident"])
                    mm.then_inc(filled, 1)
                    free_bank(i, CO + 2 * j + 1)
                    pe.wait_ge(emptied_a, i * NA + 10 + j + 1)
                    for t in range(2):
                        mm = pe.matmul(gen[:, (CO + 2 * j + 1) % 2, 0:D], oT[:, t, :], w["wo"][:, t, :], start=(t == 0), stop=(t == 1))
                    mm.then_inc(filled, 1)

        @block.vector
        def _(dve):
            steps_per_turn = Norm.STEPS + 4 * G
            sh.wait_params(dve, phase)
            dve.wait_ge(v_set, 1)
            with dve.Fori(0, TURNS) as i:
                steps = Steps(dve, dve_step, i * steps_per_turn, steps_per_turn)
                norm.statistics(dve, steps, lambda j: sh.x[:, i * G + j, :])
                for j in range(G):
                    norm.apply(dve, xn[:, j, :], sh.x[:, i * G + j, :], j).then_inc(xn_ready, 1)
                dve.wait_ge(filled, i * NC + 1)
                dve.tensor_copy(xnT[:, :, :], gen[:, 0, :].rearrange("p (a b) -> p a b", a=KT)).then_inc(emptied_v, 1)
                for n in range(4):
                    dve.wait_ge(emptied_a, i * NA + CFK + n)
                    dve.tensor_scalar(kf[:, 2 * n:2 * n + 2, :], kf[:, 2 * n:2 * n + 2, :], EPS, 0.125, ALU.add, ALU.mult).then_inc(kf_ready, 1)
                dve.wait_ge(filled, i * NC + CV + 1)
                for j in range(G):
                    last = dve.tensor_tensor(v[:, j, 0:HEADS * HW].rearrange("p (h e) -> p h e", e=HW)[:, :, 0:dh],
                                             gen[:, CV % 2, j * D:(j + 1) * D].rearrange("p (h e) -> p h e", e=dh),
                                             w["bv"].rearrange("p (h e) -> p h e", e=dh), ALU.add)
                last.then_inc(emptied_v, 1)

                def normalize(j):
                    dve.wait_ge(summed, i * G + j + 1)
                    ps = O[:, j, 0:HEADS * HW].rearrange("p (h e) -> p h e", e=HW)
                    steps.link(dve.tensor_copy(den[:, :].unsqueeze(2), ps[:, :, dh:HW]))
                    steps.link(dve.tensor_scalar(low[:, :], den[:, :], STAB, 2.0 * STAB, ALU.is_le, ALU.mult))
                    steps.link(dve.tensor_tensor(den[:, :], den[:, :], low[:, :], ALU.add))
                    steps.link(dve.reciprocal(den[:, :], den[:, :]))
                    dve.tensor_tensor(o[:, j, :].rearrange("p (h e) -> p h e", e=dh), ps[:, :, 0:dh],
                                      den[:, :].unsqueeze(2).broadcast_to([P, HEADS, dh]), ALU.mult).then_inc(normed, 1)

                for u in range(U + 2):
                    if u < U:
                        dve.wait_ge(scored, i * U + u + 1)
                        dve.tensor_tensor(at[:, u % 2, :, :], S[:, u % 2, :, :], c["causal"].unsqueeze(1).broadcast_to([P, UH, P]),
                                          ALU.mult).then_inc(cut, 1)
                    if u >= UB + 1 and (u - UB - 1) % UB == 0:
                        normalize((u - UB - 1) // UB)
                for j in range(G):
                    dve.wait_ge(filled, i * NC + CO + 2 * j + 2)
                    dve.wait_ge(bias_added, i * G + j + 1)
                    dve.tensor_tensor(sh.x[:, i * G + j, :], gen[:, (CO + 2 * j + 1) % 2, 0:D], sh.x[:, i * G + j, :],
                                      ALU.add).then_inc(emptied_v, 1)
                dve.wait_ge(emptied_v, (i + 1) * NV)
                steps.close()


def first_of_max(dve, steps, out, scores, best, marks, iota, n, size):
    steps.link(dve.tensor_reduce(best, scores, AX.X, ALU.max))
    steps.link(dve.tensor_tensor(marks, scores, best.unsqueeze(2).broadcast_to([P, n, size]), ALU.is_equal))
    steps.link(dve.scalar_tensor_tensor(out=marks, in0=marks, scalar=-float(size), in1=iota, op0=ALU.mult, op1=ALU.add))
    return marks


FIRST_STEPS = 5


def top_two(dve, steps, chosen, scores, rest, marks, best, second, iota, n, size, parts=range(4)):
    wide = lambda a: a.unsqueeze(2).broadcast_to([P, n, size])
    for part in parts:
        if part == 0:
            first_of_max(dve, steps, chosen, scores, best, marks, iota, n, size)
        if part == 1:
            steps.link(dve.tensor_reduce(second, marks, AX.X, ALU.min))
            steps.link(dve.tensor_tensor(chosen, marks, wide(second), ALU.is_equal))
            steps.link(dve.scalar_tensor_tensor(out=rest, in0=chosen, scalar=-NEVER, in1=scores, op0=ALU.mult, op1=ALU.add))
        if part == 2:
            first_of_max(dve, steps, chosen, rest, second, marks, iota, n, size)
        if part == 3:
            steps.link(dve.tensor_reduce(second, marks, AX.X, ALU.min))
            steps.link(dve.tensor_tensor(marks, marks, wide(second), ALU.is_equal))
            steps.link(dve.tensor_tensor(chosen, chosen, marks, ALU.add))


TOP_TWO_STEPS = 12


def experts_phase(nc, sh, phase, next_phase):
    G = 4
    TURNS = BATCH // G
    T = G * P
    E = 8
    relu = phase == "L1f"
    NF = 4 if relu else 2
    w, c = sh.params(phase), sh.const
    with ExitStack() as ctx:
        core = Core(nc, ctx, phase)
        norm = Norm(core, G)
        xn = core.sb("xn", [P, 2, G, D])
        xnT = core.sb("xnT", [P, 2, KT, T])
        hid = core.sb("hidden", [P, 2, NF, T])
        acc = core.sb("mixed", [P, G, D])
        gate = core.sb("gates", [P, 2, G, E])
        lg, rest, marks, chosen = (core.sb(n, [P, G, E]) for n in ("logits", "rest", "marks", "chosen"))
        best, second, total = (core.sb(n, [P, G]) for n in ("best", "second", "total"))
        if relu:
            norm2 = Norm(core, G, "close")
        else:
            silu = core.sb("silu", [P, 2, T])
        Z = core.ps("Z", [P, 4, T])
        Y = core.ps("Y", [P, 2, 2, D])
        gen = core.ps("gen", [P, 2, T])
        (xn_ready, turned, routed, xT_v, xT_a, hid_pre, hid_a, hid_v, summed, mixed, front_step, main_step, centered, exped,
         bias_added) = (core.sem(s) for s in (
            "xn_ready", "xn_turned", "logits_ready", "xnT_dve", "xnT_act", "hidden_summed", "hidden_act", "hidden_dve",
            "outputs_summed", "outputs_mixed", "front_step", "main_step", "logits_centered", "logits_exped", "bias_added"))
        block = ctx.enter_context(nc.Block())

        @block.sync
        def _(sp):
            if next_phase:
                sh.load_params(sp, next_phase)

        @block.gpsimd
        def _(pool):
            if relu:
                sh.wait_params(pool, phase)
                with pool.Fori(0, TURNS) as t:
                    pool.wait_ge(xn_ready, (t + 1) * G)
                    for j in range(G):
                        pool.tensor_tensor(sh.x[:, t * G + j, :], sh.x[:, t * G + j, :], w["beta"], ALU.add).then_inc(bias_added, 1)

        @block.scalar
        def _(act):
            def front_turn(t, s):
                act.wait_ge(turned, t * KT + 2)
                act.activation(xnT[:, s, 1, :], gen[:, 1, :], ACT.Copy).then_inc(xT_a, 1)

            def front_exp(t, s):
                act.wait_ge(centered, t + 1)
                act.activation(gate[:, s, :, :], gate[:, s, :, :], ACT.Exp).then_inc(exped, 1)

            def hidden(t, e, first=False):
                for f in range(NF):
                    act.wait_ge(hid_pre, (t * E + e) * 4 + f + 1)
                    if relu:
                        act.activation(hid[:, e % 2, f, :], Z[:, f, :], ACT.Relu, bias=w["b1"][:, e, f:f + 1]).then_inc(hid_a, 1)
                    else:
                        if not first:
                            act.wait_ge(hid_v, (t * E + e - 1) * 2 + f + 1)
                        act.activation(silu[:, f, :], Z[:, f, :], ACT.Silu).then_inc(hid_a, 1)

            sh.wait_params(act, phase)
            front_turn(0, 0)
            front_exp(0, 0)
            hidden(0, 0, first=True)
            with act.Fori(0, TURNS // 2) as i:
                for s in range(2):
                    t = i * 2 + s
                    for e in range(E):
                        hidden(*((t, e + 1) if e + 1 < E else (t + 1, 0)))
                        if e == 3:
                            front_turn(t + 1, 1 - s)
                        if e == 6:
                            front_exp(t + 1, 1 - s)

        @block.tensor
        def _(pe):
            def front_turn(t, s):
                pe.wait_ge(xn_ready, (t + 1) * G)
                for k in range(KT):
                    for j in range(G):
                        mm = pe.transpose(gen[:, k, j * P:(j + 1) * P], xn[:, s, j, k * P:(k + 1) * P], c["ident"])
                    mm.then_inc(turned, 1)

            def front_route(t, s):
                pe.wait_ge(xT_v, t + 1)
                pe.wait_ge(xT_a, t + 1)
                for j in range(G):
                    for k in range(KT):
                        mm = pe.matmul(gen[:, 0, j * P:(j + 1) * P], xnT[:, s, k, j * P:(j + 1) * P], w["wg"][:, k, :],
                                       start=(k == 0), stop=(k == KT - 1))
                mm.then_inc(routed, 1)

            def first_product(t, s, e, first=False):
                for f in range(4):
                    if not first:
                        if relu:
                            pe.wait_ge(hid_a, (t * E + e - 1) * 4 + f + 1)
                        elif f < 2:
                            pe.wait_ge(hid_a, (t * E + e - 1) * 2 + f + 1)
                        else:
                            pe.wait_ge(hid_v, (t * E + e - 1) * 2 + f - 1)
                    for k in range(KT):
                        mm = pe.matmul(Z[:, f, :], w["w1"][:, e, k, f * P:(f + 1) * P], xnT[:, s, k, :],
                                       start=(k == 0), stop=(k == KT - 1))
                    mm.then_inc(hid_pre, 1)

            def second_product(t, e):
                pe.wait_ge(*((hid_a, (t * E + e + 1) * 4) if relu else (hid_v, (t * E + e + 1) * 2)))
                for pair in range(2):
                    pe.wait_ge(mixed, (t * E + e) * 2 + pair + 1)
                    for j in range(2):
                        b = 2 * pair + j
                        for f in range(NF):
                            mm = pe.matmul(Y[:, pair, j, :], hid[:, e % 2, f, b * P:(b + 1) * P], w["w2"][:, e, f, :],
                                           start=(f == 0), stop=(f == NF - 1))
                    mm.then_inc(summed, 1)

            sh.wait_params(pe, phase)
            front_turn(0, 0)
            front_route(0, 0)
            pe.wait_ge(routed, 1)
            first_product(0, 0, 0, first=True)
            with pe.Fori(0, TURNS // 2) as i:
                for s in range(2):
                    t = i * 2 + s
                    for e in range(E):
                        first_product(*((t, s, e + 1) if e + 1 < E else (t + 1, 1 - s, 0)))
                        second_product(t, e)
                        if e == 2:
                            front_turn(t + 1, 1 - s)
                        if e == 4:
                            front_route(t + 1, 1 - s)

        @block.vector
        def _(dve):
            FRONT = Norm.STEPS + 2 + TOP_TWO_STEPS + 4
            MAIN = E + 1 + Norm.STEPS + 2 + 1 if relu else 1

            def front_norm(t, s):
                steps = Steps(dve, front_step, t * FRONT)
                norm.statistics(dve, steps, lambda j: sh.x[:, t * G + j, :])
                for j in range(G):
                    norm.apply(dve, xn[:, s, j, :], sh.x[:, t * G + j, :], j).then_inc(xn_ready, 1)

            def front_turn(t, s):
                dve.wait_ge(turned, t * KT + 1)
                dve.tensor_copy(xnT[:, s, 0, :], gen[:, 0, :]).then_inc(xT_v, 1)

            def front_center(t, s):
                steps = Steps(dve, front_step, t * FRONT + Norm.STEPS)
                dve.wait_ge(routed, t + 1)
                steps.link(dve.tensor_tensor(lg[:, :, :], gen[:, 0, :].rearrange("p (j e) -> p j e", j=G)[:, :, 0:E],
                                             w["bg"].unsqueeze(1).broadcast_to([P, G, E]), ALU.add))
                steps.link(dve.tensor_reduce(best[:, :], lg[:, :, :], AX.X, ALU.max))
                dve.tensor_tensor(gate[:, s, :, :], lg[:, :, :], best[:, :].unsqueeze(2).broadcast_to([P, G, E]),
                                  ALU.subtract).then_inc(centered, 1)

            def front_gate(t, s):
                steps = Steps(dve, front_step, t * FRONT + Norm.STEPS + 2, TOP_TWO_STEPS + 4)
                dve.wait_ge(centered, t + 1)
                top_two(dve, steps, chosen[:, :, :], lg[:, :, :], rest[:, :, :], marks[:, :, :], best[:, :], second[:, :],
                        c["iota8"].unsqueeze(1).broadcast_to([P, G, E]), G, E)
                dve.wait_ge(exped, t + 1)
                steps.link(dve.tensor_tensor(gate[:, s, :, :], gate[:, s, :, :], chosen[:, :, :], ALU.mult))
                steps.link(dve.tensor_reduce(total[:, :], gate[:, s, :, :], AX.X, ALU.add))
                steps.link(dve.reciprocal(total[:, :], total[:, :]))
                steps.link(dve.tensor_tensor(gate[:, s, :, :], gate[:, s, :, :], total[:, :].unsqueeze(2).broadcast_to([P, G, E]), ALU.mult))
                steps.close()

            def multiply(t, e):
                for f in range(2):
                    dve.wait_ge(hid_a, (t * E + e) * 2 + f + 1)
                    dve.wait_ge(hid_pre, (t * E + e) * 4 + f + 3)
                    dve.tensor_tensor(hid[:, e % 2, f, :], silu[:, f, :], Z[:, f + 2, :], ALU.mult).then_inc(hid_v, 1)

            def second_biases(steps, s):
                for e in range(E):
                    for j in range(G):
                        g = gate[:, s, j, e:e + 1]
                        if e == 0:
                            last = dve.tensor_scalar(acc[:, j, :], w["b2"][:, e, :], g, None, ALU.mult)
                        else:
                            last = dve.scalar_tensor_tensor(out=acc[:, j, :], in0=w["b2"][:, e, :], scalar=g,
                                                            in1=acc[:, j, :], op0=ALU.mult, op1=ALU.add)
                    steps.link(last)

            def mix(t, s, e):
                for pair in range(2):
                    dve.wait_ge(summed, (t * E + e) * 2 + pair + 1)
                    for j in range(2):
                        b = 2 * pair + j
                        g = gate[:, s, b, e:e + 1]
                        if e == 0 and not relu:
                            last = dve.tensor_scalar(acc[:, b, :], Y[:, pair, j, :], g, None, ALU.mult)
                        else:
                            last = dve.scalar_tensor_tensor(out=acc[:, b, :], in0=Y[:, pair, j, :], scalar=g,
                                                            in1=acc[:, b, :], op0=ALU.mult, op1=ALU.add)
                    last.then_inc(mixed, 1)

            sh.wait_params(dve, phase)
            front_norm(0, 0)
            front_turn(0, 0)
            front_center(0, 0)
            front_gate(0, 0)
            dve.sem_inc(mixed, 2)
            if not relu:
                multiply(0, 0)
            with dve.Fori(0, TURNS // 2) as i:
                for s in range(2):
                    t = i * 2 + s
                    steps = Steps(dve, main_step, t * MAIN, MAIN)
                    if relu:
                        second_biases(steps, s)
                    for e in range(E):
                        if not relu:
                            multiply(*((t, e + 1) if e + 1 < E else (t + 1, 0)))
                        mix(t, s, e)
                        if e == 0:
                            front_norm(t + 1, 1 - s)
                        if e == 2:
                            front_turn(t + 1, 1 - s)
                        if e == 4:
                            front_center(t + 1, 1 - s)
                        if e == 5:
                            front_gate(t + 1, 1 - s)
                    dve.wait_ge(mixed, (t + 1) * E * 2 + 2)
                    if relu:
                        steps.link(dve.tensor_tensor(acc[:, :, :], acc[:, :, :], xn[:, s, :, :], ALU.add))
                        norm2.statistics(dve, steps, lambda j: acc[:, j, :])
                        for j in range(G):
                            last = norm2.apply(dve, acc[:, j, :], acc[:, j, :], j)
                        steps.link(last)
                        steps.link(dve.tensor_tensor(acc[:, :, :], acc[:, :, :], w["gamma"].unsqueeze(1).broadcast_to([P, G, D]), ALU.mult))
                        dve.wait_ge(bias_added, (t + 1) * G)
                    steps.link(dve.tensor_tensor(sh.x[:, bass.ts(t, G), :], sh.x[:, bass.ts(t, G), :], acc[:, :, :], ALU.add))
                    steps.close()


def head_experts_phase(nc, sh, phase, next_phase):
    G = 4
    TURNS = BATCH // G
    T = G * P
    E, NH = 16, 8
    N = G * NH
    M = E * KT
    H = 2 * M
    w, c = sh.params(phase), sh.const
    names = (("xT0", "h0", "logits", "bias0", "proj0"), ("xT1", "h1", "gT", "bias1", "proj1"))
    tables = [([(n, 0) for n in bank[:4]], [(n, 1) for n in bank[:4]] + [(bank[4], 0)]) for bank in names]
    with ExitStack() as ctx:
        core = Core(nc, ctx, phase)
        norm = Norm(core, G)
        xn = core.sb("xn", [P, G, D])
        xnT = core.sb("xnT", [P, KT, T])
        hT = core.sb("hT", [P, KT, T])
        acc = core.sb("mixed", [P, 2, KT, T])
        hi = core.sb("h_high", [P, KT, T], F16)
        lo = core.sb("h_low", [P, KT, T], F16)
        w1s = core.sb("w1_stacked", [P, E, P], F16)
        gb = core.sb("gates_wide", [P, 2, KT, T])
        tmp = core.sb("gated", [P, 2, T])
        gT = core.sb("gatesT", [P, T])
        rest, marks, chosen = (core.sb(n, [P, N, E]) for n in ("rest", "marks", "chosen"))
        best, second = (core.sb(n, [P, N]) for n in ("best", "second"))
        stack = sh.scratch(phase, 0, (2, 2048)).rearrange("p a b -> p (a b)").bitcast(F16).rearrange(
            "p (n t s c) -> p n t s c", n=2, t=KT, s=4)
        hid = sh.scratch(phase, 4096, (4, 2, T))
        pr = sh.scratch(phase, 8192, (N, E))
        Z = core.ps("Z", [P, 2, 2, T])
        O = core.ps("O", [P, 2, T])
        gen = core.ps("gen", [P, 2, T])
        banks = Banks(core, gen, tables)
        (xn_ready, bias_added, h_ready, high, low, stacked, centered, exped, gated, stored, hid_pre,
         hid_ready, summed, weighted, mixed, norm_step, gate_step, w1_ready) = (core.sem(s) for s in (
            "xn_ready", "bias_added", "h_ready", "h_high", "h_low", "h_stacked",
            "logits_centered", "logits_exped", "gates_ready", "gates_stored", "hidden_summed", "hidden_ready",
            "outputs_summed", "outputs_weighted", "outputs_mixed", "norm_step", "gate_step", "w1_stacked"))
        block = ctx.enter_context(nc.Block())
        wide = [core.sem(f"gates_wide{n}") for n in range(2)]
        CREDIT = 2

        @block.sync
        def _(sp):
            def stack_parts(b, pieces):
                for piece in pieces:
                    part, s = piece // 4, piece % 4
                    if piece == 0:
                        sp.wait_ge(high, (b.n + 1) * KT)
                    if piece == 8:
                        sp.wait_ge(low, b.n + 1)
                    sp.dma_start(stack[32 * part:32 * part + 32, b.slot, :, s, :],
                                 (hi if part < 2 else lo)[32 * s:32 * s + 32, :, :]).then_inc(stacked, 16)

            def store_gates(b):
                sp.wait_ge(banks.emptied("gT"), banks.until_emptied("gT", b))
                detach_wait(sp)
                sp.dma_start(sh.dram["gates"][b.n], gT[:, :]).then_inc(stored, 16)
                sp.wait_ge(stored, (b.n + 1) * 16)
                detach_wait(sp)

            def load_gates(b, e):
                for t in range(KT):
                    rows = sh.dram["gates"][b.n, t * 64 + e:t * 64 + e + 3 * E + 1:E, :]
                    sp.dma_start(gb[:, e % 2, t, :], rows.unsqueeze(1).broadcast_to([4, 32, T])).then_inc(wide[e % 2], 16)

            if next_phase:
                sh.load_params(sp, next_phase)
            start = Turn(0, 0)
            stack_parts(start, range(16))
            store_gates(start)
            load_gates(start, 0)
            load_gates(start, 1)
            with sp.Fori(0, TURNS // 2) as i:
                for s in range(2):
                    b = Turn(i, s)
                    for e in range(E):
                        if 6 <= e < 14:
                            stack_parts(b.plus(1), range(2 * e - 12, 2 * e - 10))
                        if e == E - 2:
                            store_gates(b.plus(1))
                        sp.wait_ge(weighted, b.n * M + (e + 1) * KT + CREDIT)
                        detach_wait(sp)
                        load_gates(b.plus((e + 2) // E), (e + 2) % E)
            for n in range(2):
                sp.wait_ge(wide[n], (TURNS * (E // 2) + 1) * KT * 16)

        @block.gpsimd
        def _(pool):
            def bias_out(b, j):
                pool.wait_ge(xn_ready, (b.n + 1) * G)
                pool.tensor_tensor(sh.x[:, b.n * G + j, :], sh.x[:, b.n * G + j, :], w["bo"], ALU.add).then_inc(bias_added, 1)

            def high_part(b, t):
                pool.wait_ge(h_ready, b.n * KT + t + 1)
                detach_wait(pool)
                pool.tensor_copy(hi[:, t, :], hT[:, t, :]).then_inc(high, 1)

            sh.wait_params(pool, phase)
            start = Turn(0, 0)
            for j in range(G):
                bias_out(start, j)
            for t in range(KT):
                high_part(start, t)
            with pool.Fori(0, TURNS // 2) as i:
                for s in range(2):
                    b = Turn(i, s)
                    for m in range(M):
                        pool.wait_ge(weighted, b.n * M + m + 1 + CREDIT)
                        if m < KT:
                            pool.wait_ge(banks.emptied(f"bias{m}"), banks.until_emptied(f"bias{m}", b))
                        else:
                            pool.wait_ge(mixed, b.n * M + m - 1 + CREDIT)
                        pool.tensor_tensor(acc[:, s, m % KT, :], acc[:, s, m % KT, :], tmp[:, m % 2, :], ALU.add).then_inc(mixed, 1)
                        if 16 <= m < 16 + G:
                            bias_out(b.plus(1), m - 16)
                        if 8 <= m < 8 + KT:
                            high_part(b.plus(1), m - 8)

        @block.scalar
        def _(act):
            def exponentiate(b):
                act.wait_ge(centered, b.n + 1)
                act.activation(pr, pr, ACT.Exp).then_inc(exped, 1)

            sh.wait_params(act, phase)
            exponentiate(Turn(0, 0))
            with act.Fori(0, TURNS // 2) as i:
                for s in range(2):
                    b = Turn(i, s)
                    for n in range(H):
                        act.wait_ge(hid_pre, b.n * H + n + 1)
                        act.activation(hid[:, n % 4, :, :], Z[:, n % 2, :, :], ACT.Gelu, bias=w["b1"][:, n // 4:n // 4 + 1]).then_inc(hid_ready, 1)
                        if n == 30:
                            exponentiate(b.plus(1))

        @block.tensor
        def _(pe):
            def free(name, b):
                pe.wait_ge(banks.emptied(name), banks.until_free(name, b))

            def turn_rows(b):
                pe.wait_ge(xn_ready, (b.n + 1) * G)
                for k in range(KT):
                    free(f"xT{k}", b)
                    for j in range(G):
                        mm = pe.transpose(banks.at(f"xT{k}")[:, j * P:(j + 1) * P], xn[:, j, k * P:(k + 1) * P], c["ident"])
                    mm.then_inc(banks.filled(f"xT{k}"), 1)

            def project_heads(b, t):
                for k in range(KT):
                    free(f"h{k}", b)
                for k in range(KT):
                    mm = pe.matmul(banks.at(f"h{t}"), w["wm"][:, k, t * P:(t + 1) * P], xnT[:, k, :], start=(k == 0), stop=(k == KT - 1))
                mm.then_inc(banks.filled(f"h{t}"), 1)

            def route(b):
                free("logits", b)
                pe.wait_ge(h_ready, (b.n + 1) * KT)
                for j in range(G):
                    for k in range(KT):
                        mm = pe.matmul(banks.at("logits")[:, j * P:(j + 1) * P], hT[:, k, j * P:(j + 1) * P], w["emb"][:, k, :],
                                       start=(k == 0), stop=(k == KT - 1))
                mm.then_inc(banks.filled("logits"), 1)

            def turn_gates(b):
                free("gT", b)
                pe.wait_ge(gated, b.n + 1)
                for j in range(G):
                    mm = pe.transpose(banks.at("gT")[:, j * P:(j + 1) * P],
                                      chosen[:, j * NH:(j + 1) * NH, :].rearrange("p h e -> p (h e)"), c["ident"])
                mm.then_inc(banks.filled("gT"), 1)

            def weigh_biases(b, t):
                free(f"bias{t}", b)
                pe.wait_ge(banks.emptied("gT"), banks.until_emptied("gT", b))
                pe.matmul(banks.at(f"bias{t}"), w["b2"][:, t, :], gT[:, :], start=True, stop=True).then_inc(banks.filled(f"bias{t}"), 1)

            def first_product(b, n):
                e, t, half = n // 4, n // 2 % 2, n % 2
                if n == 0:
                    pe.wait_ge(stacked, (b.n + 1) * 256)
                for s in range(2):
                    mm = pe.matmul(Z[:, n % 2, s, :], w1s[:, e, :], stack[:, b.slot, t, 2 * half + s, :], start=True, stop=True)
                mm.then_inc(hid_pre, 1)

            def second_product(b, n):
                e, t, half = n // 4, n // 2 % 2, n % 2
                m = 2 * e + t
                if half == 0:
                    pe.wait_ge(weighted, b.n * M + m - 1 + CREDIT)
                for s in range(2):
                    at = 32 * (2 * half + s)
                    mm = pe.matmul(O[at:at + 32, m % 2, :], w["w2"][:, e, :], hid[:, n % 4, s, :], start=True, stop=True)
                mm.then_inc(summed, 1)

            def project_out(b, pair):
                pe.wait_ge(mixed, (b.n + 1) * M + CREDIT)
                free(f"proj{pair}", b)
                for j in range(2):
                    q = 2 * pair + j
                    for t in range(KT):
                        mm = pe.matmul(banks.at(f"proj{pair}")[:, j * D:(j + 1) * D], acc[:, b.slot, t, q * P:(q + 1) * P], w["wo"][:, t, :],
                                       start=(t == 0), stop=(t == KT - 1))
                mm.then_inc(banks.filled(f"proj{pair}"), 1)

            sh.wait_params(pe, phase)
            start = Turn(0, 0)
            turn_rows(start)
            project_heads(start, 0)
            project_heads(start, 1)
            route(start)
            pe.wait_ge(w1_ready, 2)
            first_product(start, 0)
            first_product(start, 1)
            turn_gates(start)
            weigh_biases(start, 0)
            weigh_biases(start, 1)
            with pe.Fori(0, TURNS // 2) as i:
                for s in range(2):
                    b = Turn(i, s)
                    for n in range(H):
                        pe.wait_ge(hid_ready, b.n * H + n + 1)
                        first_product(b.plus((n + 2) // H), (n + 2) % H)
                        second_product(b, n)
                        if n == 11:
                            turn_rows(b.plus(1))
                        if n in (15, 17):
                            project_heads(b.plus(1), (n - 15) // 2)
                        if n == 23:
                            route(b.plus(1))
                        if n == 50:
                            turn_gates(b.plus(1))
                        if n in (54, 56):
                            weigh_biases(b.plus(1), (n - 54) // 2)
                    project_out(b, 0)
                    project_out(b, 1)

        @block.vector
        def _(dve):
            GATE_STEPS = 1 + 3 + TOP_TWO_STEPS
            wide_ = lambda a: a.unsqueeze(2).broadcast_to([P, N, E])

            def norm_part(b, n):
                steps = Steps(dve, norm_step, b.n * Norm.STEPS + Norm.PART_STARTS[n])
                norm.part(dve, steps, lambda j: sh.x[:, b.n * G + j, :], n)

            def norm_rows(b):
                for j in range(G):
                    norm.apply(dve, xn[:, j, :], sh.x[:, b.n * G + j, :], j).then_inc(xn_ready, 1)

            def empty_rows(b, k):
                dve.wait_ge(banks.filled(f"xT{k}"), banks.until_filled(f"xT{k}", b))
                dve.tensor_copy(xnT[:, k, :], banks.at(f"xT{k}")).then_inc(banks.emptied(f"xT{k}"), 1)

            def empty_heads(b, t):
                dve.wait_ge(banks.filled(f"h{t}"), banks.until_filled(f"h{t}", b))
                dve.tensor_scalar(hT[:, t, :], banks.at(f"h{t}"), w["bm"][:, t:t + 1], None, ALU.add).then_inc(h_ready, 1)
                dve.sem_inc(banks.emptied(f"h{t}"), 1)

            def low_part(b):
                dve.wait_ge(high, (b.n + 1) * KT)
                dve.tensor_tensor(lo[:, :, :], hT[:, :, :], hi[:, :, :], ALU.subtract).then_inc(low, 1)

            def gate_part(b, n):
                starts = (0, 1, 4, 7, 10, 13)
                steps = Steps(dve, gate_step, b.n * GATE_STEPS + starts[min(n, 5)])
                if n == 0:
                    dve.wait_ge(banks.filled("logits"), banks.until_filled("logits", b))
                    logits = banks.at("logits").rearrange("p (n e) -> p n e", e=E)
                    steps.link(dve.tensor_reduce(best[:, :], logits, AX.X, ALU.max))
                    dve.tensor_tensor(pr, logits, wide_(best[:, :]), ALU.subtract).then_inc(centered, 1)
                    dve.wait_ge(centered, b.n + 1)
                    dve.sem_inc(banks.emptied("logits"), 1)
                elif n == 1:
                    dve.wait_ge(exped, b.n + 1)
                    steps.link(dve.tensor_reduce(best[:, :], pr, AX.X, ALU.add))
                    steps.link(dve.reciprocal(best[:, :], best[:, :]))
                    steps.link(dve.tensor_tensor(pr, pr, wide_(best[:, :]), ALU.mult))
                elif n < 6:
                    top_two(dve, steps, chosen[:, :, :], pr, rest[:, :, :], marks[:, :, :], best[:, :], second[:, :],
                            c["iota16"].unsqueeze(1).broadcast_to([P, N, E]), N, E, parts=[n - 2])
                else:
                    dve.tensor_tensor(chosen[:, :, :], chosen[:, :, :], pr, ALU.mult).then_inc(gated, 1)

            def empty_gates(b):
                dve.wait_ge(banks.filled("gT"), banks.until_filled("gT", b))
                dve.tensor_copy(gT[:, :], banks.at("gT")).then_inc(banks.emptied("gT"), 1)

            def empty_biases(b, t):
                dve.wait_ge(banks.filled(f"bias{t}"), banks.until_filled(f"bias{t}", b))
                dve.tensor_copy(acc[:, b.slot, t, :], banks.at(f"bias{t}")).then_inc(banks.emptied(f"bias{t}"), 1)

            def weigh(b, m):
                e = m // KT
                dve.wait_ge(summed, b.n * H + 2 * m + 2)
                dve.wait_ge(wide[e % 2], b.n * (E // 2 * KT * 16) + (e // 2 + 1) * KT * 16)
                dve.wait_ge(mixed, b.n * M + m - 1 + CREDIT)
                dve.tensor_tensor(tmp[:, m % 2, :], O[:, m % 2, :], gb[:, e % 2, m % KT, :], ALU.mult).then_inc(weighted, 1)

            def add_out(b, pair):
                name = f"proj{pair}"
                dve.wait_ge(banks.filled(name), banks.until_filled(name, b))
                dve.wait_ge(bias_added, (b.n + 1) * G)
                at = bass.ds(b.n * G + 2 * pair, 2)
                dve.tensor_tensor(sh.x[:, at, :], banks.at(name).rearrange("p (j d) -> p j d", j=2), sh.x[:, at, :],
                                  ALU.add).then_inc(banks.emptied(name), 1)

            sh.wait_params(dve, phase)
            banks.open(dve)
            dve.sem_inc(weighted, CREDIT)
            dve.sem_inc(mixed, CREDIT)
            start = Turn(0, 0)
            for n in range(3):
                norm_part(start, n)
            norm_rows(start)
            dve.tensor_copy(w1s[:, :, :], w["w1"]).then_inc(w1_ready, 1)
            dve.wait_ge(w1_ready, 1)
            for s in (1, 3):
                r = slice(32 * s, 32 * s + 32)
                last = dve.tensor_tensor(w1s[r, :, :], w["w1"][r, :, :], w1s[r, :, :], ALU.subtract)
            last.then_inc(w1_ready, 1)
            for k in range(KT):
                empty_rows(start, k)
            for t in range(KT):
                empty_heads(start, t)
            low_part(start)
            for n in range(7):
                gate_part(start, n)
            empty_gates(start)
            for t in range(KT):
                empty_biases(start, t)
            with dve.Fori(0, TURNS // 2) as i:
                for s in range(2):
                    b = Turn(i, s)
                    nxt = b.plus(1)
                    for m in range(M):
                        weigh(b, m)
                        if m == 0:
                            dve.wait_ge(xn_ready, (b.n + 1) * G)
                        if m in (0, 1, 3):
                            norm_part(nxt, (m + 1) // 2)
                        if m == 4:
                            norm_rows(nxt)
                        if m in (6, 7):
                            empty_rows(nxt, m - 6)
                        if m in (8, 9):
                            empty_heads(nxt, m - 8)
                        if m == 11:
                            low_part(nxt)
                        if m == 13:
                            gate_part(nxt, 0)
                        if m in (16, 17, 19, 21, 23):
                            gate_part(nxt, (16, 17, 19, 21, 23).index(m) + 1)
                        if m == 24:
                            dve.wait_ge(gate_step, (nxt.n + 1) * GATE_STEPS)
                            gate_part(nxt, 6)
                        if m == 26:
                            empty_gates(nxt)
                        if m in (28, 29):
                            empty_biases(nxt, m - 28)
                    for pair in range(2):
                        add_out(b, pair)
                    dve.wait_ge(banks.emptied("proj1"), banks.until_emptied("proj1", b))
                    dve.wait_ge(banks.emptied("proj0"), banks.until_emptied("proj0", b))


def quantized_phase(nc, sh, phase, next_phase):
    G = 2
    TURNS = BATCH // G
    T = G * P
    F = 1024
    FT = F // P
    FLOOR = 1e-5
    w, c = sh.params(phase), sh.const
    with ExitStack() as ctx:
        core = Core(nc, ctx, phase)
        norm, again = Norm(core, G), Norm(core, G, "ln1")
        wq1 = core.sb("w1_ternary", [P, KT, F], BF16)
        wq2 = core.sb("w2_ternary", [P, FT, D], BF16)
        ident = core.sb("ident16", [P, P], BF16)
        ws = core.sb("weight_scales", [P, 2])
        wi = core.sb("weight_inverse", [P, 2])
        xn = core.sb("xn", [P, G, D])
        xq = core.sb("x_int", [P, G, D], BF16)
        xqT = core.sb("x_intT", [P, KT, T], BF16)
        amax, inv = (core.sb(n, [P, G]) for n in ("amax", "inverse"))
        back = core.sb("back", [P, 2, G])
        h = core.sb("hidden", [P, 2, G, F])
        hn = core.sb("hidden_norm", [P, 2, G, F])
        hq = core.sb("hidden_int", [P, G, F], BF16)
        hqT = core.sb("hidden_intT", [P, G, FT, P], BF16)
        stats2 = core.sb("ln2_stats", [P, G, 2, 6])
        mv2 = core.sb("ln2_mean_var", [P, G, 2])
        half2 = core.sb("ln2_half", [P, G], I32)
        root2, tmp2, shift2, amax2, inv2, back2 = (core.sb(n, [P, G]) for n in (
            "ln2_root", "ln2_tmp", "ln2_shift", "amax2", "inverse2", "back2"))
        Hp = core.ps("H", [P, G, F])
        XT = core.ps("XT", [P, 2 * KT, T], BF16)
        HT = core.ps("HT", [P, FT, P], BF16)
        Y = core.ps("Y", [P, G, BANK])
        (w_summed, w_total, w_ready, ident_ready, norm_ready, bias_added, quantized, x_turned, xT_ready, hid_pre, hid_scaled,
         hid_biased, hid_act, shifted, normalized, gained, affine, hq_ready, h_turned, hT_ready, out_ready, out_added, prep_step,
         front_step, norm2_step, quant_step) = (core.sem(s) for s in (
            "weights_summed", "weights_total", "weights_ready", "ident16_ready", "x_read", "bias_added", "x_quantized",
            "x_turned", "xT_ready", "hidden_summed", "hidden_scaled", "hidden_biased", "hidden_act", "ln2_ready",
            "hidden_normalized", "hidden_gained", "hidden_affine", "hidden_quantized", "hidden_turned", "hiddenT_ready",
            "out_summed", "out_added", "prep_step", "front_step", "ln2_step", "quantize_step"))
        block = ctx.enter_context(nc.Block())

        @block.sync
        def _(sp):
            if next_phase:
                sh.load_params(sp, next_phase)

        @block.gpsimd
        def _(pool):
            def bias_hidden(b):
                for j in range(G):
                    pool.wait_ge(hid_scaled, b.n * G + j + 1)
                    pool.tensor_tensor(h[:, b.slot, j, :], h[:, b.slot, j, :], w["b1"], ALU.add).then_inc(hid_biased, 1)

            def affine_hidden(b):
                for j in range(G):
                    pool.wait_ge(normalized, b.n * G + j + 1)
                    pool.tensor_tensor(hn[:, b.slot, j, :], hn[:, b.slot, j, :], w["g2"], ALU.mult).then_inc(gained, 1)
                    pool.wait_ge(gained, b.n * G + j + 1)
                    pool.tensor_tensor(hn[:, b.slot, j, :], hn[:, b.slot, j, :], w["c2"], ALU.add).then_inc(affine, 1)

            def bias_out(b):
                pool.wait_ge(norm_ready, b.n + 1)
                for j in range(G):
                    pool.tensor_tensor(sh.x[:, b.n * G + j, :], sh.x[:, b.n * G + j, :], w["b2"], ALU.add).then_inc(bias_added, 1)

            sh.wait_params(pool, phase)
            pool.tensor_copy(ident[:, :], c["ident"]).then_inc(ident_ready, 1)
            start = Turn(0, 0)
            bias_hidden(start)
            bias_hidden(start.plus(1))
            affine_hidden(start)
            with pool.Fori(0, TURNS // 2) as i:
                for s in range(2):
                    b = Turn(i, s)
                    bias_hidden(b.plus(2))
                    affine_hidden(b.plus(1))
                    bias_out(b)

        @block.scalar
        def _(act):
            def empty_rows(b):
                act.wait_ge(x_turned, b.n + 1)
                act.activation(xqT[:, :, :], XT[:, 0:KT, :], ACT.Copy).then_inc(xT_ready, 1)

            def scale_hidden(b):
                for j in range(G):
                    act.wait_ge(hid_pre, b.n * G + j + 1)
                    act.activation(h[:, b.slot, j, :], Hp[:, j, :], ACT.Copy, scale=back[:, b.slot, j:j + 1]).then_inc(hid_scaled, 1)

            def gelu(b):
                for j in range(G):
                    act.wait_ge(hid_biased, b.n * G + j + 1)
                    act.activation(h[:, b.slot, j, :], h[:, b.slot, j, :], ACT.Gelu).then_inc(hid_act, 1)

            def normalize(b):
                act.wait_ge(shifted, b.n + 1)
                for j in range(G):
                    act.activation(hn[:, b.slot, j, :], h[:, b.slot, j, :], ACT.Identity, bias=shift2[:, j:j + 1],
                                   scale=root2[:, j:j + 1]).then_inc(normalized, 1)

            def empty_hidden(b):
                for j in range(G):
                    act.wait_ge(h_turned, b.n * G + j + 1)
                    act.activation(hqT[:, j, :, :], HT[:, :, :], ACT.Copy).then_inc(hT_ready, 1)

            start = Turn(0, 0)
            for k in range(2):
                empty_rows(start.plus(k))
                scale_hidden(start.plus(k))
            gelu(start)
            normalize(start)
            gelu(start.plus(1))
            empty_rows(start.plus(2))
            act.wait_ge(normalized, G)
            scale_hidden(start.plus(2))
            with act.Fori(0, TURNS // 2) as i:
                for s in range(2):
                    b = Turn(i, s)
                    normalize(b.plus(1))
                    gelu(b.plus(2))
                    empty_hidden(b)
                    empty_rows(b.plus(3))
                    act.wait_ge(normalized, (b.n + 2) * G)
                    scale_hidden(b.plus(3))

        @block.tensor
        def _(pe):
            def first_product(b, first=False):
                pe.wait_ge(quantized, b.n + 1)
                for k in range(KT):
                    for j in range(G):
                        mm = pe.transpose(XT[:, k, j * P:(j + 1) * P], xq[:, j, k * P:(k + 1) * P], ident[:, :])
                mm.then_inc(x_turned, 1)
                pe.wait_ge(xT_ready, b.n + 1)
                for j in range(G):
                    if not first:
                        pe.wait_ge(hid_scaled, b.n * G + j - 1)
                    for half in range(2):
                        for k in range(KT):
                            mm = pe.matmul(Hp[:, j, half * BANK:(half + 1) * BANK], xqT[:, k, j * P:(j + 1) * P],
                                           wq1[:, k, half * BANK:(half + 1) * BANK], start=(k == 0), stop=(k == KT - 1))
                    mm.then_inc(hid_pre, 1)

            def second_product(b):
                for j in range(G):
                    pe.wait_ge(hq_ready, b.n * G + j + 1)
                    if j >= 1:
                        pe.wait_ge(hT_ready, b.n * G + j)
                    for t in range(FT):
                        mm = pe.transpose(HT[:, t, :], hq[:, j, t * P:(t + 1) * P], ident[:, :])
                    mm.then_inc(h_turned, 1)
                for j in range(G):
                    pe.wait_ge(hT_ready, b.n * G + j + 1)
                    for t in range(FT):
                        mm = pe.matmul(Y[:, j, 0:D], hqT[:, j, t, :], wq2[:, t, :], start=(t == 0), stop=(t == FT - 1))
                    mm.then_inc(out_ready, 1)

            pe.wait_ge(w_summed, 2)
            pe.matmul(Y[:, 0, 0:2], c["ones"], ws[:, :], start=True, stop=True).then_inc(w_total, 1)
            pe.wait_ge(w_ready, 2)
            pe.wait_ge(ident_ready, 1)
            start = Turn(0, 0)
            first_product(start, first=True)
            first_product(start.plus(1))
            first_product(start.plus(2))
            with pe.Fori(0, TURNS // 2) as i:
                for s in range(2):
                    b = Turn(i, s)
                    second_product(b)
                    first_product(b.plus(3))

        @block.vector
        def _(dve):
            FRONT = 2 * Norm.STEPS + 3 + 1 + 3 + 1
            NORM2 = 2 + RSQRT_STEPS
            QUANT = 1 + 3 + 1

            def quantize(steps, amax, inv, back, scale):
                steps.link(dve.tensor_scalar(amax, amax, FLOOR, None, ALU.max))
                steps.link(dve.reciprocal(inv, amax))
                dve.tensor_scalar(back, amax, 1.0 / 127.0, scale, ALU.mult, ALU.mult)
                steps.link(dve.tensor_scalar(inv, inv, 127.0, None, ALU.mult))

            def front(b, first=False):
                steps = Steps(dve, front_step, b.n * FRONT, FRONT)
                norm.statistics(dve, steps, lambda j: sh.x[:, b.n * G + j, :])
                for j in range(G):
                    last = norm.apply(dve, xn[:, j, :], sh.x[:, b.n * G + j, :], j)
                last.then_inc(norm_ready, 1)
                dve.wait_ge(norm_ready, b.n + 1)
                again.statistics(dve, steps, lambda j: xn[:, j, :])
                for j in range(G):
                    last = again.apply(dve, xn[:, j, :], xn[:, j, :], j)
                steps.link(last)
                wide = lambda a: a.unsqueeze(1).broadcast_to([P, G, D])
                steps.link(dve.tensor_tensor(xn[:, :, :], xn[:, :, :], wide(w["g1"]), ALU.mult))
                steps.link(dve.tensor_tensor(xn[:, :, :], xn[:, :, :], wide(w["c1"]), ALU.add))
                steps.link(dve.tensor_reduce(amax[:, :], xn[:, :, :], AX.X, ALU.max, apply_absolute_value=True))
                if not first:
                    dve.wait_ge(hid_scaled, b.n * G - G)
                quantize(steps, amax[:, :], inv[:, :], back[:, b.slot, :], ws[:, 0:1])
                for j in range(G):
                    last = dve.tensor_scalar(xn[:, j, :], xn[:, j, :], inv[:, j:j + 1], ROUND, ALU.mult, ALU.add)
                steps.link(last)
                if not first or b.n == 1:
                    dve.wait_ge(x_turned, b.n)
                dve.tensor_scalar(xq[:, :, :], xn[:, :, :], -ROUND, 127.0, ALU.add, ALU.min).then_inc(quantized, 1)
                steps.close()

            def hidden_statistics(b, first=False):
                steps = Steps(dve, norm2_step, b.n * NORM2, NORM2)
                dve.wait_ge(hid_act, (b.n + 1) * G)
                for j in range(G):
                    dve.bn_stats(stats2[:, j, 0, :], h[:, b.slot, j, 0:BANK])
                    last = dve.bn_stats(stats2[:, j, 1, :], h[:, b.slot, j, BANK:F])
                steps.link(last)
                if not first:
                    dve.wait_ge(normalized, b.n * G)
                detach_wait(dve)
                for j in range(G):
                    last = dve.bn_aggr(mv2[:, j, :], stats2[:, j, :, :])
                steps.link(last)
                rsqrt(dve, steps, mv2[:, :, 1], half2[:, :], root2[:, :], tmp2[:, :], LN_EPS)
                dve.scalar_tensor_tensor(out=shift2[:, :], in0=mv2[:, :, 0], scalar=-1.0, in1=root2[:, :], op0=ALU.mult,
                                         op1=ALU.mult).then_inc(shifted, 1)
                steps.close()

            def round_hidden(b):
                steps = Steps(dve, quant_step, b.n * QUANT, QUANT)
                dve.wait_ge(affine, (b.n + 1) * G)
                hb = hn[:, b.slot, :, :]
                steps.link(dve.tensor_reduce(amax2[:, :], hb, AX.X, ALU.max, apply_absolute_value=True))
                quantize(steps, amax2[:, :], inv2[:, :], back2[:, :], ws[:, 1:2])
                for j in range(G):
                    last = dve.tensor_scalar(hb[:, j, :], hb[:, j, :], inv2[:, j:j + 1], ROUND, ALU.mult, ALU.add)
                steps.link(last)
                for j in range(G):
                    dve.tensor_scalar(hq[:, j, :], hb[:, j, :], -ROUND, 127.0, ALU.add, ALU.min).then_inc(hq_ready, 1)
                steps.close()

            def add_out(b):
                dve.wait_ge(out_ready, (b.n + 1) * G)
                dve.wait_ge(bias_added, (b.n + 1) * G)
                for j in range(G):
                    dve.scalar_tensor_tensor(out=sh.x[:, b.n * G + j, :], in0=Y[:, j, 0:D], scalar=back2[:, j:j + 1],
                                             in1=sh.x[:, b.n * G + j, :], op0=ALU.mult, op1=ALU.add).then_inc(out_added, 1)

            sh.wait_params(dve, phase)
            for n, part in enumerate(("w1", "w2")):
                dve.tensor_reduce(ws[:, n:n + 1], w[part].rearrange("p a b -> p (a b)"), AX.X, ALU.add,
                                  apply_absolute_value=True).then_inc(w_summed, 1)
            dve.wait_ge(w_total, 1)
            prep = Steps(dve, prep_step, 0, 6)
            prep.link(dve.tensor_scalar(ws[:, :], Y[:, 0, 0:2], 1.0 / (D * F), FLOOR, ALU.mult, ALU.max))
            prep.link(dve.reciprocal(wi[:, :], ws[:, :]))
            for n, (part, out) in enumerate((("w1", wq1), ("w2", wq2))):
                prep.link(dve.tensor_scalar(w[part], w[part], wi[:, n:n + 1], ROUND, ALU.mult, ALU.add))
                prep.link(dve.tensor_scalar(w[part], w[part], -ROUND, 1.0, ALU.add, ALU.min))
                dve.tensor_scalar(out[:, :, :], w[part], -1.0, None, ALU.max).then_inc(w_ready, 1)
            prep.close()
            start = Turn(0, 0)
            front(start, first=True)
            front(start.plus(1), first=True)
            hidden_statistics(start, first=True)
            front(start.plus(2))
            with dve.Fori(0, TURNS // 2) as i:
                for s in range(2):
                    b = Turn(i, s)
                    hidden_statistics(b.plus(1))
                    round_hidden(b)
                    front(b.plus(3))
                    add_out(b)
                    dve.wait_ge(out_added, (b.n + 1) * G)


PHASES = ["L0x", "L0f", "L1x", "L1f", "L2x", "L2f", "L3x", "L3f"]


def build(nc, dram, phases=PHASES):
    with ExitStack() as ctx:
        sh = Shared(nc, ctx, dram)
        first_loads(nc, sh, phases)
        for n, phase in enumerate(phases):
            following = phases[n + 1] if n + 1 < len(phases) else None
            if phase in ("L0x", "L3x"):
                attention_phase(nc, sh, phase, 16, following)
            elif phase == "L2x":
                attention_phase(nc, sh, phase, 64, following)
            elif phase == "L0f":
                head_experts_phase(nc, sh, phase, following)
            elif phase == "L1x":
                performer_phase(nc, sh, phase, following)
            elif phase == "L2f":
                quantized_phase(nc, sh, phase, following)
            else:
                experts_phase(nc, sh, phase, following)
        last_stores(nc, sh)


def _rows(a, rows=P):
    return a.reshape(-1, rows, a.shape[-1]).transpose(1, 0, 2).reshape(rows, -1)


def _cols(a):
    return a.reshape(-1, P).T


def _wide(a):
    return np.broadcast_to(a.reshape(1, -1), (P, a.size))


def _constants():
    f = np.float32
    p, q = np.arange(P)[:, None], np.arange(P)[None, :]
    out = {
        "ident": (p == q), "pick8": 0.25 * (p // 16 == np.arange(8)), "pick2": 0.125 * (p // 64 == np.arange(2)),
        "feat2": 0.125 * (p // 64 == np.arange(2)), "causal": (p <= q),
        "half": -0.5 * np.concatenate([(p // 32 == s) & ((p % 32) // 16 == q // 64) for s in range(4)], 1),
        "headsum": -0.5 * (p // 16 == np.arange(8)),
        "iota8": np.broadcast_to(np.arange(8), (P, 8)), "iota16": np.broadcast_to(np.arange(16), (P, 16)),
        "ones": np.ones((P, P)),
    }
    return np.concatenate([out[n].astype(f) for n, _ in PARTS["const"]], 1)


def _pack(i):
    z = np.zeros
    f = np.float32

    def attn(k, transposed=False):
        g = lambda n: i[f"{k}_{n}"].T if transposed and n[0] == "W" else i[f"{k}_{n}"]
        return {"wq": _rows(g("Wq")), "wk": _rows(g("Wk")), "wv": _rows(g("Wv")), "wo": _rows(g("Wo")),
                "bq": _cols(g("bq")), "bk": _cols(g("bk")), "bv": _wide(g("bv")), "bo": _wide(g("bo"))}

    def padded(a, n):
        out = z((a.shape[0], n), f)
        out[:, :a.shape[1]] = a
        return out

    rf = z((P, 4, P), f)
    for s in range(4):
        for a in range(2):
            rf[32 * s + 16 * a:32 * s + 16 * a + 16, s, 64 * a:64 * a + 64] = i["L1_xattn_random_features"]
    emb = z((P, 2, 8, 16), f)
    b2 = z((8, 16, 2, 4, 32), f)
    for h in range(8):
        emb[32 * (h % 4):32 * (h % 4) + 32, h // 4, h, :] = i["L0_ffn_expert_emb"]
        b2[h, :, h // 4, h % 4, :] = i["L0_ffn_b2"]
    parts = {
        "L0x": attn("L0_xattn"),
        "L0f": {"wm": _rows(i["L0_ffn_Wm"]), "wo": _rows(i["L0_ffn_Wo"]), "emb": emb.reshape(P, -1),
                "w1": np.tile(i["L0_ffn_W1"].transpose(1, 0, 2).reshape(32, -1), (4, 1)),
                "w2": i["L0_ffn_W2"].transpose(1, 0, 2).reshape(P, -1), "b2": b2.reshape(P, -1),
                "b1": i["L0_ffn_b1"].T, "bm": _cols(i["L0_ffn_bm"]), "bo": _wide(i["L0_ffn_bo"])},
        "L1x": attn("L1_xattn") | {"rf": rf.reshape(P, -1)},
        "L1f": {"w1": i["L1_ffn_W1"].reshape(8, 2, P, 512).transpose(2, 0, 1, 3).reshape(P, -1),
                "w2": i["L1_ffn_W2"].reshape(8, 4, P, D).transpose(2, 0, 1, 3).reshape(P, -1),
                "wg": _rows(padded(i["L1_ffn_Wg"], P)), "bg": _wide(i["L1_ffn_bg"]),
                "b1": i["L1_ffn_b1"].reshape(8, 4, P).transpose(2, 0, 1).reshape(P, -1), "b2": _wide(i["L1_ffn_b2"]),
                "gamma": _wide(i["L1_ffn_gamma"]), "beta": _wide(i["L1_ffn_beta"])},
        "L2x": {"wq": _rows(i["L2_xattn_Wq"]), "wk": _rows(i["L2_xattn_Wk"]), "wv": _rows(i["L2_xattn_Wv"]),
                "wo": _rows(i["L2_xattn_Wo"])},
        "L2f": {"w1": _rows(i["L2_ffn_w1"].T), "w2": _rows(i["L2_ffn_w2"].T), "g1": _wide(i["L2_ffn_ln1_g"]),
                "c1": _wide(i["L2_ffn_ln1_b"]), "b1": _wide(i["L2_ffn_b1"]), "g2": _wide(i["L2_ffn_ln2_g"]),
                "c2": _wide(i["L2_ffn_ln2_b"]), "b2": _wide(i["L2_ffn_b2"])},
        "L3x": attn("L3_xattn", True) | {"mask": i["fside_SxS2_0"]},
        "L3f": {"w1": i["L3_ffn_w1"].transpose(0, 2, 1).reshape(8, 2, P, 512).transpose(2, 0, 1, 3).reshape(P, -1),
                "w2": i["L3_ffn_w2"].transpose(0, 2, 1).reshape(8, 2, P, D).transpose(2, 0, 1, 3).reshape(P, -1),
                "wg": _rows(padded(i["L3_ffn_Wg"].T, P)), "bg": _wide(i["L3_ffn_bg"])},
    }
    return {f"p_{ph}": np.ascontiguousarray(np.concatenate([parts[ph][n] for n, _ in PARTS[ph]], 1)) for ph in parts}


def _arrays(i):
    i = {k: np.asarray(v) for k, v in i.items()}
    arrays = {"x": i["x"], "side": np.ascontiguousarray(i["fside_Bx16xSxS2_0"].transpose(2, 0, 1, 3).reshape(P, BATCH * HEADS, P)),
              "pad": i["mask_BxS2_bf0"].view(np.int32),
              "ctxT": np.ascontiguousarray(i["ctx_1024"].reshape(BATCH * P, KT, P).transpose(2, 1, 0)),
              "p_const": _constants()}
    arrays.update(_pack(i))
    return arrays


def _declare(nc, arrays):
    types = {"float32": F32, "int32": I32}
    dram = {n: nc.dram_tensor(f"{n}_dram", list(a.shape), types[str(a.dtype)], kind="ExternalInput").ap()
            for n, a in arrays.items()}
    dram["out"] = nc.dram_tensor("out_dram", [BATCH, P, D], F32, kind="ExternalOutput").ap()
    dram["gates"] = nc.dram_tensor("gates_dram", [9, P, 512], F32, kind="Internal").ap()
    return dram


def kernel(**inputs):
    from concourse import bacc
    from concourse.bass_utils import run_bass_kernel_spmd

    nc = bacc.Bacc("TRN2", target_bir_lowering=False, num_devices=1)
    arrays = _arrays(inputs)
    build(nc, _declare(nc, arrays))
    r = run_bass_kernel_spmd(nc, [{f"{n}_dram": a for n, a in arrays.items()}], core_ids=[0])
    return r.results[0]["out_dram"]
```

```python
from contextlib import ExitStack

import numpy as np

import concourse.bass as bass
from concourse import mybir

ALU = mybir.AluOpType
ACT = mybir.ActivationFunctionType
AX = mybir.AxisListType
F32 = mybir.dt.float32
F16 = mybir.dt.float16
BF16 = mybir.dt.bfloat16
I32 = mybir.dt.int32
U8 = mybir.dt.uint8

P = 128
BATCH = 32
D = 256
KT = D // P
HEADS = 16
BANK = 512
SPARE = 6
LN_EPS = 1e-5
RSQRT_SEED = float(0x5F3759DF)
ROUND = 1.5 * 2.0 ** 23
NEVER = 1e30
SLOT_TILES = 2 * BATCH + 8
TILES_AHEAD = 4


def detach_wait(eng):
    eng.nop(nofuse=True)


class Steps:

    def __init__(self, eng, sem, start, per_turn=None):
        self.eng, self.sem, self.start, self.n, self.per_turn = eng, sem, start, 0, per_turn

    def link(self, instruction):
        self.n += 1
        instruction.then_inc(self.sem, 1)
        self.eng.wait_ge(self.sem, self.start + self.n)

    def close(self):
        assert self.n == self.per_turn, f"{self.n} linked steps, {self.per_turn} declared"


def rsqrt(dve, steps, var, half, root, tmp, eps):
    rsqrt_seed(dve, steps, var, half, root, eps)
    rsqrt_rounds(dve, steps, var, root, tmp, 3)


def rsqrt_seed(dve, steps, var, half, root, eps):
    steps.link(dve.tensor_scalar(var, var, eps, None, ALU.add))
    steps.link(dve.tensor_scalar(half, var.bitcast(I32), 1, None, ALU.logical_shift_right))
    steps.link(dve.tensor_scalar(root.bitcast(I32), half, -1.0, RSQRT_SEED, ALU.mult, ALU.add))


def rsqrt_rounds(dve, steps, var, root, tmp, rounds):
    for _ in range(rounds):
        steps.link(dve.scalar_tensor_tensor(out=tmp, in0=root, scalar=-0.5, in1=root, op0=ALU.mult, op1=ALU.mult))
        steps.link(dve.tensor_tensor(tmp, tmp, var, ALU.mult))
        steps.link(dve.scalar_tensor_tensor(out=root, in0=tmp, scalar=1.5, in1=root, op0=ALU.add, op1=ALU.mult))


RSQRT_STEPS = 12


class Norm:

    STEPS = 2 + RSQRT_STEPS

    def __init__(self, core, group, name="ln"):
        self.group = group
        self.stats = core.sb(name + "_stats", [P, group, 6])
        self.mean_var = core.sb(name + "_mean_var", [P, group, 2])
        self.half = core.sb(name + "_half", [P, group], I32)
        self.root = core.sb(name + "_root", [P, group])
        self.tmp = core.sb(name + "_tmp", [P, group])

    def statistics(self, dve, steps, source):
        self.moments(dve, steps, source)
        rsqrt(dve, steps, self.mean_var[:, :, 1], self.half[:, :], self.root[:, :], self.tmp[:, :], LN_EPS)

    def part(self, dve, steps, source, n):
        if n == 0:
            self.moments(dve, steps, source)
        elif n == 1:
            rsqrt_seed(dve, steps, self.mean_var[:, :, 1], self.half[:, :], self.root[:, :], LN_EPS)
            rsqrt_rounds(dve, steps, self.mean_var[:, :, 1], self.root[:, :], self.tmp[:, :], 1)
        else:
            rsqrt_rounds(dve, steps, self.mean_var[:, :, 1], self.root[:, :], self.tmp[:, :], 2)

    PART_STARTS = (0, 2, 8)

    def moments(self, dve, steps, source):
        for j in range(self.group - 1):
            dve.bn_stats(self.stats[:, j, :], source(j))
        steps.link(dve.bn_stats(self.stats[:, self.group - 1, :], source(self.group - 1)))
        detach_wait(dve)
        for j in range(self.group - 1):
            dve.bn_aggr(self.mean_var[:, j, :], self.stats[:, j, :])
        steps.link(dve.bn_aggr(self.mean_var[:, self.group - 1, :], self.stats[:, self.group - 1, :]))

    def apply(self, dve, out, source, j):
        return dve.tensor_scalar(out, source, self.mean_var[:, j, 0:1], self.root[:, j:j + 1],
                                 ALU.subtract, ALU.mult)


class Core:

    def __init__(self, nc, ctx, phase):
        self.nc, self.ctx, self.phase, self.sems = nc, ctx, phase, []
        ctx.callback(self.free_semaphores)

    def free_semaphores(self):
        self.nc.clear_and_free_semaphores(self.sems)
        self.nc.all_engine_barrier()

    def sb(self, name, shape, dt=F32):
        return self.ctx.enter_context(self.nc.sbuf_tensor(f"{self.phase}_{name}", shape, dt))

    def ps(self, name, shape, dt=F32):
        return self.ctx.enter_context(self.nc.psum_tensor(f"{self.phase}_{name}", shape, dt))

    def sem(self, name):
        self.sems.append(self.nc.alloc_semaphore(f"{self.phase}_{name}"))
        return self.sems[-1]


ATTN16 = [("wq", (KT, D)), ("wk", (KT, D)), ("wv", (KT, D)), ("wo", (KT, D)),
          ("bq", (2,)), ("bk", (2,)), ("bv", (D,)), ("bo", (D,))]
W64 = HEADS * 64
PARTS = {
    "L0x": ATTN16,
    "L0f": [("wm", (KT, D)), ("wo", (KT, D)), ("emb", (KT, P)), ("w1", (16, P)), ("w2", (16, 32)), ("b2", (KT, P)),
            ("b1", (16,)), ("bm", (KT,)), ("bo", (D,))],
    "L1x": ATTN16 + [("rf", (4, P))],
    "L1f": [("w1", (8, KT, 512)), ("w2", (8, 4, D)), ("wg", (KT, P)), ("bg", (8,)), ("b1", (8, 4)), ("b2", (8, D)),
            ("gamma", (D,)), ("beta", (D,))],
    "L2x": [("wq", (KT, W64)), ("wk", (KT, W64)), ("wv", (KT, W64)), ("wo", (8, D))],
    "L2f": [("w1", (KT, 1024)), ("w2", (8, D)), ("g1", (D,)), ("c1", (D,)), ("b1", (1024,)), ("g2", (1024,)),
            ("c2", (1024,)), ("b2", (D,))],
    "L3x": ATTN16 + [("mask", (P,))],
    "L3f": [("w1", (8, KT, 512)), ("w2", (8, 2, D)), ("wg", (KT, P)), ("bg", (8,))],
    "const": [("ident", (P,)), ("pick8", (8,)), ("pick2", (2,)), ("feat2", (2,)), ("causal", (P,)), ("half", (4, P)),
              ("headsum", (8,)), ("iota8", (8,)), ("iota16", (16,)), ("ones", (P,)), ("tiles", (SLOT_TILES + TILES_AHEAD,))],
}
SIDE = {"L0x": 1, "L1x": 1, "L2x": 1, "L3x": 1, "L0f": 0, "L1f": 0, "L2f": 0, "L3f": 0}


def columns(phase):
    return sum(int(np.prod(shape)) for _, shape in PARTS[phase])


def views(store, phase):
    out, at = {}, 0
    for name, shape in PARTS[phase]:
        n = int(np.prod(shape))
        v = store[:, at:at + n]
        if len(shape) == 2:
            v = v.rearrange("p (a b) -> p a b", a=shape[0])
        if len(shape) == 3:
            v = v.rearrange("p (a b c) -> p a b c", a=shape[0], b=shape[1])
        out[name] = v
        at += n
    return out


class Shared:

    def __init__(self, nc, ctx, dram):
        self.nc, self.dram = nc, dram
        self.x = ctx.enter_context(nc.sbuf_tensor("x_sb", [P, BATCH + SPARE, D], F32))
        self.const_store = ctx.enter_context(nc.sbuf_tensor("const_sb", [P, columns("const")], F32))
        self.stores = [ctx.enter_context(nc.sbuf_tensor(f"params{s}", [P, max(columns(p) for p in SIDE if SIDE[p] == s)], F32))
                       for s in range(2)]
        self.kstab = ctx.enter_context(nc.sbuf_tensor("neg_kstab", [P, 1], F32))
        self.const = views(self.const_store, "const")
        self.loaded = {p: nc.alloc_semaphore(f"params_{p}") for p in SIDE}
        self.loads = {}
        self.x_loaded = nc.alloc_semaphore("x_loaded")
        self.const_loaded = nc.alloc_semaphore("const_loaded")

    def params(self, phase):
        return views(self.stores[SIDE[phase]], phase)

    def scratch(self, following, columns_before, shape):
        at = columns(following) + columns_before
        n = int(np.prod(shape))
        v = self.stores[SIDE[following]][:, at:at + n]
        if len(shape) == 2:
            return v.rearrange("p (a b) -> p a b", a=shape[0])
        return v.rearrange("p (a b c) -> p a b c", a=shape[0], b=shape[1])

    def load_params(self, sp, phase):
        n, step, self.loads[phase] = columns(phase), 4096, 0
        for at in range(0, n, step):
            to = min(at + step, n)
            sp.dma_start(self.stores[SIDE[phase]][:, at:to], self.dram["p_" + phase][:, at:to]).then_inc(self.loaded[phase], 16)
            self.loads[phase] += 16

    def wait_params(self, eng, phase):
        eng.wait_ge(self.loaded[phase], self.loads[phase])


def first_loads(nc, sh, phases):
    spare_set = nc.alloc_semaphore("spare_set")
    with nc.Block() as block:
        @block.gpsimd
        def _(pool):
            pool.memset(sh.x[:, BATCH:, :], 0.0).then_inc(spare_set, 1)
            pool.wait_ge(spare_set, 1)

        @block.sync
        def _(sp):
            sp.dma_start(sh.const_store[:, :], sh.dram["p_const"]).then_inc(sh.const_loaded, 16)
            sh.load_params(sp, phases[0])
            for q in range(4):
                b = BATCH // 4
                sp.dma_start(sh.x[:, q * b:(q + 1) * b, :],
                             sh.dram["x"][q * b:(q + 1) * b].rearrange("b s d -> s b d")).then_inc(sh.x_loaded, 16)
            sp.wait_ge(sh.const_loaded, 16)
            sp.wait_ge(sh.x_loaded, 64)


def last_stores(nc, sh):
    stored = nc.alloc_semaphore("out_stored")
    with nc.Block() as block:
        @block.sync
        def _(sp):
            for q in range(4):
                b = BATCH // 4
                sp.dma_start(sh.dram["out"][q * b:(q + 1) * b].rearrange("b s d -> s b d"),
                             sh.x[:, q * b:(q + 1) * b, :]).then_inc(stored, 16)
            sp.wait_ge(stored, 64)


class Turn:

    def __init__(self, i, k, per=2):
        self.i, self.k, self.per = i, k, per
        self.n, self.slot, self.round = i * per + k, k % 2, i * (per // 2) + k // 2

    def plus(self, k):
        return Turn(self.i, self.k + k, self.per)


class Bank:

    def __init__(self, core, number, before, turn):
        self.before, self.turn = before, turn
        self.filled, self.emptied = core.sem(f"bank{number}_filled"), core.sem(f"bank{number}_emptied")

    def uses_before(self, name, b):
        if isinstance(b.n, int) and (name, b.n) in self.before:
            return self.before.index((name, b.n))
        place = [n for n, _ in self.turn].index(name)
        return (b.n - self.turn[place][1]) * len(self.turn) + (len(self.before) + place)


class Banks:

    def __init__(self, core, psum, tables):
        self.psum = psum
        self.banks = [Bank(core, k, before, turn) for k, (before, turn) in enumerate(tables)]

    def find(self, name):
        return next(k for k, bank in enumerate(self.banks) if name in [n for n, _ in bank.turn])

    def open(self, eng):
        for bank in self.banks:
            eng.sem_inc(bank.emptied, 1)

    def at(self, name):
        return self.psum[:, self.find(name), :]

    def filled(self, name):
        return self.banks[self.find(name)].filled

    def emptied(self, name):
        return self.banks[self.find(name)].emptied

    def until_free(self, name, b):
        return self.banks[self.find(name)].uses_before(name, b) + 1

    def until_filled(self, name, b):
        return self.banks[self.find(name)].uses_before(name, b) + 1

    def until_emptied(self, name, b):
        return self.banks[self.find(name)].uses_before(name, b) + 2


FOLLOWING = {"L2x": "L2f", "L3x": "L3f"}


def attention_phase(nc, sh, phase, dh, next_phase):
    W = HEADS * dh
    NT = W // P
    VAR = P // dh
    UH = 4
    U = HEADS // UH
    small = dh == 16
    HW = dh + 1 if small else dh
    VW = HEADS * HW + (P - HW if small else 0)
    HO = HEADS if small else UH
    biased = small
    masked = phase == "L3x"
    BY_ACT = VAR // 2 if masked else 0
    LEAD, SR, PR, OR = (3, 4, 1, 1) if small else (2, 2, 2, 2)
    w, c = sh.params(phase), sh.const
    pick = c["pick8"] if small else c["pick2"]
    if small:
        BT = 2
        tables = [([("xT", 0), ("v0", 0), ("xT", 1)], [("v0", 1), ("xT", 2), ("proj", 0)]),
                  ([("k0", 0), ("q0", 0), ("k0", 1), ("q0", 1)], [("k0", 2), ("outT0", 0), ("q0", 2)])]
    else:
        BT = 4
        tables = [([("xT", 0), ("k0", 0), ("k1", 0), ("xT", 1), ("v1", 0)], [("k0", 1), ("k1", 1), ("xT", 2), ("v1", 1)]),
                  ([("q0", 0), ("q1", 0), ("v0", 0)], [("q0", 1), ("q1", 1), ("v0", 1), ("proj", 0)])]
    NB = NT // BT

    with ExitStack() as ctx:
        core = Core(nc, ctx, phase)
        norm = Norm(core, 2)
        xn = core.sb("xn", [P, 2, D])
        xnT = core.sb("xnT", [P, KT, P])
        cT = core.sb("ctxT", [P, 2, KT, P])
        qT = core.sb("qT", [P, 2, NT, P])
        kT = core.sb("kT", [P, NT, P])
        if small:
            km = core.sb("k_masked", [P, 2, VAR, NT, P])
            kms = [km[:, s, :, :, :] for s in range(2)]
        else:
            kms = [sh.scratch(FOLLOWING[phase], s * VAR * NT * P, (VAR, NT, P)) for s in range(2)]
        v = core.sb("v_ones", [P, 2, VW])
        d = core.sb("centered", [P, SR, UH, P])
        p = core.sb("probs", [P, 2, UH, P])
        pT = core.sb("probsT", [P, 2, UH, P])
        mx = core.sb("row_max", [P, SR, UH])
        rc = core.sb("recip_den", [P, 2, HO])
        o = core.sb("heads_out", [P, W]) if small else None
        oT = core.sb("heads_outT", [P, NT, P])
        if masked:
            sides = [sh.scratch(FOLLOWING[phase], s * HEADS * P, (HEADS, P)) for s in range(2)]
            pad_words = core.sb("pad", [P, BATCH + 1, P // 4], I32)
            pad = pad_words[:, :, :].bitcast(U8)
            half_causal = core.sb("half_causal", [P, P])
            half_mask = core.sb("half_mask", [P, P])
            sm = core.sb("side_mask", [P, SR, UH, P])
        S = core.ps("S", [P, SR, UH, P])
        PT = core.ps("PT", [P, PR, UH, P])
        O = core.ps("O", [P, OR, BANK])
        gen = core.ps("gen", [P, 2, BANK])
        banks = Banks(core, gen, tables)

        ctx_loaded = [core.sem(f"ctx{s}_loaded") for s in range(2)]
        side_loaded = [core.sem(f"side{s}_loaded") for s in range(2)]
        km_act = core.sem("k_masked_act")
        divided, sum_step = core.sem("probs_divided"), core.sem("row_sums")
        (xn_ready, bias_added, km_ready, v_set, scored, centered, exped, turned, turned_out, summed, normed, norm_step,
         max_step, recip_step, side_used, side_ready, pad_set, pad_loaded, mask_step) = (core.sem(s) for s in (
            "xn_ready", "bias_added", "k_masked_ready", "v_ones_set", "scored", "centered", "exped", "probs_turned",
            "probsT_ready", "heads_summed", "heads_normed", "norm_step", "max_step", "recip_step", "side_mask_used",
            "side_mask_ready", "pad_set", "pad_loaded", "mask_step"))
        block = ctx.enter_context(nc.Block())

        def unit(b, u):
            return b.n * U + u

        @block.sync
        def _(sp):
            def load_ctx(b, source):
                sp.dma_start(cT[:, b.slot, :, :], sh.dram["ctxT"][:, :, bass.ts(source, P)]).then_inc(ctx_loaded[b.slot], 16)

            def load_side(b, source):
                sp.dma_start(sides[b.slot], sh.dram["side"][:, bass.ts(source, HEADS), :]).then_inc(side_loaded[b.slot], 16)

            for k in range(2):
                load_ctx(Turn(0, k), k)
                if masked:
                    load_side(Turn(0, k), k)
            if next_phase:
                sh.load_params(sp, next_phase)

            def following(b, source):
                last = f"v{NB - 1}"
                sp.wait_ge(banks.emptied(last), banks.until_emptied(last, b))
                load_ctx(b.plus(2), source)
                if masked and not (isinstance(b.n, int) and b.n > BATCH - 2):
                    sp.wait_ge(side_ready, unit(b, U))
                    load_side(b.plus(2), source)

            following(Turn(0, 0), 2)
            with sp.Fori(0, BATCH // 2 - 2) as i:
                for s in range(1, 3):
                    b = Turn(i, s)
                    following(b, b.n + 2)
            following(Turn(0, BATCH - 3), BATCH - 1)
            following(Turn(0, BATCH - 2), 0)
            if small:
                following(Turn(0, BATCH - 1), 0)

        @block.gpsimd
        def _(pool):
            def bias(b):
                pool.wait_ge(xn_ready, b.n + 1)
                pool.tensor_tensor(sh.x[:, b.n, :], sh.x[:, b.n, :], w["bo"], ALU.add).then_inc(bias_added, 1)

            def mask_keys(b, k):
                pool.wait_ge(banks.emptied(f"k{k}"), banks.until_emptied(f"k{k}", b))
                detach_wait(pool)
                for m in range(BY_ACT, VAR):
                    pool.tensor_scalar(kms[b.slot][:, m, k * BT:(k + 1) * BT, :], kT[:, k * BT:(k + 1) * BT, :], pick[:, m:m + 1], 1.0,
                                       ALU.mult, ALU.mult).then_inc(km_ready, 1)

            def halve_mask(b):
                pool.tensor_copy(half_mask[:, :], pad[:, b.n, :]).then_inc(mask_step, 1)
                pool.wait_ge(mask_step, b.n * 3 + 2)
                detach_wait(pool)
                pool.tensor_scalar(half_mask[:, :], half_mask[:, :], -NEVER, 1.0, ALU.mult, ALU.mult).then_inc(mask_step, 1)
                pool.wait_ge(mask_step, b.n * 3 + 3)
                pool.tensor_tensor(half_mask[:, :], half_mask[:, :], half_causal[:, :], ALU.add).then_inc(mask_step, 1)
                pool.wait_ge(mask_step, b.n * 3 + 4)

            def mask_side(b, u, first=False):
                if u == 0:
                    pool.wait_ge(side_loaded[b.slot], (b.round + 1) * 16)
                if not first:
                    pool.wait_ge(side_used, unit(b, u) - 2)
                pool.tensor_tensor(sm[:, u % SR, :, :], sides[b.slot][:, u * UH:(u + 1) * UH, :],
                                   half_mask[:, :].unsqueeze(1).broadcast_to([P, UH, P]), ALU.add).then_inc(side_ready, 1)

            def divide(b, u):
                pool.wait_ge(recip_step, unit(b, u) + 1)
                pool.tensor_tensor(p[:, u % 2, :, :], p[:, u % 2, :, :], rc[:, u % 2, :].unsqueeze(2).broadcast_to([P, UH, P]),
                                   ALU.mult).then_inc(divided, 1)

            pool.memset(v[:, :, :], 1.0).then_inc(v_set, 1)
            sh.wait_params(pool, phase)
            if masked:
                pool.memset(pad_words[:, BATCH:, :], 0).then_inc(pad_set, 1)
                pool.wait_ge(pad_set, 1)
                pool.dma_start(pad_words[:, 0:BATCH, :], sh.dram["pad"].partition_broadcast(P)).then_inc(pad_loaded, 16)
                pool.tensor_scalar(half_causal[:, :], w["mask"], 0.5, 1.0, ALU.mult, ALU.mult).then_inc(mask_step, 1)
                pool.wait_ge(mask_step, 1)
                pool.wait_ge(pad_loaded, 16)
            start = Turn(0, 0)
            if biased:
                bias(start)
            for k in range(NB):
                mask_keys(start, k)
            if small:
                mask_keys(start.plus(1), 0)
            if masked:
                halve_mask(start)
                mask_side(start, 0, first=True)
                mask_side(start, 1, first=True)
                mask_side(start, 2, first=True)
            if not small:
                divide(start, 0)
            with pool.Fori(0, BATCH // 2) as i:
                for s in range(2):
                    b = Turn(i, s)
                    if not small:
                        for u in range(U):
                            divide(b.plus((u + 1) // U), (u + 1) % U)
                            if u < NB:
                                mask_keys(b.plus(1), u)
                        continue
                    if masked:
                        mask_side(b, 3)
                        pool.wait_ge(side_ready, unit(b, U))
                        halve_mask(b.plus(1))
                        for u in range(3):
                            mask_side(b.plus(1), u)
                    mask_keys(b.plus(2), 0)
                    if biased:
                        bias(b.plus(1))

        @block.scalar
        def _(act):
            def empty_projection(b, name, k):
                dst = kT[:, k * BT:(k + 1) * BT, :] if name == "k" else qT[:, b.slot, k * BT:(k + 1) * BT, :]
                chunk = f"{name}{k}"
                act.wait_ge(banks.filled(chunk), banks.until_filled(chunk, b))
                src = banks.at(chunk)[:, 0:BT * P].rearrange("p (a b) -> p a b", a=BT)
                if biased:
                    for t in range(BT):
                        last = act.activation(dst[:, t, :], src[:, t, :], ACT.Identity, bias=w["b" + name][:, t:t + 1])
                else:
                    last = act.activation(dst, src, ACT.Copy)
                last.then_inc(banks.emptied(chunk), 1)

            def mask_keys(b):
                act.wait_ge(banks.emptied("k0"), banks.until_emptied("k0", b))
                for m in range(BY_ACT):
                    act.activation(kms[b.slot][:, m, :, :], kT[:, :, :], ACT.Copy, scale=pick[:, m:m + 1]).then_inc(km_act, 1)

            def exponentiate(b, u):
                n = unit(b, u)
                act.wait_ge(centered, n + 1)
                act.activation(p[:, u % 2, :, :], d[:, u % SR, :, :], ACT.Exp).then_inc(exped, 1)

            def empty_probs(b, u):
                n = unit(b, u)
                act.wait_ge(turned, n + 1)
                act.activation(pT[:, u % 2, :, :], PT[:, u % PR, :, :], ACT.Copy).then_inc(turned_out, 1)

            def empty_summed(b, k):
                act.wait_ge(summed, b.n * U + (k + 1) * U // NB)
                act.activation(oT[:, k * BT:(k + 1) * BT, :], O[:, k, :].rearrange("p (a b) -> p a b", a=BT), ACT.Copy).then_inc(normed, 1)

            def empty_outputs(b, k):
                chunk = f"outT{k}"
                act.wait_ge(banks.filled(chunk), banks.until_filled(chunk, b))
                act.activation(oT[:, k * BT:(k + 1) * BT, :], banks.at(chunk)[:, 0:BT * P].rearrange("p (a b) -> p a b", a=BT),
                               ACT.Copy).then_inc(banks.emptied(chunk), 1)

            sh.wait_params(act, phase)
            start = Turn(0, 0)
            for k in range(NB):
                empty_projection(start, "k", k)
                empty_projection(start, "q", k)
            if small:
                if BY_ACT:
                    mask_keys(start)
                    act.wait_ge(km_act, BY_ACT)
                act.wait_ge(km_ready, VAR - BY_ACT)
                empty_projection(start.plus(1), "k", 0)
                empty_projection(start.plus(1), "q", 0)
                if BY_ACT:
                    mask_keys(start.plus(1))
            exponentiate(start, 0)
            exponentiate(start, 1)
            empty_probs(start, 0)
            with act.Fori(0, BATCH // 2) as i:
                for s in range(2):
                    b = Turn(i, s)
                    for u in range(U):
                        if not small:
                            if u < NB:
                                empty_projection(b.plus(1), "k", u)
                            exponentiate(b.plus((u + 2) // U), (u + 2) % U)
                            if u < NB:
                                empty_projection(b.plus(1), "q", u)
                            if u % 2 == 1:
                                empty_summed(b, u // 2)
                            empty_probs(b.plus((u + 1) // U), (u + 1) % U)
                            continue
                        empty_probs(b.plus((u + 1) // U), (u + 1) % U)
                        exponentiate(b.plus((u + 2) // U), (u + 2) % U)
                        if u == U - 1:
                            empty_projection(b.plus(2), "k", 0)
                            empty_outputs(b, 0)
                            empty_projection(b.plus(2), "q", 0)
                            if BY_ACT:
                                mask_keys(b.plus(2))

        @block.tensor
        def _(pe):
            def turn_rows(b):
                pe.wait_ge(xn_ready, b.n + 1)
                pe.wait_ge(banks.emptied("xT"), banks.until_free("xT", b))
                for k in range(KT):
                    mm = pe.transpose(banks.at("xT")[:, k * P:(k + 1) * P], xn[:, b.slot, k * P:(k + 1) * P], c["ident"])
                mm.then_inc(banks.filled("xT"), 1)

            def project(b, name, n):
                chunk = f"{name}{n}"
                pe.wait_ge(banks.emptied(chunk), banks.until_free(chunk, b))
                if name == "q":
                    pe.wait_ge(banks.emptied("xT"), banks.until_emptied("xT", b))
                elif name == "k":
                    pe.wait_ge(ctx_loaded[b.slot], (b.round + 1) * 16)
                if name == "v":
                    for k in range(KT):
                        mm = pe.matmul(banks.at(chunk)[:, 0:BT * P], cT[:, b.slot, k, :], w["wv"][:, k, n * BT * P:(n + 1) * BT * P],
                                       start=(k == 0), stop=(k == KT - 1))
                else:
                    for t in range(BT):
                        for k in range(KT):
                            mm = pe.matmul(banks.at(chunk)[:, t * P:(t + 1) * P], w["w" + name][:, k, (n * BT + t) * P:(n * BT + t + 1) * P],
                                           xnT[:, k, :] if name == "q" else cT[:, b.slot, k, :], start=(k == 0), stop=(k == KT - 1))
                mm.then_inc(banks.filled(chunk), 1)

            def score(b, u, first=False):
                n = unit(b, u)
                tiles = range(u * UH // VAR, (u * UH + UH - 1) // VAR + 1)
                chunk = tiles[-1] // BT
                pe.wait_ge(km_ready, b.n * (VAR - BY_ACT) * NB + (chunk + 1) * (VAR - BY_ACT))
                if BY_ACT:
                    pe.wait_ge(km_act, (b.n + 1) * BY_ACT)
                if u == 0 or not small:
                    pe.wait_ge(banks.emptied(f"q{chunk}"), banks.until_emptied(f"q{chunk}", b))
                if not first:
                    pe.wait_ge(centered, n - LEAD + 1)
                n_side = UH // len(tiles)
                for t, tile in enumerate(tiles):
                    m = (u * UH + t * n_side) % VAR
                    mm = pe.matmul(S[:, u % SR, t * n_side:(t + 1) * n_side, :], qT[:, b.slot, tile, :],
                                   kms[b.slot][:, m:m + n_side, tile, :], start=True, stop=True)
                mm.then_inc(scored, 1)

            def turn_probs(b, u, first=False):
                pe.wait_ge(exped if small else divided, unit(b, u) + 1)
                if small and not first:
                    pe.wait_ge(turned_out, unit(b, u))
                for r in range(UH):
                    mm = pe.transpose(PT[:, u % PR, r, :], p[:, u % 2, r, :], c["ident"])
                mm.then_inc(turned, 1)

            def sum_heads(b, u):
                n = unit(b, u)
                if u == 0:
                    for k in range(NB):
                        pe.wait_ge(banks.emptied(f"v{k}"), banks.until_emptied(f"v{k}", b))
                pe.wait_ge(turned_out, n + 1)
                if not small:
                    pe.wait_ge(normed, b.n * NB + u // 2 + 1)
                for r in range(UH):
                    h = u * UH + r
                    if small:
                        mm = pe.matmul(O[:, 0, h * HW:h * HW + P], pT[:, u % 2, r, :], v[:, b.slot, h * HW:h * HW + P],
                                       start=True, stop=True, skip_group_check=True)
                    else:
                        at, tile = (h % VAR) * dh, h // VAR % BT
                        mm = pe.matmul(O[at:at + dh, u // 2, tile * P:(tile + 1) * P], v[:, b.slot, h * HW:(h + 1) * HW],
                                       pT[:, u % 2, r, :], start=True, stop=True, skip_group_check=True)
                if not small or u == U - 1:
                    mm.then_inc(summed, 1)

            def turn_outputs(b, k):
                chunk = f"outT{k}"
                pe.wait_ge(normed, b.n + 1)
                pe.wait_ge(banks.emptied(chunk), banks.until_free(chunk, b))
                for t in range(BT):
                    at = (k * BT + t) * P
                    mm = pe.transpose(banks.at(chunk)[:, t * P:(t + 1) * P], o[:, at:at + P], c["ident"])
                mm.then_inc(banks.filled(chunk), 1)

            def project_out(b):
                pe.wait_ge(banks.emptied("proj"), banks.until_free("proj", b))
                if small:
                    pe.wait_ge(banks.emptied("outT0"), banks.until_emptied("outT0", b))
                else:
                    pe.wait_ge(normed, (b.n + 1) * NB + 2)
                for t in range(NT):
                    mm = pe.matmul(banks.at("proj")[:, 0:D], oT[:, t, :], w["wo"][:, t, :], start=(t == 0), stop=(t == NT - 1))
                mm.then_inc(banks.filled("proj"), 1)

            sh.wait_params(pe, phase)
            start = Turn(0, 0)
            turn_rows(start)
            for k in range(NB):
                project(start, "k", k)
                project(start, "q", k)
            project(start, "v", 0)
            turn_rows(start.plus(1))
            if not small:
                project(start, "v", 1)
            for k in range(NB):
                pe.wait_ge(banks.emptied(f"v{k}"), banks.until_emptied(f"v{k}", start))
            if small:
                project(start.plus(1), "k", 0)
                project(start.plus(1), "q", 0)
                pe.wait_ge(banks.emptied("q0"), banks.until_emptied("q0", start.plus(1)))
            for u in range(LEAD):
                score(start, u, first=True)
            turn_probs(start, 0, first=True)
            with pe.Fori(0, BATCH // 2) as i:
                for s in range(2):
                    b = Turn(i, s)
                    for u in range(U):
                        score(b.plus((u + LEAD) // U), (u + LEAD) % U)
                        if not small:
                            if u < NB:
                                project(b.plus(1), "k", u)
                            sum_heads(b, u)
                            if u < NB:
                                project(b.plus(1), "q", u)
                            if u == U - 2:
                                project(b.plus(1), "v", 0)
                            turn_probs(b.plus((u + 1) // U), (u + 1) % U)
                            continue
                        turn_probs(b.plus((u + 1) // U), (u + 1) % U)
                        sum_heads(b, u)
                        if u == 1:
                            project(b.plus(1), "v", 0)
                        if u == U - 2:
                            turn_rows(b.plus(2))
                        if u == U - 1:
                            project(b.plus(2), "k", 0)
                    if small:
                        turn_outputs(b, 0)
                        project(b.plus(2), "q", 0)
                    else:
                        turn_rows(b.plus(2))
                        project(b.plus(1), "v", NB - 1)
                    project_out(b)

        @block.vector
        def _(dve):
            def norm_part(b, n):
                steps = Steps(dve, norm_step, b.round * Norm.STEPS + Norm.PART_STARTS[n])
                norm.part(dve, steps, lambda j: sh.x[:, b.n + j, :], n)

            def norm_rows(b):
                for j in range(2):
                    norm.apply(dve, xn[:, j, :], sh.x[:, b.n + j, :], j).then_inc(xn_ready, 1)

            def empty_rows(b):
                dve.wait_ge(banks.filled("xT"), banks.until_filled("xT", b))
                dve.tensor_copy(xnT[:, :, :], banks.at("xT")[:, 0:KT * P].rearrange("p (a b) -> p a b", a=KT)).then_inc(banks.emptied("xT"), 1)

            def empty_values(b, k):
                chunk = f"v{k}"
                dve.wait_ge(banks.filled(chunk), banks.until_filled(chunk, b))
                n = BT * P // dh
                dst = v[:, b.slot, k * n * HW:(k + 1) * n * HW].rearrange("p (h e) -> p h e", e=HW)[:, :, 0:dh]
                src = banks.at(chunk)[:, 0:n * dh].rearrange("p (h e) -> p h e", e=dh)
                if biased:
                    last = dve.tensor_tensor(dst, src, w["bv"].rearrange("p (h e) -> p h e", e=dh), ALU.add)
                else:
                    last = dve.tensor_copy(dst, src)
                last.then_inc(banks.emptied(chunk), 1)

            def center(b, u, first=False):
                n = unit(b, u)
                dve.wait_ge(scored, n + 1)
                if not first:
                    dve.wait_ge(exped, n - LEAD + 1)
                scores = S[:, u % SR, :, :]
                if masked:
                    dve.wait_ge(side_ready, n + 1)
                    dve.scalar_tensor_tensor(out=d[:, u % SR, :, :].rearrange("p a b -> p (a b)"),
                                             in0=sm[:, u % SR, :, :].rearrange("p a b -> p (a b)"), scalar=2.0,
                                             in1=scores.rearrange("p a b -> p (a b)"), op0=ALU.mult, op1=ALU.add).then_inc(side_used, 1)
                    dve.wait_ge(side_used, n + 1)
                    scores = d[:, u % SR, :, :]
                dve.tensor_reduce(mx[:, u % SR, :], scores, AX.X, ALU.max).then_inc(max_step, 1)
                dve.wait_ge(max_step, n + 1)
                dve.tensor_tensor(d[:, u % SR, :, :], scores, mx[:, u % SR, :].unsqueeze(2).broadcast_to([P, UH, P]),
                                  ALU.subtract).then_inc(centered, 1)

            def normalize(b):
                dve.wait_ge(summed, b.n + 1)
                ps = O[:, 0, 0:HO * HW].rearrange("p (h e) -> p h e", e=HW)
                dve.reciprocal(rc[:, 0, :].unsqueeze(2), ps[:, :, dh:HW]).then_inc(recip_step, 1)
                dve.wait_ge(recip_step, b.n + 1)
                dve.tensor_tensor(o[:, :].rearrange("p (h e) -> p h e", e=dh), ps[:, :, 0:dh],
                                  rc[:, 0, :].unsqueeze(2).broadcast_to([P, HO, dh]), ALU.mult).then_inc(normed, 1)

            def invert_sums(b, u):
                n = unit(b, u)
                dve.wait_ge(exped, n + 1)
                dve.tensor_reduce(rc[:, u % 2, :], p[:, u % 2, :, :], AX.X, ALU.add).then_inc(sum_step, 1)
                dve.wait_ge(sum_step, n + 1)
                dve.reciprocal(rc[:, u % 2, :], rc[:, u % 2, :]).then_inc(recip_step, 1)

            def add_out(b):
                dve.wait_ge(banks.filled("proj"), banks.until_filled("proj", b))
                if biased:
                    dve.wait_ge(bias_added, b.n + 1)
                dve.tensor_tensor(sh.x[:, b.n, :], banks.at("proj")[:, 0:D], sh.x[:, b.n, :], ALU.add).then_inc(banks.emptied("proj"), 1)

            sh.wait_params(dve, phase)
            banks.open(dve)
            if not small:
                dve.sem_inc(normed, NB)
            dve.wait_ge(v_set, 1)
            start = Turn(0, 0)
            for n in range(3):
                norm_part(start, n)
            norm_rows(start)
            dve.wait_ge(xn_ready, 2)
            empty_rows(start)
            empty_values(start, 0)
            empty_rows(start.plus(1))
            if not small:
                empty_values(start, 1)
            for u in range(LEAD):
                center(start, u, first=True)
            if not small:
                invert_sums(start, 0)
            for n in range(3):
                norm_part(start.plus(2), n)
            with dve.Fori(0, BATCH // 2) as i:
                for s in range(2):
                    b = Turn(i, s)
                    for u in range(U):
                        if small and u == U - 1:
                            normalize(b)
                        if not small:
                            invert_sums(b.plus((u + 1) // U), (u + 1) % U)
                            if u == U - 1:
                                empty_values(b.plus(1), 0)
                        center(b.plus((u + LEAD) // U), (u + LEAD) % U)
                        if s == 0 and u == 0:
                            norm_rows(b.plus(2))
                        if s == 1 and u == 0:
                            dve.wait_ge(xn_ready, b.n + 3)
                        if s == 1 and u < 3:
                            norm_part(b.plus(3), u)
                        if u == (U - 2 if small else U - 1):
                            empty_rows(b.plus(2))
                        if small and u == 1:
                            empty_values(b.plus(1), 0)
                    if not small:
                        empty_values(b.plus(1), NB - 1)
                    add_out(b)


def key_bound(nc, sh, w, kT, keys):
    T = 512
    TURNS = BATCH * P // T
    with ExitStack() as ctx:
        core = Core(nc, ctx, "L1bound")
        cT = core.sb("ctxT", [P, 2, KT, T])
        k2 = core.sb("k_squared", [P, 2, 2, T])
        bk = core.sb("bias_scaled", [P, 2])
        top = core.sb("top", [P, TURNS])
        top1 = core.sb("top1", [P, 1])
        topT = core.sb("topT", [P, 1])
        K = core.ps("K", [P, 2, 2, T])
        H = core.ps("H", [P, 2, 2, T])
        projected, keys_out, squared, headed, topped, step, spare_set = (core.sem(s) for s in (
            "projected", "keys_out", "squared", "headed", "topped", "step", "spare_set"))
        loaded = [core.sem(f"ctx{s}_loaded") for s in range(2)]
        block = ctx.enter_context(nc.Block())

        @block.sync
        def _(sp):
            def load(b):
                sp.dma_start(cT[:, b.slot, :, :], sh.dram["ctxT"][:, :, bass.ts(b.n, T)]).then_inc(loaded[b.slot], 16)

            load(Turn(0, 0))
            load(Turn(0, 1))
            with sp.Fori(0, TURNS // 2 - 1) as i:
                for s in range(2):
                    sp.wait_ge(projected, i * 2 + s + 1)
                    load(Turn(i, s + 2))

        @block.gpsimd
        def _(pool):
            pool.memset(kT[:, :, keys:], 0.0).then_inc(spare_set, 1)
            pool.wait_ge(spare_set, 1)

        @block.tensor
        def _(pe):
            sh.wait_params(pe, "L1x")
            with pe.Fori(0, TURNS // 2) as i:
                for s in range(2):
                    pe.wait_ge(loaded[s], (i + 1) * 16)
                    for t in range(2):
                        for k in range(KT):
                            mm = pe.matmul(K[:, s, t, :], w["wk"][:, k, t * P:(t + 1) * P], cT[:, s, k, :], start=(k == 0), stop=(k == 1))
                    mm.then_inc(projected, 1)
                for s in range(2):
                    n = i * 2 + s
                    pe.wait_ge(squared, n * 2 + 2)
                    pe.wait_ge(topped, n + 1)
                    for t in range(2):
                        mm = pe.matmul(H[0:8, s, t, :], sh.const["headsum"], k2[:, s, t, :], start=True, stop=True)
                    mm.then_inc(headed, 1)
            pe.wait_ge(step, 2)
            pe.transpose(H[0:1, 0, 0, 0:8], top1[0:8, 0:1], sh.const["ident"][0:8, 0:8]).then_inc(headed, 1)
            pe.wait_ge(step, 3)
            pe.matmul(H[:, 0, 1, 0:1], sh.const["ones"][0:1, :], topT[0:1, :], start=True, stop=True).then_inc(headed, 1)

        @block.scalar
        def _(act):
            act.wait_ge(step, 1)
            with act.Fori(0, TURNS // 2) as i:
                for s in range(2):
                    n = i * 2 + s
                    act.wait_ge(projected, n + 1)
                    for t in range(2):
                        act.activation(kT[:, t, bass.ts(n, T)], K[:, s, t, :], ACT.Identity, bias=bk[:, t:t + 1],
                                       scale=0.25).then_inc(keys_out, 1)
                    for t in range(2):
                        act.activation(k2[:, s, t, :], K[:, s, t, :], ACT.Square, bias=bk[:, t:t + 1], scale=0.25).then_inc(squared, 1)
            act.wait_ge(keys_out, 2 * TURNS)

        @block.vector
        def _(dve):
            sh.wait_params(dve, "L1x")
            dve.tensor_scalar(bk[:, :], w["bk"], 0.25, None, ALU.mult).then_inc(step, 1)
            dve.sem_inc(topped, 2)
            with dve.Fori(0, TURNS // 2) as i:
                for s in range(2):
                    n = i * 2 + s
                    dve.wait_ge(headed, n + 1)
                    dve.tensor_reduce(top[0:8, bass.ds(n, 1)], H[0:8, s, :, :].rearrange("p a b -> p (a b)"), AX.X, ALU.max).then_inc(topped, 1)
            dve.wait_ge(topped, TURNS + 2)
            dve.tensor_reduce(top1[0:8, :], top[0:8, :], AX.X, ALU.max).then_inc(step, 1)
            dve.wait_ge(headed, TURNS + 1)
            dve.tensor_reduce(topT[0:1, :], H[0:1, 0, 0, 0:8], AX.X, ALU.max).then_inc(step, 1)
            dve.wait_ge(headed, TURNS + 2)
            dve.tensor_scalar(sh.kstab[:, :], H[:, 0, 1, 0:1], -1.0, None, ALU.mult).then_inc(step, 1)
            dve.wait_ge(step, 4)


def performer_phase(nc, sh, phase, next_phase):
    dh, HW = 16, 17
    VW = HEADS * HW + P - HW
    UH = 4
    U = HEADS // UH
    PAIRS = HEADS // 2
    EPS, STAB = 1e-4, 1e-6
    w, c = sh.params(phase), sh.const
    tables = [([("fq0", 0), ("fq1", 0)], [("fq0", 1), ("fq1", 1)]),
              ([("fk0", 0), ("fk1", 0)], [("fk0", 1), ("fk1", 1)]),
              ([("q", 0), ("v", 0), ("q", 1)], [("v", 1), ("q", 2)]),
              ([("xT", 0), ("xT", 1)], [("xT", 2), ("outT", 0), ("proj", 0)])]

    with ExitStack() as ctx:
        core = Core(nc, ctx, phase)
        kT = core.sb("keysT", [P, 2, (BATCH + 1) * P])
        key_bound(nc, sh, w, kT, BATCH * P)
        norm = Norm(core, 2)
        xn = core.sb("xn", [P, 2, D])
        xnT = core.sb("xnT", [P, KT, P])
        cT = core.sb("ctxT", [P, 2, KT, P])
        qT = core.sb("qT", [P, 2, P])
        k2 = core.sb("k_squared", [P, 2, P])
        b4 = core.sb("bias_scaled", [P, 2])
        qe = core.sb("q_exp", [P, PAIRS, P])
        kf = core.sb("k_features", [P, 2, PAIRS, P])
        qf = [sh.scratch(phase, s * 2048, (2, PAIRS, P)) for s in range(2)]
        v = sh.scratch(phase, 4096, (2, VW))
        at = core.sb("products", [P, 2, UH, P])
        den = core.sb("den", [P, HEADS])
        low = core.sb("den_low", [P, HEADS])
        o = core.sb("heads_out", [P, D])
        oT = core.sb("heads_outT", [P, 2, P])
        S = core.ps("S", [P, 2, UH, P])
        O = core.ps("O", [P, 2, BANK])
        gen = core.ps("gen", [P, 4, BANK])
        banks = Banks(core, gen, tables)
        ctx_loaded = [core.sem(f"ctx{s}_loaded") for s in range(2)]
        (xn_ready, bias_added, qf_ready, kf_ready, v_set, scored, cut, summed, normed, norm_step, den_step, squared,
         scaled) = (core.sem(s) for s in (
            "xn_ready", "bias_added", "q_features", "k_features", "v_ones_set", "scored", "cut", "heads_summed",
            "heads_normed", "norm_step", "den_step", "k_squared", "bias_scaled"))
        block = ctx.enter_context(nc.Block())

        @block.sync
        def _(sp):
            def load_ctx(b, source):
                sp.dma_start(cT[:, b.slot, :, :], sh.dram["ctxT"][:, :, bass.ts(source, P)]).then_inc(ctx_loaded[b.slot], 16)

            def following(b, source):
                sp.wait_ge(banks.emptied("v"), banks.until_emptied("v", b))
                load_ctx(b.plus(2), source)

            for k in range(2):
                load_ctx(Turn(0, k), k)
            if next_phase:
                sh.load_params(sp, next_phase)
            following(Turn(0, 0), 2)
            with sp.Fori(0, BATCH // 2 - 2) as i:
                for s in range(1, 3):
                    b = Turn(i, s)
                    following(b, b.n + 2)
            following(Turn(0, BATCH - 3), BATCH - 1)
            following(Turn(0, BATCH - 2), 0)

        @block.gpsimd
        def _(pool):
            def bias(b):
                pool.wait_ge(xn_ready, b.n + 1)
                pool.tensor_tensor(sh.x[:, b.n, :], sh.x[:, b.n, :], w["bo"], ALU.add).then_inc(bias_added, 1)

            def square(b):
                keys = kT[:, :, bass.ts(b.n, P)]
                pool.tensor_tensor(k2[:, :, :], keys, keys, ALU.mult).then_inc(squared, 1)

            def query_features(b, k):
                chunk = f"fq{k}"
                pool.wait_ge(banks.emptied(chunk), banks.until_emptied(chunk, b))
                detach_wait(pool)
                for m in range(2):
                    pool.tensor_scalar(qf[b.slot][:, m, 4 * k:4 * k + 4, :], qe[:, 4 * k:4 * k + 4, :], EPS, c["feat2"][:, m:m + 1],
                                       ALU.add, ALU.mult).then_inc(qf_ready, 1)

            pool.memset(v, 1.0).then_inc(v_set, 1)
            sh.wait_params(pool, phase)
            start = Turn(0, 0)
            square(start)
            bias(start)
            for k in range(2):
                query_features(start, k)
            with pool.Fori(0, BATCH // 2) as i:
                for s in range(2):
                    b = Turn(i, s)
                    pool.wait_ge(banks.emptied("fk1"), banks.until_emptied("fk1", b))
                    square(b.plus(1))
                    for k in range(2):
                        query_features(b.plus(1), k)
                    bias(b.plus(1))

        @block.scalar
        def _(act):
            def empty_queries(b):
                act.wait_ge(banks.filled("q"), banks.until_filled("q", b))
                for t in range(2):
                    last = act.activation(qT[:, t, :], banks.at("q")[:, t * P:(t + 1) * P], ACT.Identity, bias=b4[:, t:t + 1], scale=0.25)
                last.then_inc(banks.emptied("q"), 1)

            def exponentiate(b, name, k):
                chunk = f"{name}{k}"
                act.wait_ge(banks.filled(chunk), banks.until_filled(chunk, b))
                src = banks.at(chunk).rearrange("p (a b) -> p a b", a=4)
                if name == "fq":
                    act.activation(qe[:, 4 * k:4 * k + 4, :], src, ACT.Exp).then_inc(banks.emptied(chunk), 1)
                else:
                    act.activation(kf[:, b.slot, 4 * k:4 * k + 4, :], src, ACT.Exp, bias=sh.kstab[:, :]).then_inc(banks.emptied(chunk), 1)

            def empty_outputs(b):
                act.wait_ge(banks.filled("outT"), banks.until_filled("outT", b))
                act.activation(oT[:, :, :], banks.at("outT")[:, 0:D].rearrange("p (a b) -> p a b", a=2), ACT.Copy).then_inc(banks.emptied("outT"), 1)

            sh.wait_params(act, phase)
            act.activation(b4[:, :], w["bq"], ACT.Copy, scale=0.25).then_inc(scaled, 1)
            act.wait_ge(scaled, 1)
            start = Turn(0, 0)
            empty_queries(start)
            for k in range(2):
                exponentiate(start, "fq", k)
                exponentiate(start, "fk", k)
            empty_queries(start.plus(1))
            with act.Fori(0, BATCH // 2) as i:
                for s in range(2):
                    b = Turn(i, s)
                    for k in range(2):
                        exponentiate(b.plus(1), "fq", k)
                        exponentiate(b.plus(1), "fk", k)
                    empty_outputs(b)
                    empty_queries(b.plus(2))

        @block.tensor
        def _(pe):
            def free(name, b):
                pe.wait_ge(banks.emptied(name), banks.until_free(name, b))

            def turn_rows(b):
                pe.wait_ge(xn_ready, b.n + 1)
                free("xT", b)
                for k in range(KT):
                    mm = pe.transpose(banks.at("xT")[:, k * P:(k + 1) * P], xn[:, b.slot, k * P:(k + 1) * P], c["ident"])
                mm.then_inc(banks.filled("xT"), 1)

            def project_queries(b):
                free("q", b)
                pe.wait_ge(banks.emptied("xT"), banks.until_emptied("xT", b))
                for t in range(2):
                    for k in range(KT):
                        mm = pe.matmul(banks.at("q")[:, t * P:(t + 1) * P], w["wq"][:, k, t * P:(t + 1) * P], xnT[:, k, :],
                                       start=(k == 0), stop=(k == KT - 1))
                mm.then_inc(banks.filled("q"), 1)

            def project_values(b):
                free("v", b)
                pe.wait_ge(ctx_loaded[b.slot], (b.round + 1) * 16)
                for k in range(KT):
                    mm = pe.matmul(banks.at("v")[:, 0:D], cT[:, b.slot, k, :], w["wv"][:, k, :], start=(k == 0), stop=(k == KT - 1))
                mm.then_inc(banks.filled("v"), 1)

            def features(b, name, n):
                chunk = f"{name}{n}"
                free(chunk, b)
                if name == "fq" and n == 0:
                    pe.wait_ge(banks.emptied("q"), banks.until_emptied("q", b))
                if name == "fk" and n == 0:
                    pe.wait_ge(squared, b.n + 1)
                for s in range(4):
                    out = banks.at(chunk)[:, s * P:(s + 1) * P]
                    if name == "fq":
                        mm = pe.matmul(out, w["rf"][:, s, :], qT[:, n, :], start=True, stop=True)
                    else:
                        pe.matmul(out, w["rf"][:, s, :], kT[:, n, bass.ts(b.n, P)], start=True, stop=False)
                        mm = pe.matmul(out, c["half"][:, s, :], k2[:, n, :], start=False, stop=True)
                mm.then_inc(banks.filled(chunk), 1)

            def score(b, u):
                k = u // 2
                pe.wait_ge(qf_ready, b.n * 4 + 2 * k + 2)
                pe.wait_ge(kf_ready, b.n * 2 + k + 1)
                for r in range(UH):
                    h = u * UH + r
                    mm = pe.matmul(S[:, u % 2, r, :], kf[:, b.slot, h // 2, :], qf[b.slot][:, h % 2, h // 2, :], start=True, stop=True)
                mm.then_inc(scored, 1)

            def sum_heads(b, u):
                if u == 0:
                    pe.wait_ge(banks.emptied("v"), banks.until_emptied("v", b))
                pe.wait_ge(cut, b.n * U + u + 1)
                for r in range(UH):
                    h = u * UH + r
                    mm = pe.matmul(O[:, b.slot, h * HW:h * HW + P], at[:, u % 2, r, :], v[:, b.slot, h * HW:h * HW + P],
                                   start=True, stop=True, skip_group_check=True)
                if u == U - 1:
                    mm.then_inc(summed, 1)

            def turn_outputs(b):
                pe.wait_ge(normed, b.n + 1)
                free("outT", b)
                for t in range(2):
                    mm = pe.transpose(banks.at("outT")[:, t * P:(t + 1) * P], o[:, t * P:(t + 1) * P], c["ident"])
                mm.then_inc(banks.filled("outT"), 1)

            def project_out(b):
                free("proj", b)
                pe.wait_ge(banks.emptied("outT"), banks.until_emptied("outT", b))
                for t in range(2):
                    mm = pe.matmul(banks.at("proj")[:, 0:D], oT[:, t, :], w["wo"][:, t, :], start=(t == 0), stop=(t == 1))
                mm.then_inc(banks.filled("proj"), 1)

            sh.wait_params(pe, phase)
            start = Turn(0, 0)
            turn_rows(start)
            project_queries(start)
            for k in range(2):
                features(start, "fq", k)
                features(start, "fk", k)
            project_values(start)
            turn_rows(start.plus(1))
            project_queries(start.plus(1))
            score(start, 0)
            score(start, 1)
            with pe.Fori(0, BATCH // 2) as i:
                for s in range(2):
                    b = Turn(i, s)
                    nxt = b.plus(1)
                    for u in range(U):
                        sum_heads(b, u)
                        score(b.plus((u + 2) // U), (u + 2) % U)
                        if u < 2:
                            features(nxt, "fq", u)
                            features(nxt, "fk", u)
                        if u == 2:
                            project_values(nxt)
                            turn_rows(b.plus(2))
                    turn_outputs(b)
                    project_queries(b.plus(2))
                    project_out(b)

        @block.vector
        def _(dve):
            DEN = 4

            def norm_part(b, n):
                steps = Steps(dve, norm_step, b.round * Norm.STEPS + Norm.PART_STARTS[n])
                norm.part(dve, steps, lambda j: sh.x[:, b.n + j, :], n)

            def norm_rows(b):
                for j in range(2):
                    norm.apply(dve, xn[:, j, :], sh.x[:, b.n + j, :], j).then_inc(xn_ready, 1)

            def empty_rows(b):
                dve.wait_ge(banks.filled("xT"), banks.until_filled("xT", b))
                dve.tensor_copy(xnT[:, :, :], banks.at("xT")[:, 0:D].rearrange("p (a b) -> p a b", a=KT)).then_inc(banks.emptied("xT"), 1)

            def key_features(b, k):
                dve.wait_ge(banks.emptied(f"fk{k}"), banks.until_emptied(f"fk{k}", b))
                part = kf[:, b.slot, 4 * k:4 * k + 4, :]
                dve.tensor_scalar(part, part, EPS, 0.125, ALU.add, ALU.mult).then_inc(kf_ready, 1)

            def empty_values(b):
                dve.wait_ge(banks.filled("v"), banks.until_filled("v", b))
                dve.tensor_tensor(v[:, b.slot, 0:HEADS * HW].rearrange("p (h e) -> p h e", e=HW)[:, :, 0:dh],
                                  banks.at("v")[:, 0:D].rearrange("p (h e) -> p h e", e=dh),
                                  w["bv"].rearrange("p (h e) -> p h e", e=dh), ALU.add).then_inc(banks.emptied("v"), 1)

            def cut_products(b, u):
                dve.wait_ge(scored, b.n * U + u + 1)
                dve.tensor_tensor(at[:, u % 2, :, :], S[:, u % 2, :, :], c["causal"].unsqueeze(1).broadcast_to([P, UH, P]),
                                  ALU.mult).then_inc(cut, 1)

            def normalize(b):
                steps = Steps(dve, den_step, b.n * DEN, DEN)
                dve.wait_ge(summed, b.n + 1)
                ps = O[:, b.slot, 0:HEADS * HW].rearrange("p (h e) -> p h e", e=HW)
                steps.link(dve.tensor_copy(den[:, :].unsqueeze(2), ps[:, :, dh:HW]))
                steps.link(dve.tensor_scalar(low[:, :], den[:, :], STAB, 2.0 * STAB, ALU.is_le, ALU.mult))
                steps.link(dve.tensor_tensor(den[:, :], den[:, :], low[:, :], ALU.add))
                steps.link(dve.reciprocal(den[:, :], den[:, :]))
                dve.tensor_tensor(o[:, :].rearrange("p (h e) -> p h e", e=dh), ps[:, :, 0:dh],
                                  den[:, :].unsqueeze(2).broadcast_to([P, HEADS, dh]), ALU.mult).then_inc(normed, 1)
                steps.close()
                dve.wait_ge(normed, b.n + 1)

            def add_out(b):
                dve.wait_ge(banks.filled("proj"), banks.until_filled("proj", b))
                dve.wait_ge(bias_added, b.n + 1)
                dve.tensor_tensor(sh.x[:, b.n, :], banks.at("proj")[:, 0:D], sh.x[:, b.n, :], ALU.add).then_inc(banks.emptied("proj"), 1)

            sh.wait_params(dve, phase)
            banks.open(dve)
            dve.wait_ge(v_set, 1)
            start = Turn(0, 0)
            for n in range(3):
                norm_part(start, n)
            norm_rows(start)
            dve.wait_ge(xn_ready, 2)
            empty_rows(start)
            for k in range(2):
                key_features(start, k)
            empty_values(start)
            empty_rows(start.plus(1))
            cut_products(start, 0)
            cut_products(start, 1)
            for n in range(3):
                norm_part(start.plus(2), n)
            with dve.Fori(0, BATCH // 2) as i:
                for s in range(2):
                    b = Turn(i, s)
                    for u in range(U):
                        if u == U - 1:
                            normalize(b)
                        cut_products(b.plus((u + 2) // U), (u + 2) % U)
                        if s == 0 and u == 0:
                            norm_rows(b.plus(2))
                        if s == 1 and u == 0:
                            dve.wait_ge(xn_ready, b.n + 3)
                        if s == 1 and u < 3:
                            norm_part(b.plus(3), u)
                        if u < 2:
                            key_features(b.plus(1), u)
                        if u == 2:
                            empty_values(b.plus(1))
                            empty_rows(b.plus(2))
                    add_out(b)
                    dve.wait_ge(banks.emptied("proj"), banks.until_emptied("proj", b))


def first_of_max(dve, steps, scores, best, marks, iota, n, size):
    steps.link(dve.tensor_reduce(best, scores, AX.X, ALU.max))
    steps.link(dve.tensor_tensor(marks, scores, best.unsqueeze(2).broadcast_to([P, n, size]), ALU.is_equal))
    steps.link(dve.scalar_tensor_tensor(out=marks, in0=marks, scalar=-float(size), in1=iota, op0=ALU.mult, op1=ALU.add))


def top_two(dve, steps, chosen, scores, rest, marks, best, second, iota, n, size, parts=range(4)):
    wide = lambda a: a.unsqueeze(2).broadcast_to([P, n, size])
    for part in parts:
        if part == 0:
            first_of_max(dve, steps, scores, best, marks, iota, n, size)
        if part == 1:
            steps.link(dve.tensor_reduce(second, marks, AX.X, ALU.min))
            steps.link(dve.tensor_tensor(chosen, marks, wide(second), ALU.is_equal))
            steps.link(dve.scalar_tensor_tensor(out=rest, in0=chosen, scalar=-NEVER, in1=scores, op0=ALU.mult, op1=ALU.add))
        if part == 2:
            first_of_max(dve, steps, rest, second, marks, iota, n, size)
        if part == 3:
            steps.link(dve.tensor_reduce(second, marks, AX.X, ALU.min))
            steps.link(dve.tensor_tensor(marks, marks, wide(second), ALU.is_equal))
            steps.link(dve.tensor_tensor(chosen, chosen, marks, ALU.add))


TOP_TWO_STEPS = 12


def experts_phase(nc, sh, phase, next_phase):
    E = 8
    TILES = SLOT_TILES
    relu = phase == "L1f"
    NF = 4 if relu else 2
    w, c = sh.params(phase), sh.const
    rows_in, rows_out = sh.dram["rows_in"], sh.dram["rows_out"]
    with ExitStack() as ctx:
        core = Core(nc, ctx, phase)
        kept = core.sb("normalized", [P, BATCH, D])
        gate = core.sb("gates", [P, BATCH, E])
        lg = core.sb("logits", [P, BATCH, E])
        slot = core.sb("slots", [P, 2, BATCH], I32)
        share = core.sb("shares", [P, 2, BATCH])
        expert = core.sb("tile_experts", [P, TILES + TILES_AHEAD], I32)
        route(nc, sh, phase, w, c, kept, lg, rows_in, next_phase)
        place(nc, sh, phase, c, lg[:, :, :], gate, slot, share, expert)

        with ExitStack() as inner:
            stage = Core(nc, inner, phase + "scatter")
            scattered = stage.sem("rows_scattered")
            with nc.Block() as block:
                @block.gpsimd
                def _(pool):
                    for b in range(BATCH):
                        for k in range(2):
                            pool.indirect_dma_start(out=rows_in, out_offset=bass.IndirectOffsetOnAxis(ap=slot[:, k, b:b + 1], axis=0),
                                                    in_=kept[:, b, :], in_offset=None).then_inc(scattered, 16)
                    pool.wait_ge(scattered, 2 * BATCH * 16)

        compute_tiles(nc, sh, phase, w, c, expert, rows_in, rows_out, relu, NF)
        combine(nc, sh, phase, w, slot, share, kept, rows_out, relu)


def route(nc, sh, phase, w, c, kept, lg, rows_in, next_phase):
    G = 4
    TURNS = BATCH // G
    T = G * P
    E = 8
    with ExitStack() as ctx:
        core = Core(nc, ctx, phase + "route")
        norm = Norm(core, G)
        xn = core.sb("xn", [P, 2, G, D])
        xnT = core.sb("xnT", [P, KT, T])
        zero = core.sb("zero", [P, D])
        X = core.ps("X", [P, KT, T])
        L = core.ps("L", [P, T])
        xn_ready, turned, xT_ready, routed, logits_out, rows_kept, norm_step, zero_set, zeroed = (core.sem(s) for s in (
            "xn_ready", "xn_turned", "xnT_ready", "logits_ready", "logits_out", "rows_kept", "norm_step", "zero_set", "rows_zeroed"))
        block = ctx.enter_context(nc.Block())

        @block.sync
        def _(sp):
            sp.wait_ge(zero_set, 1)
            tiles = rows_in.rearrange("(j p) d -> p j d", p=P)
            half = (SLOT_TILES + TILES_AHEAD) // 2
            for k in range(2):
                sp.dma_start(tiles[:, k * half:(k + 1) * half, :],
                             zero[:, :].unsqueeze(1).broadcast_to([P, half, D])).then_inc(zeroed, 16)
            if next_phase:
                sh.load_params(sp, next_phase)
            sp.wait_ge(zeroed, 32)

        @block.gpsimd
        def _(pool):
            def keep(b):
                pool.wait_ge(xn_ready, b.n + 1)
                pool.tensor_copy(kept[:, bass.ts(b.n, G), :], xn[:, b.slot, :, :]).then_inc(rows_kept, 1)

            pool.memset(zero[:, :], 0.0).then_inc(zero_set, 1)
            pool.sem_inc(rows_kept, 1)
            with pool.Fori(0, TURNS // 2) as i:
                for s in range(2):
                    keep(Turn(i, s))

        @block.scalar
        def _(act):
            with act.Fori(0, TURNS // 2) as i:
                for s in range(2):
                    act.wait_ge(turned, i * 2 + s + 1)
                    act.activation(xnT[:, :, :], X[:, :, :], ACT.Copy).then_inc(xT_ready, 1)

        @block.tensor
        def _(pe):
            sh.wait_params(pe, phase)
            with pe.Fori(0, TURNS // 2) as i:
                for s in range(2):
                    t = i * 2 + s
                    pe.wait_ge(xn_ready, t + 1)
                    for k in range(KT):
                        for j in range(G):
                            mm = pe.transpose(X[:, k, j * P:(j + 1) * P], xn[:, s, j, k * P:(k + 1) * P], c["ident"])
                    mm.then_inc(turned, 1)
                    pe.wait_ge(xT_ready, t + 1)
                    pe.wait_ge(logits_out, t + 1)
                    for j in range(G):
                        for k in range(KT):
                            mm = pe.matmul(L[:, j * P:(j + 1) * P], xnT[:, k, j * P:(j + 1) * P], w["wg"][:, k, :],
                                           start=(k == 0), stop=(k == KT - 1))
                    mm.then_inc(routed, 1)

        @block.vector
        def _(dve):
            def norm_rows(b):
                steps = Steps(dve, norm_step, b.n * Norm.STEPS, Norm.STEPS)
                norm.statistics(dve, steps, lambda j: sh.x[:, b.n * G + j, :])
                dve.wait_ge(rows_kept, b.n)
                detach_wait(dve)
                for j in range(G):
                    last = norm.apply(dve, xn[:, b.slot, j, :], sh.x[:, b.n * G + j, :], j)
                last.then_inc(xn_ready, 1)
                dve.wait_ge(xn_ready, b.n + 1)
                steps.close()

            def add_bias(b):
                dve.wait_ge(routed, b.n + 1)
                dve.tensor_tensor(lg[:, bass.ts(b.n, G), :], L[:, :].rearrange("p (j e) -> p j e", j=G)[:, :, 0:E],
                                  w["bg"].unsqueeze(1).broadcast_to([P, G, E]), ALU.add).then_inc(logits_out, 1)

            sh.wait_params(dve, phase)
            dve.sem_inc(logits_out, 1)
            steps = Steps(dve, norm_step, 0, Norm.STEPS)
            norm.statistics(dve, steps, lambda j: sh.x[:, j, :])
            for j in range(G):
                last = norm.apply(dve, xn[:, 0, j, :], sh.x[:, j, :], j)
            last.then_inc(xn_ready, 1)
            dve.wait_ge(xn_ready, 1)
            with dve.Fori(0, TURNS // 2) as i:
                for s in range(2):
                    norm_rows(Turn(i, s + 1))
                    add_bias(Turn(i, s))
            dve.wait_ge(logits_out, TURNS + 1)


def place(nc, sh, phase, c, lg, gate, slot, share, expert):
    E = 8
    TILES = SLOT_TILES + TILES_AHEAD
    with ExitStack() as ctx:
        core = Core(nc, ctx, phase + "place")
        big = lambda name: core.sb(name, [P, BATCH, E])
        rest, marks, chosen, place_, sums, more = (big(n) for n in ("rest", "marks", "chosen", "place", "sums", "more"))
        best, second, total = (core.sb(n, [P, BATCH]) for n in ("best", "second", "total"))
        tiles, ends, ends2, starts = (core.sb(n, [P, E]) for n in ("tiles", "ends", "ends_next", "starts"))
        over = core.sb("over", [P, TILES, E])
        owner = core.sb("owner", [P, TILES])
        R = core.ps("R", [P, BATCH * E])
        C = core.ps("C", [P, BATCH * E])
        step, exped, centered, chosen_ready, counted = (core.sem(s) for s in (
            "place_step", "logits_exped", "logits_centered", "chosen_ready", "tokens_counted"))
        block = ctx.enter_context(nc.Block())
        wide = lambda a: a.unsqueeze(2).broadcast_to([P, BATCH, E])

        @block.scalar
        def _(act):
            act.wait_ge(centered, 1)
            act.activation(gate[:, :, :], gate[:, :, :], ACT.Exp).then_inc(exped, 1)

        @block.tensor
        def _(pe):
            pe.wait_ge(chosen_ready, 1)
            flat = chosen[:, :, :].rearrange("p b e -> p (b e)")
            pe.matmul(R[:, :], c["causal"], flat, start=True, stop=True).then_inc(counted, 1)
            pe.matmul(C[:, :], c["ones"], flat, start=True, stop=True).then_inc(counted, 1)

        @block.vector
        def _(dve):
            steps = Steps(dve, step, 0)
            link = steps.link
            link(dve.tensor_reduce(best[:, :], lg, AX.X, ALU.max))
            dve.tensor_tensor(gate[:, :, :], lg, wide(best[:, :]), ALU.subtract).then_inc(centered, 1)
            dve.wait_ge(centered, 1)
            top_two(dve, steps, chosen[:, :, :], lg, rest[:, :, :], marks[:, :, :], best[:, :], second[:, :],
                    c["iota8"].unsqueeze(1).broadcast_to([P, BATCH, E]), BATCH, E)
            dve.sem_inc(chosen_ready, 1)
            dve.wait_ge(exped, 1)
            link(dve.tensor_tensor(gate[:, :, :], gate[:, :, :], chosen[:, :, :], ALU.mult))
            link(dve.tensor_reduce(total[:, :], gate[:, :, :], AX.X, ALU.add))
            link(dve.reciprocal(total[:, :], total[:, :]))
            link(dve.tensor_tensor(gate[:, :, :], gate[:, :, :], wide(total[:, :]), ALU.mult))
            dve.wait_ge(counted, 2)
            counts = C[:, :].rearrange("p (b e) -> p b e", e=E)
            link(dve.tensor_copy(sums[:, :, :], counts))
            source, target = sums, more
            stride = 1
            while stride < BATCH:
                dve.tensor_copy(target[:, 0:stride, :], source[:, 0:stride, :])
                link(dve.tensor_tensor(target[:, stride:, :], source[:, stride:, :], source[:, 0:BATCH - stride, :], ALU.add))
                source, target = target, source
                stride *= 2
            link(dve.tensor_scalar(tiles[:, :], source[:, BATCH - 1, :], P / 2 - 0.5, 1.0 / P, ALU.add, ALU.mult))
            link(dve.tensor_scalar(tiles[:, :], tiles[:, :], ROUND, None, ALU.add))
            link(dve.tensor_scalar(tiles[:, :], tiles[:, :], -ROUND, None, ALU.add))
            link(dve.tensor_copy(ends[:, :], tiles[:, :]))
            a, b, stride = ends, ends2, 1
            while stride < E:
                dve.tensor_copy(b[:, 0:stride], a[:, 0:stride])
                link(dve.tensor_tensor(b[:, stride:], a[:, stride:], a[:, 0:E - stride], ALU.add))
                a, b, stride = b, a, stride * 2
            link(dve.tensor_tensor(starts[:, :], a[:, :], tiles[:, :], ALU.subtract))
            link(dve.tensor_scalar(starts[:, :], starts[:, :], float(P), None, ALU.mult))
            link(dve.tensor_tensor(place_[:, :, :], source[:, :, :], counts, ALU.subtract))
            link(dve.tensor_tensor(place_[:, :, :], place_[:, :, :], R[:, :].rearrange("p (b e) -> p b e", e=E), ALU.add))
            link(dve.tensor_tensor(place_[:, :, :], place_[:, :, :], starts[:, :].unsqueeze(1).broadcast_to([P, BATCH, E]), ALU.add))
            link(dve.tensor_tensor(place_[:, :, :], place_[:, :, :], chosen[:, :, :], ALU.mult))
            link(dve.tensor_reduce(best[:, :], place_[:, :, :], AX.X, ALU.max))
            link(dve.tensor_reduce(second[:, :], place_[:, :, :], AX.X, ALU.add))
            link(dve.tensor_tensor(second[:, :], second[:, :], best[:, :], ALU.subtract))
            link(dve.tensor_tensor(marks[:, :, :], place_[:, :, :], wide(best[:, :]), ALU.is_equal))
            link(dve.tensor_tensor(marks[:, :, :], marks[:, :, :], gate[:, :, :], ALU.mult))
            link(dve.tensor_reduce(share[:, 0, :], marks[:, :, :], AX.X, ALU.add))
            link(dve.tensor_tensor(marks[:, :, :], gate[:, :, :], marks[:, :, :], ALU.subtract))
            link(dve.tensor_reduce(share[:, 1, :], marks[:, :, :], AX.X, ALU.add))
            link(dve.tensor_scalar(slot[:, 0, :], best[:, :], -1.0, None, ALU.add))
            link(dve.tensor_scalar(slot[:, 1, :], second[:, :], -1.0, None, ALU.add))
            link(dve.tensor_tensor(over[:, :, :], c["tiles"].unsqueeze(2).broadcast_to([P, TILES, E]),
                                   a[:, :].unsqueeze(1).broadcast_to([P, TILES, E]), ALU.is_ge))
            link(dve.tensor_reduce(owner[:, :], over[:, :, :], AX.X, ALU.add))
            link(dve.tensor_scalar(expert[:, :], owner[:, :], float(E - 1), None, ALU.min))


def compute_tiles(nc, sh, phase, w, c, expert, rows_in, rows_out, relu, NF):
    E = 8
    TILES = SLOT_TILES
    QUAD = TILES_AHEAD
    with ExitStack() as ctx:
        core = Core(nc, ctx, phase + "tiles")
        rows = core.sb("rows", [P, QUAD, D])
        rT = core.sb("rowsT", [P, 2, KT, P])
        w1 = core.sb("w1_tile", [P, 2, KT, 512])
        b1 = core.sb("b1_tile", [P, 2, 4])
        hid = core.sb("hidden", [P, 2, NF, P])
        y = core.sb("outputs", [P, 2, D])
        silu = None if relu else core.sb("silu", [P, 2, 2, P])
        X = core.ps("X", [P, 2, BANK])
        H = core.ps("H", [P, 2, 4, P])
        Y = core.ps("Y", [P, 2, BANK])
        shifted = core.sem("x_shifted")
        turned, rT_ready, w_ready, hid_pre, silu_ready, hid_ready, summed, y_ready = (core.sem(s) for s in (
            "rows_turned", "rowsT_ready", "w1_ready", "hidden_summed", "silu_ready", "hidden_ready", "outputs_summed", "outputs_ready"))
        loaded = [core.sem(f"rows{s}_loaded") for s in range(QUAD)]
        stored = [core.sem(f"outputs{s}_stored") for s in range(2)]
        block = ctx.enter_context(nc.Block())
        CREDIT = 2

        def expert_of(eng, b):
            return eng.value_load(expert[0:1, bass.ds(b.n, 1)], min_val=0, max_val=E - 1)

        @block.sync
        def _(sp):
            def load(b):
                sp.dma_start(rows[:, b.k % QUAD, :], rows_in[bass.ts(b.n, P), :]).then_inc(loaded[b.k % QUAD], 16)

            for k in range(QUAD):
                load(Turn(0, k))
            with sp.Fori(0, TILES // QUAD) as i:
                for s in range(QUAD):
                    b = Turn(i, s, QUAD)
                    sp.wait_ge(turned, b.n + 1)
                    detach_wait(sp)
                    load(b.plus(QUAD))
                    sp.wait_ge(y_ready, b.n + 1 + CREDIT)
                    detach_wait(sp)
                    sp.dma_start(rows_out[bass.ts(b.n, P), :], y[:, b.slot, :]).then_inc(stored[b.slot], 16)
            for s in range(2):
                sp.wait_ge(stored[s], TILES // 2 * 16)
            for s in range(QUAD):
                sp.wait_ge(loaded[s], (TILES // QUAD + 1) * 16)

        if relu:
            @block.gpsimd
            def _(pool):
                with pool.Fori(0, BATCH) as i:
                    pool.tensor_tensor(sh.x[:, i, :], sh.x[:, i, :], w["beta"], ALU.add).then_inc(shifted, 1)
                pool.wait_ge(shifted, BATCH)

        @block.scalar
        def _(act):
            def hidden(b):
                act.wait_ge(hid_pre, b.n + 1)
                if relu:
                    for f in range(4):
                        last = act.activation(hid[:, b.slot, f, :], H[:, b.slot, f, :], ACT.Relu, bias=b1[:, b.slot, f:f + 1])
                    last.then_inc(hid_ready, 1)
                else:
                    act.activation(silu[:, b.slot, :, :], H[:, b.slot, 0:2, :], ACT.Silu).then_inc(silu_ready, 1)

            hidden(Turn(0, 0))
            with act.Fori(0, TILES // QUAD) as i:
                for s in range(QUAD):
                    hidden(Turn(i, s + 1, QUAD))

        @block.tensor
        def _(pe):
            def turn_rows(b):
                pe.wait_ge(loaded[b.k % QUAD], (b.i + b.k // QUAD + 1) * 16)
                for k in range(KT):
                    mm = pe.transpose(X[:, b.slot, k * P:(k + 1) * P], rows[:, b.k % QUAD, k * P:(k + 1) * P], c["ident"])
                mm.then_inc(turned, 1)

            def first_product(b):
                pe.wait_ge(rT_ready, b.n + 1)
                pe.wait_ge(w_ready, b.n + 1)
                for f in range(4):
                    for k in range(KT):
                        mm = pe.matmul(H[:, b.slot, f, :], w1[:, b.slot, k, f * P:(f + 1) * P], rT[:, b.slot, k, :],
                                       start=(k == 0), stop=(k == KT - 1))
                mm.then_inc(hid_pre, 1)

            def second_product(b):
                e = expert_of(pe, b)
                pe.wait_ge(hid_ready, b.n + 1)
                pe.wait_ge(y_ready, b.n - 1 + CREDIT)
                detach_wait(pe)
                for f in range(NF):
                    mm = pe.matmul(Y[:, b.slot, 0:D], hid[:, b.slot, f, :],
                                   w["w2"][:, bass.ds(e, 1), f, :].rearrange("p a d -> p (a d)"), start=(f == 0), stop=(f == NF - 1))
                mm.then_inc(summed, 1)

            turn_rows(Turn(0, 0))
            first_product(Turn(0, 0))
            turn_rows(Turn(0, 1))
            with pe.Fori(0, TILES // QUAD) as i:
                for s in range(QUAD):
                    b = Turn(i, s, QUAD)
                    first_product(b.plus(1))
                    turn_rows(b.plus(2))
                    second_product(b)

        @block.vector
        def _(dve):
            def empty_rows(b):
                dve.wait_ge(turned, b.n + 1)
                dve.tensor_copy(rT[:, b.slot, :, :].rearrange("p k t -> p (k t)"), X[:, b.slot, 0:D]).then_inc(rT_ready, 1)

            def multiply(b):
                dve.wait_ge(silu_ready, b.n + 1)
                dve.tensor_tensor(hid[:, b.slot, :, :], silu[:, b.slot, :, :], H[:, b.slot, 2:4, :], ALU.mult).then_inc(hid_ready, 1)

            def fetch(b, first=False):
                e = expert_of(dve, b)
                if not first:
                    dve.wait_ge(hid_ready, b.n - 1)
                detach_wait(dve)
                if relu:
                    dve.tensor_copy(b1[:, b.slot, :], w["b1"][:, bass.ds(e, 1), :].rearrange("p a b -> p (a b)"))
                dve.tensor_copy(w1[:, b.slot, :, :].rearrange("p k f -> p (k f)"),
                                w["w1"][:, bass.ds(e, 1), :, :].rearrange("p a k f -> p (a k f)")).then_inc(w_ready, 1)

            def empty_outputs(b):
                if relu:
                    e = expert_of(dve, b)
                dve.wait_ge(summed, b.n + 1)
                dve.wait_ge(stored[b.slot], b.round * 16)
                detach_wait(dve)
                if relu:
                    dve.tensor_tensor(y[:, b.slot, :], Y[:, b.slot, 0:D], w["b2"][:, bass.ds(e, 1), :].rearrange("p a d -> p (a d)"),
                                      ALU.add).then_inc(y_ready, 1)
                else:
                    dve.tensor_copy(y[:, b.slot, :], Y[:, b.slot, 0:D]).then_inc(y_ready, 1)

            dve.sem_inc(y_ready, CREDIT)
            for k in range(2):
                fetch(Turn(0, k), first=True)
                empty_rows(Turn(0, k))
            if not relu:
                multiply(Turn(0, 0))
            with dve.Fori(0, TILES // QUAD) as i:
                for s in range(QUAD):
                    b = Turn(i, s, QUAD)
                    fetch(b.plus(2))
                    empty_rows(b.plus(2))
                    if not relu:
                        multiply(b.plus(1))
                    empty_outputs(b)


def combine(nc, sh, phase, w, slot, share, kept, rows_out, relu):
    G = 4
    TURNS = BATCH // G
    with ExitStack() as ctx:
        core = Core(nc, ctx, phase + "combine")
        both = core.sb("gathered", [P, 2, G, 2, D])
        acc = core.sb("mixed", [P, G, D])
        now = core.sb("shares_now", [P, 2, G])
        norm = Norm(core, G, "close")
        gathered = [core.sem(f"gathered{s}") for s in range(2)]
        used, step = core.sem("gathered_used"), core.sem("combine_step")
        block = ctx.enter_context(nc.Block())

        @block.gpsimd
        def _(pool):
            for t in range(TURNS):
                if t >= 2:
                    pool.wait_ge(used, t - 1)
                for j in range(G):
                    for k in range(2):
                        pool.indirect_dma_start(out=both[:, t % 2, j, k, :], out_offset=None, in_=rows_out,
                                                in_offset=bass.IndirectOffsetOnAxis(ap=slot[:, k, t * G + j:t * G + j + 1], axis=0)
                                                ).then_inc(gathered[t % 2], 16)

        @block.vector
        def _(dve):
            per = 3 + Norm.STEPS + 2 if relu else 3
            with dve.Fori(0, TURNS // 2) as i:
                for s in range(2):
                    t = i * 2 + s
                    steps = Steps(dve, step, t * per, per)
                    row = lambda j: sh.x[:, t * G + j, :]
                    steps.link(dve.tensor_copy(now[:, :, :], share[:, :, bass.ts(t, G)]))
                    dve.wait_ge(gathered[s], (i + 1) * G * 2 * 16)
                    for k in range(2):
                        for j in range(G):
                            base = acc[:, j, :] if k else kept[:, t * G + j, :] if relu else row(j)
                            out = row(j) if k and not relu else acc[:, j, :]
                            last = dve.scalar_tensor_tensor(out=out, in0=both[:, s, j, k, :], scalar=now[:, k, j:j + 1], in1=base,
                                                            op0=ALU.mult, op1=ALU.add)
                        steps.link(last)
                    dve.sem_inc(used, 1)
                    if relu:
                        norm.statistics(dve, steps, lambda j: acc[:, j, :])
                        for j in range(G):
                            last = dve.scalar_tensor_tensor(out=acc[:, j, :], in0=acc[:, j, :], scalar=norm.mean_var[:, j, 0:1],
                                                            in1=w["gamma"], op0=ALU.subtract, op1=ALU.mult)
                        steps.link(last)
                        for j in range(G):
                            last = dve.scalar_tensor_tensor(out=row(j), in0=acc[:, j, :], scalar=norm.root[:, j:j + 1], in1=row(j),
                                                            op0=ALU.mult, op1=ALU.add)
                        steps.link(last)
                    steps.close()


def head_experts_phase(nc, sh, phase, next_phase):
    G = 4
    TURNS = BATCH // G
    T = G * P
    E, NH = 16, 8
    N = G * NH
    M = E * KT
    H = 2 * M
    w, c = sh.params(phase), sh.const
    names = (("xT0", "h0", "logits", "bias0", "proj0"), ("xT1", "h1", "gT", "bias1", "proj1"))
    tables = [([(n, 0) for n in bank[:4]], [(n, 1) for n in bank[:4]] + [(bank[4], 0)]) for bank in names]
    with ExitStack() as ctx:
        core = Core(nc, ctx, phase)
        norm = Norm(core, G)
        xn = core.sb("xn", [P, G, D])
        xnT = core.sb("xnT", [P, KT, T])
        hT = core.sb("hT", [P, KT, T])
        acc = core.sb("mixed", [P, 2, KT, T])
        hi = core.sb("h_high", [P, KT, T], F16)
        lo = core.sb("h_low", [P, KT, T], F16)
        w1s = core.sb("w1_stacked", [P, E, P], F16)
        gb = core.sb("gates_wide", [P, 2, KT, T])
        tmp = core.sb("gated", [P, 2, T])
        gT = core.sb("gatesT", [P, T])
        rest, marks, chosen = (core.sb(n, [P, N, E]) for n in ("rest", "marks", "chosen"))
        best, second = (core.sb(n, [P, N]) for n in ("best", "second"))
        stack = sh.scratch(phase, 0, (2, 2048)).rearrange("p a b -> p (a b)").bitcast(F16).rearrange(
            "p (n t s c) -> p n t s c", n=2, t=KT, s=4)
        hid = sh.scratch(phase, 4096, (4, 2, T))
        pr = sh.scratch(phase, 8192, (N, E))
        Z = core.ps("Z", [P, 2, 2, T])
        O = core.ps("O", [P, 2, T])
        gen = core.ps("gen", [P, 2, T])
        banks = Banks(core, gen, tables)
        (xn_ready, bias_added, h_ready, high, low, stacked, centered, exped, gated, stored, hid_pre,
         hid_ready, summed, weighted, mixed, norm_step, gate_step, w1_ready) = (core.sem(s) for s in (
            "xn_ready", "bias_added", "h_ready", "h_high", "h_low", "h_stacked",
            "logits_centered", "logits_exped", "gates_ready", "gates_stored", "hidden_summed", "hidden_ready",
            "outputs_summed", "outputs_weighted", "outputs_mixed", "norm_step", "gate_step", "w1_stacked"))
        block = ctx.enter_context(nc.Block())
        wide = [core.sem(f"gates_wide{n}") for n in range(2)]
        CREDIT = 2

        @block.sync
        def _(sp):
            def stack_parts(b, pieces):
                for piece in pieces:
                    part, s = piece // 4, piece % 4
                    if piece == 0:
                        sp.wait_ge(high, (b.n + 1) * KT)
                    if piece == 8:
                        sp.wait_ge(low, b.n + 1)
                    sp.dma_start(stack[32 * part:32 * part + 32, b.slot, :, s, :],
                                 (hi if part < 2 else lo)[32 * s:32 * s + 32, :, :]).then_inc(stacked, 16)

            def store_gates(b):
                sp.wait_ge(banks.emptied("gT"), banks.until_emptied("gT", b))
                detach_wait(sp)
                sp.dma_start(sh.dram["gates"][b.n], gT[:, :]).then_inc(stored, 16)
                sp.wait_ge(stored, (b.n + 1) * 16)
                detach_wait(sp)

            def load_gates(b, e):
                for t in range(KT):
                    rows = sh.dram["gates"][b.n, t * 64 + e:t * 64 + e + 3 * E + 1:E, :]
                    sp.dma_start(gb[:, e % 2, t, :], rows.unsqueeze(1).broadcast_to([4, 32, T])).then_inc(wide[e % 2], 16)

            if next_phase:
                sh.load_params(sp, next_phase)
            start = Turn(0, 0)
            stack_parts(start, range(16))
            store_gates(start)
            load_gates(start, 0)
            load_gates(start, 1)
            with sp.Fori(0, TURNS // 2) as i:
                for s in range(2):
                    b = Turn(i, s)
                    for e in range(E):
                        if 6 <= e < 14:
                            stack_parts(b.plus(1), range(2 * e - 12, 2 * e - 10))
                        if e == E - 2:
                            store_gates(b.plus(1))
                        sp.wait_ge(weighted, b.n * M + (e + 1) * KT + CREDIT)
                        detach_wait(sp)
                        load_gates(b.plus((e + 2) // E), (e + 2) % E)
            for n in range(2):
                sp.wait_ge(wide[n], (TURNS * (E // 2) + 1) * KT * 16)

        @block.gpsimd
        def _(pool):
            def bias_out(b, j):
                pool.wait_ge(xn_ready, (b.n + 1) * G)
                pool.tensor_tensor(sh.x[:, b.n * G + j, :], sh.x[:, b.n * G + j, :], w["bo"], ALU.add).then_inc(bias_added, 1)

            def high_part(b, t):
                pool.wait_ge(h_ready, b.n * KT + t + 1)
                detach_wait(pool)
                pool.tensor_copy(hi[:, t, :], hT[:, t, :]).then_inc(high, 1)

            sh.wait_params(pool, phase)
            start = Turn(0, 0)
            for j in range(G):
                bias_out(start, j)
            for t in range(KT):
                high_part(start, t)
            with pool.Fori(0, TURNS // 2) as i:
                for s in range(2):
                    b = Turn(i, s)
                    for m in range(M):
                        pool.wait_ge(weighted, b.n * M + m + 1 + CREDIT)
                        if m < KT:
                            pool.wait_ge(banks.emptied(f"bias{m}"), banks.until_emptied(f"bias{m}", b))
                        else:
                            pool.wait_ge(mixed, b.n * M + m - 1 + CREDIT)
                        pool.tensor_tensor(acc[:, s, m % KT, :], acc[:, s, m % KT, :], tmp[:, m % 2, :], ALU.add).then_inc(mixed, 1)
                        if 16 <= m < 16 + G:
                            bias_out(b.plus(1), m - 16)
                        if 8 <= m < 8 + KT:
                            high_part(b.plus(1), m - 8)

        @block.scalar
        def _(act):
            def exponentiate(b):
                act.wait_ge(centered, b.n + 1)
                act.activation(pr, pr, ACT.Exp).then_inc(exped, 1)

            sh.wait_params(act, phase)
            exponentiate(Turn(0, 0))
            with act.Fori(0, TURNS // 2) as i:
                for s in range(2):
                    b = Turn(i, s)
                    for n in range(H):
                        act.wait_ge(hid_pre, b.n * H + n + 1)
                        act.activation(hid[:, n % 4, :, :], Z[:, n % 2, :, :], ACT.Gelu, bias=w["b1"][:, n // 4:n // 4 + 1]).then_inc(hid_ready, 1)
                        if n == 30:
                            exponentiate(b.plus(1))

        @block.tensor
        def _(pe):
            def free(name, b):
                pe.wait_ge(banks.emptied(name), banks.until_free(name, b))

            def turn_rows(b):
                pe.wait_ge(xn_ready, (b.n + 1) * G)
                for k in range(KT):
                    free(f"xT{k}", b)
                    for j in range(G):
                        mm = pe.transpose(banks.at(f"xT{k}")[:, j * P:(j + 1) * P], xn[:, j, k * P:(k + 1) * P], c["ident"])
                    mm.then_inc(banks.filled(f"xT{k}"), 1)

            def project_heads(b, t):
                for k in range(KT):
                    free(f"h{k}", b)
                for k in range(KT):
                    mm = pe.matmul(banks.at(f"h{t}"), w["wm"][:, k, t * P:(t + 1) * P], xnT[:, k, :], start=(k == 0), stop=(k == KT - 1))
                mm.then_inc(banks.filled(f"h{t}"), 1)

            def route(b):
                free("logits", b)
                pe.wait_ge(h_ready, (b.n + 1) * KT)
                for j in range(G):
                    for k in range(KT):
                        mm = pe.matmul(banks.at("logits")[:, j * P:(j + 1) * P], hT[:, k, j * P:(j + 1) * P], w["emb"][:, k, :],
                                       start=(k == 0), stop=(k == KT - 1))
                mm.then_inc(banks.filled("logits"), 1)

            def turn_gates(b):
                free("gT", b)
                pe.wait_ge(gated, b.n + 1)
                for j in range(G):
                    mm = pe.transpose(banks.at("gT")[:, j * P:(j + 1) * P],
                                      chosen[:, j * NH:(j + 1) * NH, :].rearrange("p h e -> p (h e)"), c["ident"])
                mm.then_inc(banks.filled("gT"), 1)

            def weigh_biases(b, t):
                free(f"bias{t}", b)
                pe.wait_ge(banks.emptied("gT"), banks.until_emptied("gT", b))
                pe.matmul(banks.at(f"bias{t}"), w["b2"][:, t, :], gT[:, :], start=True, stop=True).then_inc(banks.filled(f"bias{t}"), 1)

            def first_product(b, n):
                e, t, half = n // 4, n // 2 % 2, n % 2
                if n == 0:
                    pe.wait_ge(stacked, (b.n + 1) * 256)
                for s in range(2):
                    mm = pe.matmul(Z[:, n % 2, s, :], w1s[:, e, :], stack[:, b.slot, t, 2 * half + s, :], start=True, stop=True)
                mm.then_inc(hid_pre, 1)

            def second_product(b, n):
                e, t, half = n // 4, n // 2 % 2, n % 2
                m = 2 * e + t
                if half == 0:
                    pe.wait_ge(weighted, b.n * M + m - 1 + CREDIT)
                for s in range(2):
                    at = 32 * (2 * half + s)
                    mm = pe.matmul(O[at:at + 32, m % 2, :], w["w2"][:, e, :], hid[:, n % 4, s, :], start=True, stop=True)
                mm.then_inc(summed, 1)

            def project_out(b, pair):
                pe.wait_ge(mixed, (b.n + 1) * M + CREDIT)
                free(f"proj{pair}", b)
                for j in range(2):
                    q = 2 * pair + j
                    for t in range(KT):
                        mm = pe.matmul(banks.at(f"proj{pair}")[:, j * D:(j + 1) * D], acc[:, b.slot, t, q * P:(q + 1) * P], w["wo"][:, t, :],
                                       start=(t == 0), stop=(t == KT - 1))
                mm.then_inc(banks.filled(f"proj{pair}"), 1)

            sh.wait_params(pe, phase)
            start = Turn(0, 0)
            turn_rows(start)
            project_heads(start, 0)
            project_heads(start, 1)
            route(start)
            pe.wait_ge(w1_ready, 2)
            first_product(start, 0)
            first_product(start, 1)
            turn_gates(start)
            weigh_biases(start, 0)
            weigh_biases(start, 1)
            with pe.Fori(0, TURNS // 2) as i:
                for s in range(2):
                    b = Turn(i, s)
                    for n in range(H):
                        pe.wait_ge(hid_ready, b.n * H + n + 1)
                        first_product(b.plus((n + 2) // H), (n + 2) % H)
                        second_product(b, n)
                        if n == 11:
                            turn_rows(b.plus(1))
                        if n in (15, 17):
                            project_heads(b.plus(1), (n - 15) // 2)
                        if n == 23:
                            route(b.plus(1))
                        if n == 50:
                            turn_gates(b.plus(1))
                        if n in (54, 56):
                            weigh_biases(b.plus(1), (n - 54) // 2)
                    project_out(b, 0)
                    project_out(b, 1)

        @block.vector
        def _(dve):
            GATE_STEPS = 1 + 3 + TOP_TWO_STEPS
            wide_ = lambda a: a.unsqueeze(2).broadcast_to([P, N, E])

            def norm_part(b, n):
                steps = Steps(dve, norm_step, b.n * Norm.STEPS + Norm.PART_STARTS[n])
                norm.part(dve, steps, lambda j: sh.x[:, b.n * G + j, :], n)

            def norm_rows(b):
                for j in range(G):
                    norm.apply(dve, xn[:, j, :], sh.x[:, b.n * G + j, :], j).then_inc(xn_ready, 1)

            def empty_rows(b, k):
                dve.wait_ge(banks.filled(f"xT{k}"), banks.until_filled(f"xT{k}", b))
                dve.tensor_copy(xnT[:, k, :], banks.at(f"xT{k}")).then_inc(banks.emptied(f"xT{k}"), 1)

            def empty_heads(b, t):
                dve.wait_ge(banks.filled(f"h{t}"), banks.until_filled(f"h{t}", b))
                dve.tensor_scalar(hT[:, t, :], banks.at(f"h{t}"), w["bm"][:, t:t + 1], None, ALU.add).then_inc(h_ready, 1)
                dve.sem_inc(banks.emptied(f"h{t}"), 1)

            def low_part(b):
                dve.wait_ge(high, (b.n + 1) * KT)
                dve.tensor_tensor(lo[:, :, :], hT[:, :, :], hi[:, :, :], ALU.subtract).then_inc(low, 1)

            def gate_part(b, n):
                starts = (0, 1, 4, 7, 10, 13)
                steps = Steps(dve, gate_step, b.n * GATE_STEPS + starts[min(n, 5)])
                if n == 0:
                    dve.wait_ge(banks.filled("logits"), banks.until_filled("logits", b))
                    logits = banks.at("logits").rearrange("p (n e) -> p n e", e=E)
                    steps.link(dve.tensor_reduce(best[:, :], logits, AX.X, ALU.max))
                    dve.tensor_tensor(pr, logits, wide_(best[:, :]), ALU.subtract).then_inc(centered, 1)
                    dve.wait_ge(centered, b.n + 1)
                    dve.sem_inc(banks.emptied("logits"), 1)
                elif n == 1:
                    dve.wait_ge(exped, b.n + 1)
                    steps.link(dve.tensor_reduce(best[:, :], pr, AX.X, ALU.add))
                    steps.link(dve.reciprocal(best[:, :], best[:, :]))
                    steps.link(dve.tensor_tensor(pr, pr, wide_(best[:, :]), ALU.mult))
                elif n < 6:
                    top_two(dve, steps, chosen[:, :, :], pr, rest[:, :, :], marks[:, :, :], best[:, :], second[:, :],
                            c["iota16"].unsqueeze(1).broadcast_to([P, N, E]), N, E, parts=[n - 2])
                else:
                    dve.tensor_tensor(chosen[:, :, :], chosen[:, :, :], pr, ALU.mult).then_inc(gated, 1)

            def empty_gates(b):
                dve.wait_ge(banks.filled("gT"), banks.until_filled("gT", b))
                dve.tensor_copy(gT[:, :], banks.at("gT")).then_inc(banks.emptied("gT"), 1)

            def empty_biases(b, t):
                dve.wait_ge(banks.filled(f"bias{t}"), banks.until_filled(f"bias{t}", b))
                dve.tensor_copy(acc[:, b.slot, t, :], banks.at(f"bias{t}")).then_inc(banks.emptied(f"bias{t}"), 1)

            def weigh(b, m):
                e = m // KT
                dve.wait_ge(summed, b.n * H + 2 * m + 2)
                dve.wait_ge(wide[e % 2], b.n * (E // 2 * KT * 16) + (e // 2 + 1) * KT * 16)
                dve.wait_ge(mixed, b.n * M + m - 1 + CREDIT)
                dve.tensor_tensor(tmp[:, m % 2, :], O[:, m % 2, :], gb[:, e % 2, m % KT, :], ALU.mult).then_inc(weighted, 1)

            def add_out(b, pair):
                name = f"proj{pair}"
                dve.wait_ge(banks.filled(name), banks.until_filled(name, b))
                dve.wait_ge(bias_added, (b.n + 1) * G)
                at = bass.ds(b.n * G + 2 * pair, 2)
                dve.tensor_tensor(sh.x[:, at, :], banks.at(name).rearrange("p (j d) -> p j d", j=2), sh.x[:, at, :],
                                  ALU.add).then_inc(banks.emptied(name), 1)

            sh.wait_params(dve, phase)
            banks.open(dve)
            dve.sem_inc(weighted, CREDIT)
            dve.sem_inc(mixed, CREDIT)
            start = Turn(0, 0)
            for n in range(3):
                norm_part(start, n)
            norm_rows(start)
            dve.tensor_copy(w1s[:, :, :], w["w1"]).then_inc(w1_ready, 1)
            dve.wait_ge(w1_ready, 1)
            for s in (1, 3):
                r = slice(32 * s, 32 * s + 32)
                last = dve.tensor_tensor(w1s[r, :, :], w["w1"][r, :, :], w1s[r, :, :], ALU.subtract)
            last.then_inc(w1_ready, 1)
            for k in range(KT):
                empty_rows(start, k)
            for t in range(KT):
                empty_heads(start, t)
            low_part(start)
            for n in range(7):
                gate_part(start, n)
            empty_gates(start)
            for t in range(KT):
                empty_biases(start, t)
            with dve.Fori(0, TURNS // 2) as i:
                for s in range(2):
                    b = Turn(i, s)
                    nxt = b.plus(1)
                    for m in range(M):
                        weigh(b, m)
                        if m == 0:
                            dve.wait_ge(xn_ready, (b.n + 1) * G)
                        if m in (0, 1, 3):
                            norm_part(nxt, (m + 1) // 2)
                        if m == 4:
                            norm_rows(nxt)
                        if m in (6, 7):
                            empty_rows(nxt, m - 6)
                        if m in (8, 9):
                            empty_heads(nxt, m - 8)
                        if m == 11:
                            low_part(nxt)
                        if m == 13:
                            gate_part(nxt, 0)
                        if m in (16, 17, 19, 21, 23):
                            gate_part(nxt, (16, 17, 19, 21, 23).index(m) + 1)
                        if m == 24:
                            dve.wait_ge(gate_step, (nxt.n + 1) * GATE_STEPS)
                            gate_part(nxt, 6)
                        if m == 26:
                            empty_gates(nxt)
                        if m in (28, 29):
                            empty_biases(nxt, m - 28)
                    for pair in range(2):
                        add_out(b, pair)
                    dve.wait_ge(banks.emptied("proj1"), banks.until_emptied("proj1", b))
                    dve.wait_ge(banks.emptied("proj0"), banks.until_emptied("proj0", b))


def quantized_phase(nc, sh, phase, next_phase):
    G = 2
    TURNS = BATCH // G
    T = G * P
    F = 1024
    FT = F // P
    FLOOR = 1e-5
    w, c = sh.params(phase), sh.const
    with ExitStack() as ctx:
        core = Core(nc, ctx, phase)
        norm, again = Norm(core, 2 * G), Norm(core, G, "ln1")
        wq1 = core.sb("w1_ternary", [P, KT, F], BF16)
        wq2 = core.sb("w2_ternary", [P, FT, D], BF16)
        ident = core.sb("ident16", [P, P], BF16)
        ws = core.sb("weight_scales", [P, 2])
        wi = core.sb("weight_inverse", [P, 2])
        xn = core.sb("xn", [P, G, D])
        xq = core.sb("x_int", [P, G, D], BF16)
        xqT = core.sb("x_intT", [P, KT, T], BF16)
        amax, inv = (core.sb(n, [P, G]) for n in ("amax", "inverse"))
        back = core.sb("back", [P, 2, G])
        h = core.sb("hidden", [P, 2, G, F])
        hn = core.sb("hidden_norm", [P, 2, G, F])
        hq = core.sb("hidden_int", [P, G, F], BF16)
        hqT = core.sb("hidden_intT", [P, G, FT, P], BF16)
        stats2 = core.sb("ln2_stats", [P, G, 2, 6])
        mv2, root2 = norm.mean_var[:, G:, :], norm.root[:, G:]
        shift2, amax2, inv2, back2 = (core.sb(n, [P, G]) for n in ("ln2_shift", "amax2", "inverse2", "back2"))
        Hp = core.ps("H", [P, G, F])
        XT = core.ps("XT", [P, 2 * KT, T], BF16)
        HT = core.ps("HT", [P, FT, P], BF16)
        Y = core.ps("Y", [P, G, BANK])
        (w_summed, w_total, w_ready, ident_ready, norm_ready, bias_added, quantized, x_turned, xT_ready, hid_pre, hid_scaled,
         hid_biased, hid_act, shifted, normalized, gained, affine, hq_ready, h_turned, hT_ready, out_ready, out_added, prep_step,
         front_step, quant_step) = (core.sem(s) for s in (
            "weights_summed", "weights_total", "weights_ready", "ident16_ready", "x_read", "bias_added", "x_quantized",
            "x_turned", "xT_ready", "hidden_summed", "hidden_scaled", "hidden_biased", "hidden_act", "ln2_ready",
            "hidden_normalized", "hidden_gained", "hidden_affine", "hidden_quantized", "hidden_turned", "hiddenT_ready",
            "out_summed", "out_added", "prep_step", "front_step", "quantize_step"))
        block = ctx.enter_context(nc.Block())

        @block.sync
        def _(sp):
            if next_phase:
                sh.load_params(sp, next_phase)

        @block.gpsimd
        def _(pool):
            def bias_hidden(b):
                for j in range(G):
                    pool.wait_ge(hid_scaled, b.n * G + j + 1)
                    pool.tensor_tensor(h[:, b.slot, j, :], h[:, b.slot, j, :], w["b1"], ALU.add).then_inc(hid_biased, 1)

            def affine_hidden(b):
                for j in range(G):
                    pool.wait_ge(normalized, b.n * G + j + 1)
                    pool.tensor_tensor(hn[:, b.slot, j, :], hn[:, b.slot, j, :], w["g2"], ALU.mult).then_inc(gained, 1)
                    pool.wait_ge(gained, b.n * G + j + 1)
                    pool.tensor_tensor(hn[:, b.slot, j, :], hn[:, b.slot, j, :], w["c2"], ALU.add).then_inc(affine, 1)

            def bias_out(b):
                pool.wait_ge(norm_ready, b.n + 1)
                for j in range(G):
                    pool.tensor_tensor(sh.x[:, b.n * G + j, :], sh.x[:, b.n * G + j, :], w["b2"], ALU.add).then_inc(bias_added, 1)

            sh.wait_params(pool, phase)
            pool.tensor_copy(ident[:, :], c["ident"]).then_inc(ident_ready, 1)
            start = Turn(0, 0)
            bias_hidden(start)
            bias_hidden(start.plus(1))
            affine_hidden(start)
            with pool.Fori(0, TURNS // 2) as i:
                for s in range(2):
                    b = Turn(i, s)
                    bias_hidden(b.plus(2))
                    affine_hidden(b.plus(1))
                    bias_out(b)

        @block.scalar
        def _(act):
            def empty_rows(b):
                act.wait_ge(x_turned, b.n + 1)
                act.activation(xqT[:, :, :], XT[:, 0:KT, :], ACT.Copy).then_inc(xT_ready, 1)

            def scale_hidden(b):
                for j in range(G):
                    act.wait_ge(hid_pre, b.n * G + j + 1)
                    act.activation(h[:, b.slot, j, :], Hp[:, j, :], ACT.Copy, scale=back[:, b.slot, j:j + 1]).then_inc(hid_scaled, 1)

            def gelu(b):
                for j in range(G):
                    act.wait_ge(hid_biased, b.n * G + j + 1)
                    act.activation(h[:, b.slot, j, :], h[:, b.slot, j, :], ACT.Gelu).then_inc(hid_act, 1)

            def normalize(b):
                act.wait_ge(shifted, b.n + 1)
                for j in range(G):
                    act.activation(hn[:, b.slot, j, :], h[:, b.slot, j, :], ACT.Identity, bias=shift2[:, j:j + 1],
                                   scale=norm.root[:, G + j:G + j + 1]).then_inc(normalized, 1)

            def empty_hidden(b):
                for j in range(G):
                    act.wait_ge(h_turned, b.n * G + j + 1)
                    act.activation(hqT[:, j, :, :], HT[:, :, :], ACT.Copy).then_inc(hT_ready, 1)

            start = Turn(0, 0)
            for k in range(2):
                empty_rows(start.plus(k))
                scale_hidden(start.plus(k))
            gelu(start)
            normalize(start)
            gelu(start.plus(1))
            empty_rows(start.plus(2))
            act.wait_ge(normalized, G)
            scale_hidden(start.plus(2))
            with act.Fori(0, TURNS // 2) as i:
                for s in range(2):
                    b = Turn(i, s)
                    normalize(b.plus(1))
                    gelu(b.plus(2))
                    empty_hidden(b)
                    empty_rows(b.plus(3))
                    act.wait_ge(normalized, (b.n + 2) * G)
                    scale_hidden(b.plus(3))

        @block.tensor
        def _(pe):
            def first_product(b, first=False):
                pe.wait_ge(quantized, b.n + 1)
                for k in range(KT):
                    for j in range(G):
                        mm = pe.transpose(XT[:, k, j * P:(j + 1) * P], xq[:, j, k * P:(k + 1) * P], ident[:, :])
                mm.then_inc(x_turned, 1)
                pe.wait_ge(xT_ready, b.n + 1)
                for j in range(G):
                    if not first:
                        pe.wait_ge(hid_scaled, b.n * G + j - 1)
                    for half in range(2):
                        for k in range(KT):
                            mm = pe.matmul(Hp[:, j, half * BANK:(half + 1) * BANK], xqT[:, k, j * P:(j + 1) * P],
                                           wq1[:, k, half * BANK:(half + 1) * BANK], start=(k == 0), stop=(k == KT - 1))
                    mm.then_inc(hid_pre, 1)

            def second_product(b):
                for j in range(G):
                    pe.wait_ge(hq_ready, b.n * G + j + 1)
                    if j >= 1:
                        pe.wait_ge(hT_ready, b.n * G + j)
                    for t in range(FT):
                        mm = pe.transpose(HT[:, t, :], hq[:, j, t * P:(t + 1) * P], ident[:, :])
                    mm.then_inc(h_turned, 1)
                for j in range(G):
                    pe.wait_ge(hT_ready, b.n * G + j + 1)
                    for t in range(FT):
                        mm = pe.matmul(Y[:, j, 0:D], hqT[:, j, t, :], wq2[:, t, :], start=(t == 0), stop=(t == FT - 1))
                    mm.then_inc(out_ready, 1)

            pe.wait_ge(w_summed, 2)
            pe.matmul(Y[:, 0, 0:2], c["ones"], ws[:, :], start=True, stop=True).then_inc(w_total, 1)
            pe.wait_ge(w_ready, 2)
            pe.wait_ge(ident_ready, 1)
            start = Turn(0, 0)
            first_product(start, first=True)
            first_product(start.plus(1))
            first_product(start.plus(2))
            with pe.Fori(0, TURNS // 2) as i:
                for s in range(2):
                    b = Turn(i, s)
                    second_product(b)
                    first_product(b.plus(3))

        @block.vector
        def _(dve):
            FRONT = 2 * Norm.STEPS + 3 + 1 + 3 + 1
            QUANT = 1 + 3 + 1

            def quantize(steps, amax, inv, back, scale):
                steps.link(dve.tensor_scalar(amax, amax, FLOOR, None, ALU.max))
                steps.link(dve.reciprocal(inv, amax))
                dve.tensor_scalar(back, amax, 1.0 / 127.0, scale, ALU.mult, ALU.mult)
                steps.link(dve.tensor_scalar(inv, inv, 127.0, None, ALU.mult))

            def statistics(b, hidden=None, first=False):
                steps = Steps(dve, front_step, b.n * FRONT)
                last = None
                for j in range(G):
                    last = dve.bn_stats(norm.stats[:, j, :], sh.x[:, b.n * G + j, :])
                if hidden:
                    dve.wait_ge(hid_act, (hidden.n + 1) * G)
                    for j in range(G):
                        dve.bn_stats(stats2[:, j, 0, :], h[:, hidden.slot, j, 0:BANK])
                        last = dve.bn_stats(stats2[:, j, 1, :], h[:, hidden.slot, j, BANK:F])
                steps.link(last)
                if hidden and not first:
                    dve.wait_ge(normalized, hidden.n * G)
                detach_wait(dve)
                for j in range(G):
                    last = dve.bn_aggr(norm.mean_var[:, j, :], norm.stats[:, j, :])
                if hidden:
                    for j in range(G):
                        last = dve.bn_aggr(mv2[:, j, :], stats2[:, j, :, :])
                steps.link(last)
                n = 2 * G if hidden else G
                rsqrt(dve, steps, norm.mean_var[:, 0:n, 1], norm.half[:, 0:n], norm.root[:, 0:n], norm.tmp[:, 0:n], LN_EPS)
                if hidden:
                    dve.scalar_tensor_tensor(out=shift2[:, :], in0=mv2[:, :, 0], scalar=-1.0, in1=root2, op0=ALU.mult,
                                             op1=ALU.mult).then_inc(shifted, 1)

            def front(b, first=False):
                steps = Steps(dve, front_step, b.n * FRONT + Norm.STEPS, FRONT - Norm.STEPS)
                for j in range(G):
                    last = norm.apply(dve, xn[:, j, :], sh.x[:, b.n * G + j, :], j)
                last.then_inc(norm_ready, 1)
                dve.wait_ge(norm_ready, b.n + 1)
                again.statistics(dve, steps, lambda j: xn[:, j, :])
                for j in range(G):
                    last = again.apply(dve, xn[:, j, :], xn[:, j, :], j)
                steps.link(last)
                wide = lambda a: a.unsqueeze(1).broadcast_to([P, G, D])
                steps.link(dve.tensor_tensor(xn[:, :, :], xn[:, :, :], wide(w["g1"]), ALU.mult))
                steps.link(dve.tensor_tensor(xn[:, :, :], xn[:, :, :], wide(w["c1"]), ALU.add))
                steps.link(dve.tensor_reduce(amax[:, :], xn[:, :, :], AX.X, ALU.max, apply_absolute_value=True))
                if not first:
                    dve.wait_ge(hid_scaled, b.n * G - G)
                quantize(steps, amax[:, :], inv[:, :], back[:, b.slot, :], ws[:, 0:1])
                for j in range(G):
                    last = dve.tensor_scalar(xn[:, j, :], xn[:, j, :], inv[:, j:j + 1], ROUND, ALU.mult, ALU.add)
                steps.link(last)
                if not first or b.n == 1:
                    dve.wait_ge(x_turned, b.n)
                dve.tensor_scalar(xq[:, :, :], xn[:, :, :], -ROUND, 127.0, ALU.add, ALU.min).then_inc(quantized, 1)
                steps.close()

            def round_hidden(b):
                steps = Steps(dve, quant_step, b.n * QUANT, QUANT)
                dve.wait_ge(affine, (b.n + 1) * G)
                hb = hn[:, b.slot, :, :]
                steps.link(dve.tensor_reduce(amax2[:, :], hb, AX.X, ALU.max, apply_absolute_value=True))
                quantize(steps, amax2[:, :], inv2[:, :], back2[:, :], ws[:, 1:2])
                for j in range(G):
                    last = dve.tensor_scalar(hb[:, j, :], hb[:, j, :], inv2[:, j:j + 1], ROUND, ALU.mult, ALU.add)
                steps.link(last)
                for j in range(G):
                    dve.tensor_scalar(hq[:, j, :], hb[:, j, :], -ROUND, 127.0, ALU.add, ALU.min).then_inc(hq_ready, 1)
                steps.close()

            def add_out(b):
                dve.wait_ge(out_ready, (b.n + 1) * G)
                dve.wait_ge(bias_added, (b.n + 1) * G)
                for j in range(G):
                    dve.scalar_tensor_tensor(out=sh.x[:, b.n * G + j, :], in0=Y[:, j, 0:D], scalar=back2[:, j:j + 1],
                                             in1=sh.x[:, b.n * G + j, :], op0=ALU.mult, op1=ALU.add).then_inc(out_added, 1)

            sh.wait_params(dve, phase)
            for n, part in enumerate(("w1", "w2")):
                dve.tensor_reduce(ws[:, n:n + 1], w[part].rearrange("p a b -> p (a b)"), AX.X, ALU.add,
                                  apply_absolute_value=True).then_inc(w_summed, 1)
            dve.wait_ge(w_total, 1)
            prep = Steps(dve, prep_step, 0, 6)
            prep.link(dve.tensor_scalar(ws[:, :], Y[:, 0, 0:2], 1.0 / (D * F), FLOOR, ALU.mult, ALU.max))
            prep.link(dve.reciprocal(wi[:, :], ws[:, :]))
            for n, (part, out) in enumerate((("w1", wq1), ("w2", wq2))):
                prep.link(dve.tensor_scalar(w[part], w[part], wi[:, n:n + 1], ROUND, ALU.mult, ALU.add))
                prep.link(dve.tensor_scalar(w[part], w[part], -ROUND, 1.0, ALU.add, ALU.min))
                dve.tensor_scalar(out[:, :, :], w[part], -1.0, None, ALU.max).then_inc(w_ready, 1)
            prep.close()
            start = Turn(0, 0)
            for k in range(2):
                statistics(start.plus(k))
                front(start.plus(k), first=True)
            statistics(start.plus(2), hidden=start, first=True)
            front(start.plus(2))
            with dve.Fori(0, TURNS // 2) as i:
                for s in range(2):
                    b = Turn(i, s)
                    statistics(b.plus(3), hidden=b.plus(1))
                    round_hidden(b)
                    front(b.plus(3))
                    add_out(b)
                    dve.wait_ge(out_added, (b.n + 1) * G)


PHASES = ["L0x", "L0f", "L1x", "L1f", "L2x", "L2f", "L3x", "L3f"]


def build(nc, dram, phases=PHASES):
    with ExitStack() as ctx:
        sh = Shared(nc, ctx, dram)
        first_loads(nc, sh, phases)
        for n, phase in enumerate(phases):
            following = phases[n + 1] if n + 1 < len(phases) else None
            if phase in ("L0x", "L3x"):
                attention_phase(nc, sh, phase, 16, following)
            elif phase == "L2x":
                attention_phase(nc, sh, phase, 64, following)
            elif phase == "L0f":
                head_experts_phase(nc, sh, phase, following)
            elif phase == "L1x":
                performer_phase(nc, sh, phase, following)
            elif phase == "L2f":
                quantized_phase(nc, sh, phase, following)
            else:
                experts_phase(nc, sh, phase, following)
        last_stores(nc, sh)


def _rows(a, rows=P):
    return a.reshape(-1, rows, a.shape[-1]).transpose(1, 0, 2).reshape(rows, -1)


def _cols(a):
    return a.reshape(-1, P).T


def _wide(a):
    return np.broadcast_to(a.reshape(1, -1), (P, a.size))


def _constants():
    f = np.float32
    p, q = np.arange(P)[:, None], np.arange(P)[None, :]
    out = {
        "ident": (p == q), "pick8": 0.25 * (p // 16 == np.arange(8)), "pick2": 0.125 * (p // 64 == np.arange(2)),
        "feat2": 0.125 * (p // 64 == np.arange(2)), "causal": (p <= q),
        "half": -0.5 * np.concatenate([(p // 32 == s) & ((p % 32) // 16 == q // 64) for s in range(4)], 1),
        "headsum": -0.5 * (p // 16 == np.arange(8)),
        "iota8": np.broadcast_to(np.arange(8), (P, 8)), "iota16": np.broadcast_to(np.arange(16), (P, 16)),
        "ones": np.ones((P, P)),
        "tiles": np.broadcast_to(np.arange(SLOT_TILES + TILES_AHEAD), (P, SLOT_TILES + TILES_AHEAD)),
    }
    return np.concatenate([out[n].astype(f) for n, _ in PARTS["const"]], 1)


def _pack(i):
    z = np.zeros
    f = np.float32

    def attn(k, transposed=False):
        g = lambda n: i[f"{k}_{n}"].T if transposed and n[0] == "W" else i[f"{k}_{n}"]
        return {"wq": _rows(g("Wq")), "wk": _rows(g("Wk")), "wv": _rows(g("Wv")), "wo": _rows(g("Wo")),
                "bq": _cols(g("bq")), "bk": _cols(g("bk")), "bv": _wide(g("bv")), "bo": _wide(g("bo"))}

    def padded(a, n):
        out = z((a.shape[0], n), f)
        out[:, :a.shape[1]] = a
        return out

    rf = z((P, 4, P), f)
    for s in range(4):
        for a in range(2):
            rf[32 * s + 16 * a:32 * s + 16 * a + 16, s, 64 * a:64 * a + 64] = i["L1_xattn_random_features"]
    emb = z((P, 2, 8, 16), f)
    b2 = z((8, 16, 2, 4, 32), f)
    for h in range(8):
        emb[32 * (h % 4):32 * (h % 4) + 32, h // 4, h, :] = i["L0_ffn_expert_emb"]
        b2[h, :, h // 4, h % 4, :] = i["L0_ffn_b2"]
    parts = {
        "L0x": attn("L0_xattn"),
        "L0f": {"wm": _rows(i["L0_ffn_Wm"]), "wo": _rows(i["L0_ffn_Wo"]), "emb": emb.reshape(P, -1),
                "w1": np.tile(i["L0_ffn_W1"].transpose(1, 0, 2).reshape(32, -1), (4, 1)),
                "w2": i["L0_ffn_W2"].transpose(1, 0, 2).reshape(P, -1), "b2": b2.reshape(P, -1),
                "b1": i["L0_ffn_b1"].T, "bm": _cols(i["L0_ffn_bm"]), "bo": _wide(i["L0_ffn_bo"])},
        "L1x": attn("L1_xattn") | {"rf": rf.reshape(P, -1)},
        "L1f": {"w1": i["L1_ffn_W1"].reshape(8, 2, P, 512).transpose(2, 0, 1, 3).reshape(P, -1),
                "w2": i["L1_ffn_W2"].reshape(8, 4, P, D).transpose(2, 0, 1, 3).reshape(P, -1),
                "wg": _rows(padded(i["L1_ffn_Wg"], P)), "bg": _wide(i["L1_ffn_bg"]),
                "b1": i["L1_ffn_b1"].reshape(8, 4, P).transpose(2, 0, 1).reshape(P, -1), "b2": _wide(i["L1_ffn_b2"]),
                "gamma": _wide(i["L1_ffn_gamma"]), "beta": _wide(i["L1_ffn_beta"])},
        "L2x": {"wq": _rows(i["L2_xattn_Wq"]), "wk": _rows(i["L2_xattn_Wk"]), "wv": _rows(i["L2_xattn_Wv"]),
                "wo": _rows(i["L2_xattn_Wo"])},
        "L2f": {"w1": _rows(i["L2_ffn_w1"].T), "w2": _rows(i["L2_ffn_w2"].T), "g1": _wide(i["L2_ffn_ln1_g"]),
                "c1": _wide(i["L2_ffn_ln1_b"]), "b1": _wide(i["L2_ffn_b1"]), "g2": _wide(i["L2_ffn_ln2_g"]),
                "c2": _wide(i["L2_ffn_ln2_b"]), "b2": _wide(i["L2_ffn_b2"])},
        "L3x": attn("L3_xattn", True) | {"mask": i["fside_SxS2_0"]},
        "L3f": {"w1": i["L3_ffn_w1"].transpose(0, 2, 1).reshape(8, 2, P, 512).transpose(2, 0, 1, 3).reshape(P, -1),
                "w2": i["L3_ffn_w2"].transpose(0, 2, 1).reshape(8, 2, P, D).transpose(2, 0, 1, 3).reshape(P, -1),
                "wg": _rows(padded(i["L3_ffn_Wg"].T, P)), "bg": _wide(i["L3_ffn_bg"])},
    }
    return {f"p_{ph}": np.ascontiguousarray(np.concatenate([parts[ph][n] for n, _ in PARTS[ph]], 1)) for ph in parts}


def _arrays(i):
    i = {k: np.asarray(v) for k, v in i.items()}
    arrays = {"x": i["x"], "side": np.ascontiguousarray(i["fside_Bx16xSxS2_0"].transpose(2, 0, 1, 3).reshape(P, BATCH * HEADS, P)),
              "pad": i["mask_BxS2_bf0"].view(np.int32),
              "ctxT": np.ascontiguousarray(i["ctx_1024"].reshape(BATCH * P, KT, P).transpose(2, 1, 0)),
              "p_const": _constants()}
    arrays.update(_pack(i))
    return arrays


def _declare(nc, arrays):
    types = {"float32": F32, "int32": I32}
    dram = {n: nc.dram_tensor(f"{n}_dram", list(a.shape), types[str(a.dtype)], kind="ExternalInput").ap()
            for n, a in arrays.items()}
    dram["out"] = nc.dram_tensor("out_dram", [BATCH, P, D], F32, kind="ExternalOutput").ap()
    dram["gates"] = nc.dram_tensor("gates_dram", [9, P, 512], F32, kind="Internal").ap()
    for n, tiles in (("rows_in", SLOT_TILES + TILES_AHEAD), ("rows_out", SLOT_TILES)):
        dram[n] = nc.dram_tensor(f"{n}_dram", [tiles * P, D], F32, kind="Internal").ap()
    return dram


def kernel(**inputs):
    from concourse import bacc
    from concourse.bass_utils import run_bass_kernel_spmd

    nc = bacc.Bacc("TRN2", target_bir_lowering=False, num_devices=1)
    arrays = _arrays(inputs)
    build(nc, _declare(nc, arrays))
    r = run_bass_kernel_spmd(nc, [{f"{n}_dram": a for n, a in arrays.items()}], core_ids=[0])
    return r.results[0]["out_dram"]
```
